# Optimizing a Trainium2 kernel written in Bass

```python
import numpy as np
import jax
import jax.numpy as jnp

def _softmax(x, axis=-1):
    return jax.nn.softmax(x, axis=axis)

def _gelu(x):
    return jax.nn.gelu(x, approximate=True)

def _silu(x):
    return jax.nn.silu(x)

def _sigmoid(x):
    return jax.nn.sigmoid(x)

def _layernorm(x, axis=-1, eps=1e-05):
    m = jnp.mean(x, axis=axis, keepdims=True)
    v = jnp.var(x, axis=axis, keepdims=True)
    return (x - m) / jnp.sqrt(v + eps)

def _scatter_add(tgt, idx, src, axis=0):
    return tgt.at[idx].add(src)

def _segment_sum(src, seg, n):
    return jax.ops.segment_sum(src, seg, n)
kernel_name = 'mk_gnn_resnorm_d2_gnn_r64_9df5e3'

def setup_inputs(seed: int=0):
    np.random.seed(seed)
    _w = jnp.asarray

    def _rec_inputs():
        import jax
        import jax.numpy as jnp
        _gk = jax.random.key(seed)
        x = -0.0005121 + 1.001 * jax.random.normal(jax.random.fold_in(_gk, 1), (100000, 64), jnp.float32)
        src = jax.random.randint(jax.random.fold_in(_gk, 2), (25000,), 0, 100000, jnp.int32)
        dst = jnp.minimum((100000 * jax.random.uniform(jax.random.fold_in(_gk, 3), (25000,)) ** 2.0).astype(jnp.int32), 99999)
        _o = jnp.argsort(dst, stable=True)
        src = src[_o]
        dst = dst[_o]
        edge_attr_16 = 0.000254156 + 0.999948 * jax.random.normal(jax.random.fold_in(_gk, 12), (25000, 16), jnp.float32)
        edge_attr_3 = 0.00117183 + 1.0004 * jax.random.normal(jax.random.fold_in(_gk, 13), (25000, 3), jnp.float32)
        return (x, src, dst, edge_attr_16, edge_attr_3)
    x, src, dst, edge_attr_16, edge_attr_3 = _rec_inputs()

    def _L0_gnn_setup():
        import jax, jax.numpy as jnp
        import numpy as np
        N, E = (50000, 12500)
        EMB, HEADS, EDGE_DIM = (64, 4, 16)
        NEG_SLOPE = 0.2
        LN_EPS = 1e-05
        key = jax.random.key(seed)
        ks = jax.random.split(key, 12)
        HC = HEADS * EMB
        inp = {'x': jax.random.normal(ks[0], (N, EMB), jnp.float32), 'edge_index': jax.random.randint(ks[1], (2, E), 0, N, jnp.int32), 'edge_attr': jax.random.normal(ks[2], (E, EDGE_DIM), jnp.float32), 'W': jax.random.normal(ks[3], (EMB, HC), jnp.float32) * 0.1, 'W_edge': jax.random.normal(ks[4], (EDGE_DIM, HC), jnp.float32) * 0.1, 'att_src': jax.random.normal(ks[5], (HEADS, EMB), jnp.float32) * 0.1, 'att_dst': jax.random.normal(ks[6], (HEADS, EMB), jnp.float32) * 0.1, 'att_edge': jax.random.normal(ks[7], (HEADS, EMB), jnp.float32) * 0.1, 'bias': jnp.zeros((HC,), jnp.float32), 'Wp': jax.random.normal(ks[8], (HC, EMB), jnp.float32) * 0.05, 'bp': jnp.zeros((EMB,), jnp.float32), 'gamma': jnp.ones((EMB,), jnp.float32), 'beta': jnp.zeros((EMB,), jnp.float32)}
        return inp
    _L0_gnn_all = _L0_gnn_setup()
    _L0_gnn_in = {k: v for k, v in _L0_gnn_all.items() if k in ('W', 'W_edge', 'att_src', 'att_dst', 'att_edge', 'bias', 'Wp', 'bp', 'gamma', 'beta')}
    del _L0_gnn_all

    def _L1_gnn_setup():
        import jax, jax.numpy as jnp
        import numpy as np
        M = 50000
        E = 12500
        C_IN = 64
        C_OUT = 64
        DIM = 3
        RADIUS = 1.0
        EPS = 1e-05

        def layer_norm(x, g, b):
            mu = jnp.mean(x, axis=-1, keepdims=True)
            var = jnp.mean((x - mu) ** 2, axis=-1, keepdims=True)
            return (x - mu) * jax.lax.rsqrt(var + EPS) * g + b
        key = jax.random.key(seed)
        ks = jax.random.split(key, 12)
        inv = 1.0 / np.sqrt(C_OUT)
        return {'source': jax.random.randint(ks[0], (E,), 0, M), 'target': jax.random.randint(ks[1], (E,), 0, M), 'features': jax.random.normal(ks[2], (M, C_IN), dtype=jnp.float32), 'hood_coords': jax.random.normal(ks[3], (E, DIM), dtype=jnp.float32), 'Wd1': jax.random.normal(ks[4], (DIM, C_OUT), dtype=jnp.float32) / np.sqrt(DIM), 'bd1': jnp.zeros((C_OUT,), jnp.float32), 'g1': jnp.ones((C_OUT,), jnp.float32), 'b1': jnp.zeros((C_OUT,), jnp.float32), 'Wd2': jax.random.normal(ks[5], (C_OUT, C_OUT), dtype=jnp.float32) * inv, 'bd2': jnp.zeros((C_OUT,), jnp.float32), 'g2': jnp.ones((C_OUT,), jnp.float32), 'b2': jnp.zeros((C_OUT,), jnp.float32), 'W1': jax.random.normal(ks[6], (C_IN, C_OUT), dtype=jnp.float32) / np.sqrt(C_IN), 'W2': jax.random.normal(ks[7], (C_IN, C_OUT), dtype=jnp.float32) / np.sqrt(C_IN), 'W3': jax.random.normal(ks[8], (C_IN, C_OUT), dtype=jnp.float32) / np.sqrt(C_IN)}
    _L1_gnn_all = _L1_gnn_setup()
    _L1_gnn_in = {k: v for k, v in _L1_gnn_all.items() if k in ('Wd1', 'bd1', 'g1', 'b1', 'Wd2', 'bd2', 'g2', 'b2', 'W1', 'W2', 'W3')}
    del _L1_gnn_all
    return {'x': x, 'src': src, 'dst': dst, 'edge_attr_16': edge_attr_16, 'edge_attr_3': edge_attr_3, 'L0_gnn_W': _L0_gnn_in['W'], 'L0_gnn_W_edge': _L0_gnn_in['W_edge'], 'L0_gnn_att_src': _L0_gnn_in['att_src'], 'L0_gnn_att_dst': _L0_gnn_in['att_dst'], 'L0_gnn_att_edge': _L0_gnn_in['att_edge'], 'L0_gnn_bias': _L0_gnn_in['bias'], 'L0_gnn_Wp': _L0_gnn_in['Wp'], 'L0_gnn_bp': _L0_gnn_in['bp'], 'L0_gnn_gamma': _L0_gnn_in['gamma'], 'L0_gnn_beta': _L0_gnn_in['beta'], 'L1_gnn_Wd1': _L1_gnn_in['Wd1'], 'L1_gnn_bd1': _L1_gnn_in['bd1'], 'L1_gnn_g1': _L1_gnn_in['g1'], 'L1_gnn_b1': _L1_gnn_in['b1'], 'L1_gnn_Wd2': _L1_gnn_in['Wd2'], 'L1_gnn_bd2': _L1_gnn_in['bd2'], 'L1_gnn_g2': _L1_gnn_in['g2'], 'L1_gnn_b2': _L1_gnn_in['b2'], 'L1_gnn_W1': _L1_gnn_in['W1'], 'L1_gnn_W2': _L1_gnn_in['W2'], 'L1_gnn_W3': _L1_gnn_in['W3']}

def reference(x, src, dst, edge_attr_16, edge_attr_3, L0_gnn_W, L0_gnn_W_edge, L0_gnn_att_src, L0_gnn_att_dst, L0_gnn_att_edge, L0_gnn_bias, L0_gnn_Wp, L0_gnn_bp, L0_gnn_gamma, L0_gnn_beta, L1_gnn_Wd1, L1_gnn_bd1, L1_gnn_g1, L1_gnn_b1, L1_gnn_Wd2, L1_gnn_bd2, L1_gnn_g2, L1_gnn_b2, L1_gnn_W1, L1_gnn_W2, L1_gnn_W3):
    import jax
    import jax.numpy as jnp

    def _L0_gnn_ref(x, edge_index, edge_attr, W, W_edge, att_src, att_dst, att_edge, bias, Wp, bp, gamma, beta):
        import jax, jax.numpy as jnp
        import numpy as np
        N, E = (50000, 12500)
        EMB, HEADS, EDGE_DIM = (64, 4, 16)
        NEG_SLOPE = 0.2
        LN_EPS = 1e-05
        n = x.shape[0]
        H, C = att_src.shape
        xw = (x @ W).reshape(n, H, C)
        a_src_n = jnp.einsum('nhc,hc->nh', xw, att_src)
        a_dst_n = jnp.einsum('nhc,hc->nh', xw, att_dst)
        src, dst = (edge_index[0], edge_index[1])
        loop = jnp.arange(n, dtype=edge_index.dtype)
        cnt = jax.ops.segment_sum(jnp.ones_like(dst, jnp.float32), dst, num_segments=n)
        loop_attr = jax.ops.segment_sum(edge_attr, dst, num_segments=n) / jnp.maximum(cnt, 1.0)[:, None]
        src2 = jnp.concatenate([src, loop])
        dst2 = jnp.concatenate([dst, loop])
        ea = jnp.concatenate([edge_attr, loop_attr], axis=0)
        ew = (ea @ W_edge).reshape(-1, H, C)
        a_edge = jnp.einsum('ehc,hc->eh', ew, att_edge)
        alpha = a_src_n[src2] + a_dst_n[dst2] + a_edge
        alpha = jnp.where(alpha >= 0, alpha, NEG_SLOPE * alpha)
        amax = jax.ops.segment_max(alpha, dst2, num_segments=n)
        ae = jnp.exp(alpha - amax[dst2])
        denom = jax.ops.segment_sum(ae, dst2, num_segments=n)
        attn = ae / denom[dst2]
        msg = xw[src2] * attn[:, :, None]
        agg = jax.ops.segment_sum(msg, dst2, num_segments=n)
        gat_out = agg.reshape(n, H * C) + bias
        proj = gat_out @ Wp + bp
        h = x + jax.nn.elu(proj)
        mu = jnp.mean(h, axis=-1, keepdims=True)
        var = jnp.mean((h - mu) ** 2, axis=-1, keepdims=True)
        out = (h - mu) * jax.lax.rsqrt(var + LN_EPS) * gamma + beta
        return out

    def _L1_gnn_ref(source, target, features, hood_coords, Wd1, bd1, g1, b1, Wd2, bd2, g2, b2, W1, W2, W3):
        import jax, jax.numpy as jnp
        import numpy as np
        M = 50000
        E = 12500
        C_IN = 64
        C_OUT = 64
        DIM = 3
        RADIUS = 1.0
        EPS = 1e-05

        def layer_norm(x, g, b):
            mu = jnp.mean(x, axis=-1, keepdims=True)
            var = jnp.mean((x - mu) ** 2, axis=-1, keepdims=True)
            return (x - mu) * jax.lax.rsqrt(var + EPS) * g + b
        m = features.shape[0]
        x = hood_coords / RADIUS
        d = jax.nn.gelu(layer_norm(x @ Wd1 + bd1, g1, b1), approximate=False)
        d = jax.nn.gelu(layer_norm(d @ Wd2 + bd2, g2, b2), approximate=False)
        w1 = features @ W1
        w2 = features @ W2
        w3 = features @ W3
        logits = w1[target] - w2[source] + d
        seg_max = jax.ops.segment_max(logits, target, num_segments=m)
        seg_max = jnp.where(jnp.isfinite(seg_max), seg_max, 0.0)
        e = jnp.exp(logits - seg_max[target])
        denom = jax.ops.segment_sum(e, target, num_segments=m)
        a = e / denom[target]
        out = jax.ops.segment_sum(a * (w3[source] + d), target, num_segments=m)
        return out
    edge_index = jnp.stack([src, dst])
    x = _layernorm(x + _L0_gnn_ref(x, edge_index, edge_attr_16, L0_gnn_W, L0_gnn_W_edge, L0_gnn_att_src, L0_gnn_att_dst, L0_gnn_att_edge, L0_gnn_bias, L0_gnn_Wp, L0_gnn_bp, L0_gnn_gamma, L0_gnn_beta), axis=-1)
    x = _layernorm(x + _L1_gnn_ref(src, dst, x, edge_attr_3, L1_gnn_Wd1, L1_gnn_bd1, L1_gnn_g1, L1_gnn_b1, L1_gnn_Wd2, L1_gnn_bd2, L1_gnn_g2, L1_gnn_b2, L1_gnn_W1, L1_gnn_W2, L1_gnn_W3), axis=-1)
    return x

_drawn_inputs = setup_inputs


def setup_inputs(seed=0):
    import zlib

    import numpy as np

    out = dict(_drawn_inputs(seed))
    spreads = {'L0_gnn_bias': (0.0, 0.1),
     'L0_gnn_bp': (0.0, 0.1),
     'L0_gnn_gamma': (1.0, 0.2),
     'L0_gnn_beta': (0.0, 0.1),
     'L1_gnn_bd1': (0.0, 0.28),
     'L1_gnn_g1': (1.0, 0.2),
     'L1_gnn_b1': (0.0, 0.41),
     'L1_gnn_bd2': (0.0, 0.287),
     'L1_gnn_g2': (1.0, 0.2),
     'L1_gnn_b2': (0.0, 0.359)}
    factors = {'edge_attr_16': 8.0,
     'L0_gnn_W_edge': 8.0,
     'L0_gnn_att_src': 3.096,
     'L0_gnn_att_dst': 8.0,
     'L0_gnn_att_edge': 8.0,
     'L1_gnn_W1': 8.0}
    for name, (base, spread) in spreads.items():
        noise = np.random.default_rng([zlib.crc32(name.encode()), seed]).standard_normal(out[name].shape)
        drawn = base * np.exp(spread * noise) if base else spread * noise
        out[name] = jnp.asarray(drawn.astype(out[name].dtype))
    for name, factor in factors.items():
        out[name] = (out[name] * factor).astype(out[name].dtype)
    return out
```

```python
import concourse.bass as bass
from concourse import mybir
from contextlib import ExitStack

N, E, F, H = 100000, 25000, 64, 4
EPS = 1e-5
BIG = 1.0e30
SKIP = 8388608.0
COLS = 512
NODES = 2 * COLS
DENSE = -(-N // NODES)
UNITS = 50
TILES = 4 * UNITS
EP = UNITS * COLS
QR = TILES // 2
PAIRS = UNITS // 2
CH = 12
ALU = mybir.AluOpType
ACT = mybir.ActivationFunctionType
AX = mybir.AxisListType
fp32, bf16, i32 = mybir.dt.float32, mybir.dt.bfloat16, mybir.dt.int32

P64 = {}
_at = 0
for _n, _w in (("WT", H * 128), ("Wp", H * 128), ("WeT", H * 16), ("aS", H), ("aD", H), ("aE", H), ("bias", H)):
    P64[_n] = (_at, _at + _w)
    _at += _w
W64 = _at
P128 = {}
_at = 0
for _n, _w in (("bp", 1), ("gamma", 1), ("beta", 1), ("g1", 1), ("b1", 1), ("bd2", 1), ("g2", 1), ("b2", 1),
               ("Wd1T", 7), ("Wd2T", 128), ("Wqq", 128), ("Wv", 128), ("ident", 128), ("C", 128),
               ("J", 128), ("ind", 2), ("xdA", 128), ("xdB", 128), ("dA", 128), ("dB", 128), ("head", H * 128)):
    P128[_n] = (_at, _at + _w)
    _at += _w
W128 = _at


class Unit:

    def __init__(self, i, off):
        self.i, self.off = i, off

    def back(self, n):
        return Unit(self.i, self.off - n)

    def count(self, n=1):
        return self.i * 4 + (self.off + n)

    def halves(self, n=0):
        return self.i * 2 + (self.off // 2 + n)

    def edge(self, n):
        return EdgeUnit(self.i, (self.off - 1) // 2 - n)

    def static(self):
        return isinstance(self.i, int)

    def valid(self, n):
        return not self.static() or 0 <= self.count(0) < n


class EdgeUnit:

    def __init__(self, i, off):
        self.i, self.off = i, off

    def count(self, n=1):
        return self.i * 2 + (self.off + n)

    def halves(self, n=0):
        return self.i + (self.off // 2 + n)

    def next(self):
        return EdgeUnit(self.i, self.off + 1)

    def valid(self, n):
        return not isinstance(self.i, int) or 0 <= self.count(0) < n


def atleast(eng, sem, value):
    if not isinstance(value, int) or value > 0:
        eng.wait_ge(sem, value)


MAGIC = float(0x5F1FFFF9)


def inverse_roots(nc, dve, v, w, ta, tb, step, before, made):
    c1, c2 = 0.703952253, 0.703952253 * 2.38924456
    n = before * 7
    nc.vector.tensor_scalar(ta.bitcast(i32), v.bitcast(i32), 1, None, ALU.arith_shift_right).then_inc(step, 1)
    dve.wait_ge(step, n + 1)
    nc.vector.tensor_scalar(w.bitcast(i32), ta.bitcast(i32), -1.0, MAGIC, ALU.mult, ALU.add).then_inc(step, 1)
    dve.wait_ge(step, n + 2)
    nc.vector.scalar_tensor_tensor(ta, w, -c1, w, ALU.mult, ALU.mult).then_inc(step, 1)
    dve.wait_ge(step, n + 3)
    nc.vector.tensor_tensor(ta, ta, v, ALU.mult).then_inc(step, 1)
    dve.wait_ge(step, n + 4)
    nc.vector.scalar_tensor_tensor(tb, ta, c2, w, ALU.add, ALU.mult).then_inc(step, 1)
    dve.wait_ge(step, n + 5)
    nc.vector.scalar_tensor_tensor(ta, tb, -0.5, tb, ALU.mult, ALU.mult).then_inc(step, 1)
    dve.wait_ge(step, n + 6)
    nc.vector.tensor_tensor(ta, ta, v, ALU.mult).then_inc(step, 1)
    dve.wait_ge(step, n + 7)
    nc.vector.scalar_tensor_tensor(w, ta, 1.5, tb, ALU.add, ALU.mult).then_inc(made, 1)


def slots(eng, total, skew, body):
    loops = total // 4
    for k in range(8):
        body(Unit(0, k))
    with eng.Fori(2, loops) as i:
        for k in range(4):
            body(Unit(i, k))
    for k in range(4 * loops, total + skew):
        body(Unit(0, k))


def gnn(nc, x, gidx, drow, dblk, eaT, ea3, p64, p128, out):
    x1 = nc.dram_tensor("x1_table", [N, F], fp32, kind="Internal").ap()
    logit_rows = nc.dram_tensor("logit_rows", [CH, EP], fp32, kind="Internal").ap()

    weight_rows = nc.dram_tensor("weight_rows", [24, EP], bf16, kind="Internal").ap()
    mask_rows = nc.dram_tensor("mask_rows", [2, EP], bf16, kind="Internal").ap()

    with ExitStack() as ctx:
        def sb(name, shape, dt=fp32):
            return ctx.enter_context(nc.sbuf_tensor(name, shape, dt))

        def sem(name):
            return ctx.enter_context(nc.semaphore(name))

        def places(ph, phase):
            def buffer(name, shape, dt=fp32):
                return ph.enter_context(nc.sbuf_tensor(f"{phase}_{name}", shape, dt))

            def semaphore(name):
                return ph.enter_context(nc.semaphore(f"{phase}_{name}"))

            return buffer, semaphore

        bank = [ctx.enter_context(nc.psum_tensor(f"bank{i}", [128, COLS], fp32)) for i in range(8)]
        prm64 = sb("prm64", [64, W64])
        prm = sb("prm", [128, W128])
        gix = sb("gix", [128, UNITS * 8], i32)
        XT = sb("XT", [128, EP])

        def c64(n):
            return prm64[:, P64[n][0]:P64[n][1]]

        def c128(n):
            return prm[:, P128[n][0]:P128[n][1]]

        ident, Cm, Jm = c128("ident"), c128("C"), c128("J")
        Mstack = sb("Mstack", [128, H, F])
        Mblk = sb("Mblk", [128, 128])
        Wal = sb("Wal", [128, CH])
        WalE = sb("WalE", [16, CH])
        c0 = sb("c0", [128, 1])
        c0x = sb("c0x", [128, 1])
        ncbeta = sb("ncbeta", [128, 1])
        CG = sb("CG", [128, 128])
        Wd1 = sb("Wd1", [7, 128])
        b2row = sb("b2row", [1, 128])
        ones = sb("ones", [1, 128])
        Wd2 = sb("Wd2", [128, 128])
        headsel = sb("headsel", [24, H, 128], bf16)

        s_prm, s_pe0, s_ev0, s_pe1, s_z0, s_gix = (sem(n) for n in (
            "params_loaded", "products_made", "products_copied", "beta_projected", "zeroed", "indices_loaded"))
        with nc.Block() as block:
            @block.sync
            def _(sp):
                sp.dma_start(prm64[:, :], p64).then_inc(s_prm, 16)
                sp.dma_start(prm[:, :], p128).then_inc(s_prm, 16)
                sp.dma_start(gix[:, :], gidx).then_inc(s_gix, 16)
                sp.wait_ge(s_gix, 16)

            @block.tensor
            def _(pe):
                pe.wait_ge(s_prm, 32)
                WT, Wp, WeT = (c64(n).rearrange("c (h k) -> c h k", h=H) for n in ("WT", "Wp", "WeT"))
                for h in range(H):
                    nc.tensor.matmul(bank[0][:, h * F:(h + 1) * F], WT[:, h, :], Wp[:, h, 0:F],
                                     start=True, stop=True)
                    nc.tensor.matmul(bank[1][:, 0:F], WT[:, h, :], Wp[:, h, 0:F], start=(h == 0), stop=(h == H - 1))
                for h in range(H):
                    nc.tensor.matmul(bank[2][:, h:h + 1], WT[:, h, :], c64("aS")[:, h:h + 1], start=True, stop=True)
                    nc.tensor.matmul(bank[2][:, 4 + h:5 + h], WT[:, h, :], c64("aD")[:, h:h + 1], start=True, stop=True)
                    nc.tensor.matmul(bank[3][0:16, h:h + 1], WeT[:, h, :], c64("aE")[:, h:h + 1], start=True, stop=True)
                for h in range(H):
                    nc.tensor.matmul(bank[4][:, 0:1], Wp[:, h, :], c64("bias")[:, h:h + 1],
                                     start=(h == 0), stop=(h == H - 1))
                nc.tensor.matmul(bank[5][:, 0:1], Cm, c128("beta"), start=True, stop=True)
                nc.tensor.matmul(bank[0][0:1, 256:384], c128("bd2"), Cm, start=True, stop=True)
                nc.tensor.matmul(bank[6][0:7, 0:128], c128("Wd1T"), Cm, start=True, stop=True)
                nc.tensor.matmul(bank[7][:, 0:128], c128("Wd2T"), Cm, start=True, stop=True).then_inc(s_pe0, 1)
                pe.wait_ge(s_ev0, 2)
                nc.tensor.matmul(bank[5][:, 3:4], Mblk[:, :], c128("beta"), start=True, stop=True).then_inc(s_pe1, 1)

            @block.vector
            def _(dve):
                nc.vector.memset(Mblk[:, :], 0.0)
                nc.vector.memset(Wal[:, :], 0.0)
                nc.vector.memset(WalE[:, :], 0.0).then_inc(s_z0, 1)
                dve.wait_ge(s_z0, 1)
                dve.wait_ge(s_prm, 32)
                nc.vector.tensor_copy(headsel[:, :, :], c128("head")[0:24, :].rearrange("r (h m) -> r h m", h=H))
                dve.wait_ge(s_pe0, 1)
                nc.vector.tensor_copy(Mstack[:, :, :], bank[0][:, 0:H * F].rearrange("p (h f) -> p h f", h=H))
                nc.vector.tensor_copy(Mblk[0:64, 0:64], bank[1][0:64, 0:F])
                nc.vector.tensor_copy(Mblk[64:128, 64:128], bank[1][64:128, 0:F])
                nc.vector.tensor_copy(Wal[0:64, 0:4], bank[2][0:64, 0:4])
                nc.vector.tensor_copy(Wal[64:128, 0:4], bank[2][64:128, 4:8])
                nc.vector.tensor_copy(Wal[64:128, 8:12], bank[2][64:128, 0:4]).then_inc(s_ev0, 1)
                dve.wait_ge(s_ev0, 1)
                nc.vector.tensor_tensor(Wal[64:128, 8:12], Wal[64:128, 8:12], bank[2][64:128, 4:8], ALU.add)
                nc.vector.tensor_copy(WalE[:, 0:4], bank[3][0:16, 0:4])
                nc.vector.tensor_copy(WalE[:, 4:8], bank[3][0:16, 0:4])
                nc.vector.tensor_tensor(c0[:, :], bank[4][:, 0:1], c128("bp"), ALU.add)
                nc.vector.tensor_scalar(ncbeta[:, :], bank[5][:, 0:1], -1.0, None, ALU.mult)
                nc.vector.tensor_scalar(CG[:, :], Cm, c128("gamma"), None, ALU.mult)
                nc.vector.memset(ones[:, :], 1.0)
                nc.vector.tensor_copy(b2row[:, :], bank[0][0:1, 256:384])
                nc.vector.tensor_copy(Wd1[:, :], bank[6][0:7, 0:128])
                nc.vector.tensor_copy(Wd2[:, :], bank[7][:, 0:128])
                nc.vector.tensor_scalar(c128("Wqq")[0:64, :], c128("Wqq")[0:64, :], -1.0, None, ALU.mult).then_inc(s_ev0, 1)
                dve.wait_ge(s_ev0, 2)
                dve.wait_ge(s_pe1, 1)
                nc.vector.tensor_tensor(c0x[:, :], c0[:, :], bank[5][:, 3:4], ALU.subtract)

        with ExitStack() as ph:
            sbp, semp = places(ph, "dense")

            rows = [sbp(f"rows{i}", [128, 8 * F]) for i in range(2)]
            xT = [sbp(f"xT{i}", [128, COLS]) for i in range(4)]
            ex = [sbp(f"ex{i}", [128, COLS]) for i in range(2)]
            rl = [sbp(f"rl{i}", [128, COLS]) for i in range(2)]
            gb = sbp("gb", [128, COLS])
            hb = [sbp(f"hb{i}", [128, COLS]) for i in range(2)]
            sq = [sbp(f"sq{i}", [128, COLS]) for i in range(2)]
            hc = [sbp(f"hc{i}", [128, COLS]) for i in range(2)]
            yb = sbp("yb", [128, 8, F])
            yc = [sbp(f"yc{i}", [128, 8, F]) for i in range(2)]
            q2 = [sbp(f"q2{i}", [128, 8, F]) for i in range(2)]
            s2 = sbp("s2", [128, 8])
            v, w, ta, tb = (sbp(n, [128, 24]) for n in ("v", "w", "ta", "tb"))
            xr = [sbp(f"xr{i}", [128, 8, F]) for i in range(2)]
            orow = [sbp(f"orow{i}", [128, 8, F]) for i in range(2)]
            stage = [sbp(f"stage{i}", [128, 8], i32) for i in range(2)]
            pairs = [sbp(f"pairs{i}", [128, 4, 2 * F]) for i in range(2)]
            eab = [sbp(f"eab{i}", [16, COLS]) for i in range(2)]
            lrow = [sbp(f"lrow{i}", [CH, COLS]) for i in range(2)]
            pT, pH, pR, pA = bank[0], bank[1], bank[2], bank[3]
            pG, pX = [bank[4], bank[5]], [bank[6], bank[7]]

            x_loaded = [semp(f"x_loaded{i}") for i in range(2)]
            stored = [semp(f"stored{i}") for i in range(2)]
            (xt_made, x_copied, p_made, e_made, g_made, h_made, hc_made, sq_made, var_made, g_rows_made, v1_made,
             scaled, y_made, y_squared, y_summed, v2_made, out_made) = (semp(n) for n in (
                 "xt_made", "x_copied", "p_made", "e_made", "g_made", "h_made", "hc_made", "sq_made", "var_made",
                 "g_rows_made", "v1_made", "scaled", "y_made", "y_squared", "y_summed", "v2_made", "out_made"))
            v_cleared, root_step, roots_made = semp("v_cleared"), semp("root_step"), semp("roots_made")
            gathered = [semp(f"gathered{i}") for i in range(2)]
            ea_loaded = [semp(f"ea_loaded{i}") for i in range(2)]
            l_stored = [semp(f"l_stored{i}") for i in range(2)]
            sources_staged, targets_staged, pair_turned, pair_copied, l_made, l_copied = (semp(n) for n in (
                "sources_staged", "targets_staged", "pair_turned", "pair_copied", "l_made", "l_copied"))

            def node_rows(table, u):
                if u.static():
                    n0 = min(u.count(0) * NODES, N - NODES)
                    t = table[n0:n0 + NODES, :]
                else:
                    t = table[bass.ds(u.count(0) * NODES, NODES), :]
                return t.rearrange("(p r) f -> p (r f)", p=128)

            block = ph.enter_context(nc.Block())

            @block.sync
            def _(sp):
                def load(u):
                    atleast(sp, xt_made, u.count(-1))
                    sp.dma_start(rows[u.off % 2][:, :], node_rows(x, u)).then_inc(x_loaded[u.off % 2], 16)

                def store(u):
                    b = u.off % 2
                    sp.wait_ge(out_made, u.count(1))
                    if u.static() and u.count(0) == DENSE - 1:
                        sp.wait_ge(stored[1 - b], 32 * ((DENSE - 2) // 2 + 1))
                    sp.dma_start(node_rows(x1, u), xr[b][:, :, :].rearrange("p r f -> p (r f)")).then_inc(stored[b], 16)
                    sp.dma_start(node_rows(out, u), orow[b][:, :, :].rearrange("p r f -> p (r f)")).then_inc(stored[b], 16)

                def load_attributes(e):
                    atleast(sp, l_made, e.count(-1))
                    sp.dma_start(eab[e.off % 2][:, :], eaT[:, bass.ds(e.count(0) * COLS, COLS)])\
                        .then_inc(ea_loaded[e.off % 2], 16)

                def store_logits(e):
                    sp.wait_ge(l_copied, e.count(1))
                    sp.dma_start(logit_rows[:, bass.ds(e.count(0) * COLS, COLS)], lrow[e.off % 2][:, :])\
                        .then_inc(l_stored[e.off % 2], 16)

                def slot(u):
                    if u.static() and u.count(0) == 0:
                        load(u)
                        load_attributes(EdgeUnit(0, 0))
                    if u.back(-1).valid(DENSE):
                        load(u.back(-1))
                    if u.off % 2 == 1:
                        if u.edge(-1).valid(UNITS):
                            load_attributes(u.edge(-1))
                        if u.edge(1).valid(UNITS):
                            store_logits(u.edge(1))
                    if u.back(3).valid(DENSE):
                        store(u.back(3))

                slots(sp, DENSE, 5, slot)
                for b in range(2):
                    sp.wait_ge(stored[b], 32 * (DENSE // 2))
                    sp.wait_ge(l_stored[b], 16 * (UNITS // 2))

            @block.gpsimd
            def _(pool):
                def stage_sources(e):
                    if e.valid(UNITS):
                        atleast(pool, gathered[e.off % 2], e.halves(0) * 128)
                        nc.gpsimd.tensor_copy(stage[e.off % 2][:, 0:4], gix[:, bass.ds(e.count(0) * 8, 4)])\
                            .then_inc(sources_staged, 1)

                def stage_targets(e):
                    nc.gpsimd.tensor_copy(stage[e.off % 2][:, 4:8], gix[:, bass.ds(e.count(0) * 8 + 4, 4)])\
                        .then_inc(targets_staged, 1)

                def gather(e, js):
                    a = e.off % 2
                    for j in js:
                        pool.indirect_dma_start(
                            out=pairs[a][:, j % 4, F * (j // 4):F * (j // 4) + F], out_offset=None, in_=x,
                            in_offset=bass.IndirectOffsetOnAxis(ap=stage[a][:, j:j + 1], axis=0))\
                            .then_inc(gathered[a], 16)

                def edge_unit(e):
                    atleast(pool, pair_turned, e.count(-1))
                    pool.wait_ge(sources_staged, e.count(1))
                    stage_targets(e)
                    gather(e, range(4))
                    pool.wait_ge(targets_staged, e.count(1))
                    stage_sources(e.next())
                    gather(e, range(4, 8))

                def slot(u):
                    if u.static() and u.count(0) == 0:
                        stage_sources(EdgeUnit(0, 0))
                    if u.off % 2 == 1 and u.edge(0).valid(UNITS):
                        edge_unit(u.edge(0))

                slots(pool, DENSE, 5, slot)

            @block.tensor
            def _(pe):
                def turn_rows(u):
                    pe.wait_ge(x_loaded[u.off % 2], u.halves(1) * 16)
                    atleast(pe, e_made, u.count(0))
                    for j in range(4):
                        last = nc.tensor.transpose(pT[:, j * 128:(j + 1) * 128],
                                                   rows[u.off % 2][:, j * 128:(j + 1) * 128], ident)
                    last.then_inc(xt_made, 1)

                def project(u):
                    pe.wait_ge(x_copied, u.count(1))
                    nc.tensor.matmul(pT[:, :], Mblk[:, :], xT[u.off % 4][:, :], start=True, stop=True).then_inc(p_made, 1)

                def centre(u):
                    pe.wait_ge(h_made, u.count(1))
                    atleast(pe, sq_made, u.count(0))
                    nc.tensor.matmul(pH[:, :], Cm, hb[u.off % 2][:, :], start=True, stop=True).then_inc(hc_made, 1)

                def variance(u):
                    b = u.off % 2
                    pe.wait_ge(sq_made, u.count(1))
                    atleast(pe, v1_made, u.count(0))
                    for j in range(4):
                        last = nc.tensor.matmul(pR[:, 2 * j:2 * j + 2], sq[b][:, j * 128:(j + 1) * 128], c128("ind"),
                                                start=True, stop=True)
                    last.then_inc(var_made, 1)

                def to_rows(u):
                    b = u.off % 2
                    atleast(pe, y_made, u.count(-1))
                    for j in range(4):
                        c = slice(j * 128, (j + 1) * 128)
                        nc.tensor.matmul(pG[b][:, c], hc[b][:, c], CG[:, :], start=True, stop=True)
                        last = nc.tensor.matmul(pX[b][:, c], xT[u.off % 4][:, c], Cm, start=True, stop=True)
                    last.then_inc(g_rows_made, 1)

                def turn_pairs(e):
                    a = e.off % 2
                    pe.wait_ge(gathered[a], e.halves(1) * 128)
                    atleast(pe, l_copied, e.count(0))
                    for j in range(4):
                        last = nc.tensor.transpose(pA[:, j * 128:(j + 1) * 128], pairs[a][:, j, :], ident)
                    last.then_inc(pair_turned, 1)

                def logits(e):
                    a = e.off % 2
                    pe.wait_ge(pair_copied, e.count(1))
                    pe.wait_ge(ea_loaded[a], e.halves(1) * 16)
                    nc.tensor.matmul(pA[0:CH, :], Wal[:, :], XT[:, bass.ds(e.count(0) * COLS, COLS)],
                                     start=True, stop=False)
                    nc.tensor.matmul(pA[0:CH, :], WalE[:, :], eab[a][:, :], start=False, stop=True).then_inc(l_made, 1)

                def slot(u):
                    if u.back(2).valid(DENSE):
                        variance(u.back(2))
                    if u.valid(DENSE):
                        turn_rows(u)
                    if u.back(2).valid(DENSE):
                        to_rows(u.back(2))
                    if u.back(1).valid(DENSE):
                        centre(u.back(1))
                    if u.valid(DENSE):
                        project(u)
                    if u.off % 2 == 1 and u.edge(1).valid(UNITS):
                        turn_pairs(u.edge(1))
                    if u.off % 2 == 0 and u.edge(1).valid(UNITS):
                        logits(u.edge(1))

                slots(pe, DENSE, 5, slot)

            @block.scalar
            def _(act):
                def copy_x(u):
                    act.wait_ge(xt_made, u.count(1))
                    atleast(act, g_rows_made, u.count(-3))
                    nc.scalar.activation(xT[u.off % 4][:, :], pT[:, :], ACT.Identity, bias=c128("beta")).then_inc(x_copied, 1)

                def elu_parts(u):
                    b = u.off % 2
                    act.wait_ge(p_made, u.count(1))
                    atleast(act, g_made, u.count(-1))
                    nc.scalar.activation(ex[b][:, :], pT[:, :], ACT.Exp, bias=c0x[:, :])
                    nc.scalar.activation(rl[b][:, :], pT[:, :], ACT.Relu, bias=c0x[:, :]).then_inc(e_made, 1)

                def square(u):
                    b = u.off % 2
                    act.wait_ge(hc_made, u.count(1))
                    atleast(act, g_rows_made, u.count(-1))
                    nc.scalar.activation(sq[b][:, :], pH[:, :], ACT.Square, bias=ncbeta[:, :])
                    nc.scalar.activation(hc[b][:, :], pH[:, :], ACT.Identity, bias=ncbeta[:, :]).then_inc(sq_made, 1)

                def square_y(u):
                    b = u.off % 2
                    act.wait_ge(y_made, u.count(1))
                    atleast(act, y_summed, u.count(-1))
                    nc.scalar.activation(q2[b][:, :, :], yc[b][:, :, :], ACT.Square, scale=F ** -0.5).then_inc(y_squared, 1)

                def copy_pairs(e):
                    act.wait_ge(pair_turned, e.count(1))
                    nc.scalar.activation(XT[:, bass.ds(e.count(0) * COLS, COLS)], pA[:, :], ACT.Copy).then_inc(pair_copied, 1)

                def copy_logits(e):
                    a = e.off % 2
                    act.wait_ge(l_made, e.count(1))
                    atleast(act, l_stored[a], e.halves(0) * 16)
                    nc.scalar.activation(lrow[a][:, :], pA[0:CH, :], ACT.Copy).then_inc(l_copied, 1)

                def slot(u):
                    if u.valid(DENSE):
                        copy_x(u)
                    if u.back(1).valid(DENSE):
                        square(u.back(1))
                    if u.valid(DENSE):
                        elu_parts(u)
                    if u.back(2).valid(DENSE):
                        square_y(u.back(2))
                    if u.off % 2 == 1 and u.edge(1).valid(UNITS):
                        copy_pairs(u.edge(1))
                    if u.off % 2 == 0 and u.edge(1).valid(UNITS):
                        copy_logits(u.edge(1))

                slots(act, DENSE, 5, slot)

            @block.vector
            def _(dve):
                def residual(u):
                    b = u.off % 2
                    dve.wait_ge(e_made, u.count(1))
                    atleast(dve, h_made, u.count(0))
                    nc.vector.scalar_tensor_tensor(gb[:, :], ex[b][:, :], 1.0, rl[b][:, :], ALU.min, ALU.add).then_inc(g_made, 1)
                    atleast(dve, hc_made, u.count(-1))
                    dve.wait_ge(g_made, u.count(1))
                    nc.vector.tensor_tensor(hb[b][:, :], gb[:, :], xT[u.off % 4][:, :], ALU.add).then_inc(h_made, 1)

                def add_eps(u):
                    dve.wait_ge(var_made, u.count(1))
                    atleast(dve, roots_made, u.count(0))
                    nc.vector.tensor_scalar(v[:, 0:8], pR[:, 0:8], EPS, None, ALU.add).then_inc(v1_made, 1)

                def roots(u):
                    if u.valid(DENSE):
                        dve.wait_ge(v1_made, u.count(1))
                    atleast(dve, v2_made, u.count(0) if u.valid(DENSE) else DENSE)
                    atleast(dve, out_made, u.count(-1))
                    inverse_roots(nc, dve, v[:, :], w[:, :], ta[:, :], tb[:, :], root_step, u.count(0), roots_made)

                def scale(u):
                    b = u.off % 2
                    dve.wait_ge(roots_made, u.count(1))
                    dve.wait_ge(g_rows_made, u.count(1))
                    atleast(dve, y_made, u.count(0))
                    nc.vector.tensor_tensor(yb[:, :, :], pG[b][:, :].rearrange("p (r f) -> p r f", f=F),
                                            w[:, 0:8].unsqueeze(2).to_broadcast([128, 8, F]), ALU.mult).then_inc(scaled, 1)
                    dve.wait_ge(scaled, u.count(1))
                    atleast(dve, out_made, u.count(-1))
                    nc.vector.tensor_tensor(yc[b][:, :, :], yb[:, :, :], pX[b][:, :].rearrange("p (r f) -> p r f", f=F),
                                            ALU.add).then_inc(y_made, 1)

                def sum_squares(u):
                    b = u.off % 2
                    dve.wait_ge(y_squared, u.count(1))
                    atleast(dve, v2_made, u.count(0))
                    nc.vector.tensor_reduce(s2[:, :], q2[b][:, :, :], AX.X, ALU.add).then_inc(y_summed, 1)
                    dve.wait_ge(y_summed, u.count(1))
                    dve.wait_ge(roots_made, u.count(1))
                    nc.vector.tensor_scalar(v[:, 8:16], s2[:, :], EPS, None, ALU.add)
                    nc.vector.tensor_scalar(v[:, 16:24], s2[:, :], 1.0 + EPS, EPS * EPS, ALU.mult, ALU.add)\
                        .then_inc(v2_made, 1)

                def finish(u):
                    b = u.off % 2
                    dve.wait_ge(roots_made, u.count(2))
                    atleast(dve, stored[b], u.halves(0) * 32)
                    nc.vector.tensor_tensor(xr[b][:, :, :], yc[b][:, :, :],
                                            w[:, 8:16].unsqueeze(2).to_broadcast([128, 8, F]), ALU.mult)
                    nc.vector.tensor_tensor(orow[b][:, :, :], yc[b][:, :, :],
                                            w[:, 16:24].unsqueeze(2).to_broadcast([128, 8, F]), ALU.mult)\
                        .then_inc(out_made, 1)

                def slot(u):
                    if u.static() and u.count(0) == 0:
                        nc.vector.memset(v[:, :], 1.0).then_inc(v_cleared, 1)
                        dve.wait_ge(v_cleared, 1)
                    if u.back(1).valid(DENSE):
                        residual(u.back(1))
                    if u.back(2).valid(DENSE):
                        add_eps(u.back(2))
                    if u.back(2).valid(DENSE + 1):
                        roots(u.back(2))
                    if u.back(2).valid(DENSE):
                        scale(u.back(2))
                    if u.back(3).valid(DENSE):
                        finish(u.back(3))
                    if u.back(2).valid(DENSE):
                        sum_squares(u.back(2))

                slots(dve, DENSE, 5, slot)

        scatter_rows = sb("scatter_rows", [128, TILES], i32)
        with ExitStack() as ph:
            sbp, semp = places(ph, "weigh")

            ids = sbp("ids", [QR, 3, 2, 128], i32)
            idf = sbp("idf", [QR, 3, 2, 128])
            rid = sbp("rid", [128, 2, TILES], i32)
            rif = sbp("rif", [128, 2, TILES])
            lg = sbp("lg", [QR, 2, CH, 128])
            goes_on = sbp("goes_on", [QR, 2, 128])
            lasts = sbp("lasts", [QR, 2, 128])
            stays = sbp("stays", [QR, 2, 128])
            drop = sbp("drop", [QR, 2, 128])
            narrow = sbp("narrow", [QR, 2, 2, 128], bf16)
            val = sbp("val", [QR, 2, 9, 128])
            pre = sbp("pre", [QR, 2, 9, 128])
            tot = sbp("tot", [QR, 2, 9, 128])
            loop = sbp("loop", [QR, 2, 4, 128])
            tmp = sbp("tmp", [QR, 2, 4, 128])
            peak = sbp("peak", [QR, 2, 4, 128])
            weight, rest = tot[:, :, 0:8, :], pre[:, :, 0:8, :]
            part = sbp("part", [QR, 3, 2, 8, 128], bf16)
            keep = sbp("keep", [QR, 4, 2])
            ends = sbp("ends", [QR, 2, 2, 9])
            rowT = sbp("rowT", [9, 2, 2, 2 * QR])
            chain = sbp("chain", [9, 2, 2 * QR + 1])
            carry = sbp("carry", [QR, 2, 9])

            loaded, ends_made, turned, chained, back, stepped, weights_done, exps_asked, exps_made, saved = (
                semp(n) for n in ("loaded", "ends_made", "turned", "chained", "back", "stepped", "weights_done",
                                  "exps_asked", "exps_made", "saved"))
            ROUNDS = [(0, 9, True, 4), (0, 9, False, 0), (0, 4, True, 0), (0, 4, False, 0)]
            block = ph.enter_context(nc.Block())

            @block.sync
            def _(sp):
                sp.dma_start(ids[:, :, :, :].rearrange("q a h j -> q (a h j)"), dblk).then_inc(loaded, 16)
                sp.dma_start(rid[:, :, :].rearrange("p a t -> p (a t)"), drow).then_inc(loaded, 16)
                for h in range(2):
                    sp.dma_start(lg[:, h, :, :],
                                 logit_rows[:, h * QR * 128:(h + 1) * QR * 128].rearrange("c (q j) -> q c j", j=128))\
                        .then_inc(loaded, 16)
                sp.wait_ge(weights_done, 1)
                for h in range(2):
                    span = slice(h * QR * 128, (h + 1) * QR * 128)
                    for a in range(3):
                        sp.dma_start(weight_rows[8 * a:8 * a + 8, span].rearrange("c (q j) -> q c j", j=128),
                                     part[:, a, h, :, :]).then_inc(saved, 16)
                    for a in range(2):
                        sp.dma_start(mask_rows[a, span].rearrange("(q j) -> q j", j=128), narrow[:, a, h, :])\
                            .then_inc(saved, 16)
                sp.wait_ge(saved, 16 * 10)

            @block.tensor
            def _(pe):
                for n, (c0_, c1_, forward, maxima) in enumerate(ROUNDS):
                    groups = [(c0_, maxima), (maxima, c1_)] if maxima else [(c0_, c1_)]
                    pe.wait_ge(ends_made, n + 1)
                    for g, (a, b) in enumerate(groups):
                        for k in range(2):
                            for h in range(2):
                                last = nc.tensor.transpose(bank[2 * g + k][0:b - a, h * QR:(h + 1) * QR],
                                                           ends[:, k, h, a:b], ident[0:QR, 0:QR])
                    last.then_inc(turned, 1)
                    pe.wait_ge(chained, n + 1)
                    for g, (a, b) in enumerate(groups):
                        for h in range(2):
                            first = h * QR + (0 if forward else 1)
                            last = nc.tensor.transpose(bank[4 + h][0:QR, a:b], chain[0:b - a, g, first:first + QR],
                                                       ident[0:b - a, 0:b - a])
                    last.then_inc(back, 1)

            @block.scalar
            def _(act):
                act.wait_ge(exps_asked, 1)
                nc.scalar.activation(val[:, :, 0:4, :], peak[:, :, :, :], ACT.Exp)
                nc.scalar.activation(loop[:, :, :, :], tmp[:, :, :, :], ACT.Exp).then_inc(exps_made, 1)

            @block.vector
            def _(dve):
                count = [0]

                def step(ins):
                    count[0] += 1
                    ins.then_inc(stepped, 1)
                    dve.wait_ge(stepped, count[0])

                def spread(t, n):
                    return t.unsqueeze(2).to_broadcast([QR, 2, n, 128])

                def scans(n, out_, from_, initial):
                    c0_, c1_, forward, maxima = ROUNDS[n]
                    for h in range(2):
                        for c in range(c0_, c1_):
                            o, f = out_[:, h, c, :], from_[:, h, c, :]
                            if forward and c < maxima:
                                last = nc.vector.tensor_tensor_scan(o, drop[:, h, :], f, initial(h, c), ALU.add, ALU.max)
                            elif forward:
                                last = nc.vector.tensor_tensor_scan(o, goes_on[:, h, :], f, initial(h, c), ALU.mult, ALU.add)
                            else:
                                last = nc.vector.tensor_tensor_scan(o[:, ::-1], stays[:, h, ::-1], f[:, ::-1],
                                                                    initial(h, c), ALU.mult, ALU.add)
                    return last

                def segment_scan(n, out_, from_):
                    c0_, c1_, forward, maxima = ROUNDS[n]
                    step(scans(n, out_, from_, lambda h, c: -BIG if forward and c < maxima else 0.0))
                    edge = 127 if forward else 0
                    nc.vector.tensor_copy(ends[:, 0, :, c0_:c1_], out_[:, :, c0_:c1_, edge])
                    if maxima:
                        nc.vector.tensor_copy(ends[:, 1, :, 0:maxima], keep[:, 2, :].unsqueeze(2).to_broadcast([QR, 2, maxima]))
                    nc.vector.tensor_copy(ends[:, 1, :, maxima:c1_],
                                          keep[:, 0 if forward else 1, :].unsqueeze(2).to_broadcast([QR, 2, c1_ - maxima]))\
                        .then_inc(ends_made, 1)
                    groups = [(c0_, maxima), (maxima, c1_)] if maxima else [(c0_, c1_)]
                    dve.wait_ge(turned, n + 1)
                    for g, (a, b) in enumerate(groups):
                        for k in range(2):
                            last = nc.vector.tensor_copy(rowT[0:b - a, g, k, :], bank[2 * g + k][0:b - a, 0:2 * QR])
                        start = -BIG if maxima and g == 0 else 0.0
                        first = 0 if forward else 2 * QR
                        last = nc.vector.memset(chain[0:b - a, g, first:first + 1], start)
                    step(last)
                    for g, (a, b) in enumerate(groups):
                        m = b - a
                        start = -BIG if maxima and g == 0 else 0.0
                        if forward:
                            ops = (ALU.add, ALU.max) if maxima and g == 0 else (ALU.mult, ALU.add)
                            last = nc.vector.tensor_tensor_scan(chain[0:m, g, 1:], rowT[0:m, g, 1, :], rowT[0:m, g, 0, :],
                                                                start, *ops)
                        else:
                            o = chain[0:m, g, 0:2 * QR]
                            last = nc.vector.tensor_tensor_scan(o[:, ::-1], rowT[0:m, g, 1, ::-1], rowT[0:m, g, 0, ::-1],
                                                                start, ALU.mult, ALU.add)
                    last.then_inc(chained, 1)
                    dve.wait_ge(back, n + 1)
                    for h in range(2):
                        last = nc.vector.tensor_copy(carry[:, h, c0_:c1_], bank[4 + h][0:QR, c0_:c1_])
                    step(last)
                    step(scans(n, out_, from_, lambda h, c: carry[:, h, c:c + 1]))

                dve.wait_ge(loaded, 64)
                nc.vector.tensor_copy(rif[:, :, :], rid[:, :, :])
                step(nc.vector.tensor_copy(idf[:, :, :, :], ids[:, :, :, :]))
                nc.vector.tensor_tensor(goes_on[:, :, :], idf[:, 0, :, :], idf[:, 1, :, :], ALU.is_equal)
                nc.vector.tensor_tensor(lasts[:, :, :], idf[:, 1, :, :], idf[:, 2, :, :], ALU.not_equal)
                nc.vector.tensor_tensor(stays[:, :, :], idf[:, 1, :, :], idf[:, 2, :, :], ALU.is_equal)
                step(nc.vector.tensor_tensor(rif[:, 1, :], rif[:, 0, :], rif[:, 1, :], ALU.is_equal))
                nc.vector.tensor_scalar(drop[:, :, :], goes_on[:, :, :], 1.0, BIG, ALU.subtract, ALU.mult)
                nc.vector.tensor_copy(narrow[:, 0, :, :], goes_on[:, :, :])
                nc.vector.tensor_reduce(keep[:, 0, :], goes_on[:, :, :], AX.X, ALU.min)
                nc.vector.tensor_reduce(keep[:, 1, :], stays[:, :, :], AX.X, ALU.min)
                step(nc.vector.scalar_tensor_tensor(rif[:, 0, :], rif[:, 1, :], SKIP, rif[:, 0, :], ALU.mult, ALU.max))
                nc.vector.tensor_copy(scatter_rows[:, :], rif[:, 0, :])
                nc.vector.tensor_copy(narrow[:, 1, :, :], drop[:, :, :])
                nc.vector.tensor_scalar(keep[:, 2, :], keep[:, 0, :], 1.0, BIG, ALU.subtract, ALU.mult)
                nc.vector.scalar_tensor_tensor(val[:, :, 0:4, :], lg[:, :, 0:4, :], 0.2, lg[:, :, 0:4, :], ALU.mult, ALU.max)
                nc.vector.tensor_copy(val[:, :, 4:8, :], lg[:, :, 4:8, :])
                step(nc.vector.memset(val[:, :, 8, :], 1.0))
                segment_scan(0, pre, val)
                step(nc.vector.tensor_tensor(pre[:, :, :, :], pre[:, :, :, :], spread(lasts[:, :, :], 9), ALU.mult))
                segment_scan(1, tot, pre)
                step(nc.vector.reciprocal(tot[:, :, 8, :], tot[:, :, 8, :]))
                step(nc.vector.tensor_tensor(loop[:, :, :, :], tot[:, :, 4:8, :], spread(tot[:, :, 8, :], 4), ALU.mult))
                step(nc.vector.tensor_tensor(tmp[:, :, :, :], loop[:, :, :, :], lg[:, :, 8:12, :], ALU.add))
                step(nc.vector.scalar_tensor_tensor(loop[:, :, :, :], tmp[:, :, :, :], 0.2, tmp[:, :, :, :], ALU.mult, ALU.max))
                step(nc.vector.tensor_tensor(rest[:, :, 0:4, :], loop[:, :, :, :], tot[:, :, 0:4, :], ALU.max))
                nc.vector.tensor_tensor(peak[:, :, :, :], val[:, :, 0:4, :], rest[:, :, 0:4, :], ALU.subtract)
                nc.vector.tensor_tensor(tmp[:, :, :, :], loop[:, :, :, :], rest[:, :, 0:4, :], ALU.subtract)\
                    .then_inc(exps_asked, 1)
                dve.wait_ge(exps_made, 1)
                segment_scan(2, pre, val)
                step(nc.vector.tensor_tensor(pre[:, :, 0:4, :], pre[:, :, 0:4, :], spread(lasts[:, :, :], 4), ALU.mult))
                segment_scan(3, tot, pre)
                step(nc.vector.tensor_tensor(peak[:, :, :, :], tot[:, :, 0:4, :], loop[:, :, :, :], ALU.add))
                step(nc.vector.reciprocal(tmp[:, :, :, :], peak[:, :, :, :]))
                nc.vector.tensor_tensor(weight[:, :, 0:4, :], val[:, :, 0:4, :], tmp[:, :, :, :], ALU.mult)
                step(nc.vector.tensor_tensor(peak[:, :, :, :], loop[:, :, :, :], tmp[:, :, :, :], ALU.mult))
                step(nc.vector.tensor_tensor(weight[:, :, 4:8, :], peak[:, :, :, :], spread(lasts[:, :, :], 4), ALU.mult))
                step(nc.vector.tensor_copy(part[:, 0, :, :, :], weight[:, :, :, :]))
                step(nc.vector.tensor_tensor(rest[:, :, :, :], weight[:, :, :, :], part[:, 0, :, :, :], ALU.subtract))
                step(nc.vector.tensor_copy(part[:, 1, :, :, :], rest[:, :, :, :]))
                step(nc.vector.tensor_tensor(weight[:, :, :, :], rest[:, :, :, :], part[:, 1, :, :, :], ALU.subtract))
                nc.vector.tensor_copy(part[:, 2, :, :, :], weight[:, :, :, :]).then_inc(weights_done, 1)

        with ExitStack() as ph:
            sbp, semp = places(ph, "first")

            wt = [sbp(f"wt{i}", [24, 2 * COLS], bf16) for i in range(2)]
            mask = [sbp(f"mask{i}", [128, COLS], bf16) for i in range(2)]
            zb = [sbp(f"zb{i}", [128, COLS]) for i in range(2)]
            ysum = sbp("ysum", [128, COLS])
            ys = [sbp(f"ys{i}", [128, COLS]) for i in range(2)]
            start = sbp("start", [128, 1])
            xd = [sbp(f"xd{i}", [128, COLS]) for i in range(2)]
            ex, rl, gb, hb, sq, hc = (sbp(n, [128, COLS]) for n in ("ex", "rl", "gb", "hb", "sq", "hc"))
            yb, yc, q2 = (sbp(n, [128, 8, F]) for n in ("yb", "yc", "q2"))
            xr = [sbp(f"xr{i}", [128, 8, F]) for i in range(2)]
            s2 = sbp("s2", [128, 8])
            v, w, ta, tb = (sbp(n, [128, 16]) for n in ("v", "w", "ta", "tb"))
            stage = [sbp(f"stage{i}", [128, 8], i32) for i in range(2)]
            pB, pY, pX, pH, pR, pG = [bank[0], bank[1]], bank[2], bank[3], bank[4], bank[5], bank[6]
            pC = bank[7]

            w_loaded = [semp(f"w_loaded{i}") for i in range(2)]
            scattered = [semp(f"scattered{i}") for i in range(2)]
            (spread_made, z_made, z_used, y_made, y_copied, halfway, crossed, summed, ended, xd_made, xd_copied,
             e_made, g_made, h_made, hc_made, sq_made, var_made, rows_made, v1_made, roots_made, root_step, scaled,
             yc_made, squared, s_made, v2_made, xr_made, a_staged, b_staged, cleared) = (semp(n) for n in (
                 "spread_made", "z_made", "z_used", "y_made", "y_copied", "halfway", "crossed", "summed", "ended",
                 "xd_made", "xd_copied", "e_made", "g_made", "h_made", "hc_made", "sq_made", "var_made", "rows_made",
                 "v1_made", "roots_made", "root_step", "scaled", "yc_made", "squared", "s_made", "v2_made", "xr_made",
                 "a_staged", "b_staged", "cleared"))
            block = ph.enter_context(nc.Block())

            def columns(u, s):
                return bass.ds(u.count(0) * (2 * COLS) + s * COLS, COLS)

            @block.sync
            def _(sp):
                def load(u):
                    b = u.off % 2
                    atleast(sp, summed, u.count(-1))
                    sp.dma_start(wt[b][:, :], weight_rows[:, bass.ds(u.count(0) * 2 * COLS, 2 * COLS)])\
                        .then_inc(w_loaded[b], 16)
                    for s in range(2):
                        sp.dma_start(mask[b][64 * s:64 * s + 64, :],
                                     mask_rows[0:1, columns(u, s)].to_broadcast([64, COLS])).then_inc(w_loaded[b], 16)

                def slot(u):
                    if u.static() and u.count(0) == 0:
                        load(u)
                    if u.back(-1).valid(PAIRS):
                        load(u.back(-1))

                slots(sp, PAIRS, 3, slot)

            @block.gpsimd
            def _(pool):
                def stage_part(u, s, staged):
                    if not u.valid(PAIRS):
                        return
                    atleast(pool, scattered[u.off % 2], u.halves(0) * 128)
                    nc.gpsimd.tensor_copy(stage[u.off % 2][:, 4 * s:4 * s + 4],
                                          scatter_rows[:, bass.ds(u.count(0) * 8 + 4 * s, 4)]).then_inc(staged, 1)

                def scatter(u, s):
                    b = u.off % 2
                    for j in range(4):
                        pool.indirect_dma_start(
                            out=x1, out_offset=bass.IndirectOffsetOnAxis(ap=stage[b][:, 4 * s + j:4 * s + j + 1], axis=0),
                            in_=xr[b][:, 2 * j + s, :], in_offset=None, bounds_check=last_row, oob_is_err=False)\
                            .then_inc(scattered[b], 16)

                last_row = pool.alloc_register("last_row")
                pool.reg_mov(last_row, N - 1)

                def slot(u):
                    if u.static() and u.count(0) == 0:
                        stage_part(u, 0, a_staged)
                    u = u.back(2)
                    if not u.valid(PAIRS):
                        return
                    pool.wait_ge(xr_made, u.count(1))
                    pool.wait_ge(a_staged, u.count(1))
                    stage_part(u, 1, b_staged)
                    scatter(u, 0)
                    pool.wait_ge(b_staged, u.count(1))
                    stage_part(u.back(-1), 0, a_staged)
                    scatter(u, 1)

                slots(pool, PAIRS, 3, slot)
                for b in range(2):
                    pool.wait_ge(scattered[b], 128 * ((PAIRS + 1 - b) // 2))

            @block.tensor
            def _(pe):
                def sums(u):
                    b = u.off % 2
                    pe.wait_ge(w_loaded[b], u.halves(1) * 48)
                    for n in range(2 * H + 1):
                        if n < 2 * H:
                            s, h = n // H, n % H
                            atleast(pe, z_made, u.count(0) * (2 * H) + (n - 1))
                            nc.tensor.matmul(pB[n % 2][:, :], headsel[:, h, :], wt[b][:, s * COLS:(s + 1) * COLS],
                                             start=True, stop=True).then_inc(spread_made, 1)
                        if n:
                            s, h = (n - 1) // H, (n - 1) % H
                            if n == 1:
                                atleast(pe, y_copied, u.count(0))
                            pe.wait_ge(z_made, u.count(0) * (2 * H) + n)
                            last = nc.tensor.matmul(pY[64 * s:64 * s + 64, :], Mstack[:, h, :], zb[(n - 1) % 2][:, :],
                                                    start=(h == 0), stop=(h == H - 1))
                            last.then_inc(z_used, 1)
                    atleast(pe, xd_copied, u.count(0))
                    nc.tensor.matmul(pX[:, :], c128("xdA"), XT[:, columns(u, 0)], start=True, stop=False)
                    nc.tensor.matmul(pX[:, :], c128("xdB"), XT[:, columns(u, 1)], start=False, stop=True).then_inc(xd_made, 1)

                def centre(u):
                    pe.wait_ge(h_made, u.count(1))
                    atleast(pe, sq_made, u.count(0))
                    nc.tensor.matmul(pH[:, :], Cm, hb[:, :], start=True, stop=True).then_inc(hc_made, 1)

                def to_rows(u):
                    b = u.off % 2
                    pe.wait_ge(sq_made, u.count(1))
                    atleast(pe, v1_made, u.count(0))
                    for j in range(4):
                        last = nc.tensor.matmul(pR[:, 2 * j:2 * j + 2], sq[:, j * 128:(j + 1) * 128], c128("ind"),
                                                start=True, stop=True)
                    last.then_inc(var_made, 1)
                    atleast(pe, yc_made, u.count(0))
                    for j in range(4):
                        c = slice(j * 128, (j + 1) * 128)
                        nc.tensor.matmul(pG[:, c], hc[:, c], CG[:, :], start=True, stop=True)
                        last = nc.tensor.matmul(pC[:, c], xd[b][:, c], Cm, start=True, stop=True)
                    last.then_inc(rows_made, 1)

                def slot(u):
                    if u.back(1).valid(PAIRS):
                        centre(u.back(1))
                        to_rows(u.back(1))
                    if u.valid(PAIRS):
                        sums(u)

                slots(pe, PAIRS, 3, slot)

            @block.scalar
            def _(act):
                def copies(u):
                    b = u.off % 2
                    act.wait_ge(y_made_of(u), u.count(1) * (2 * H))
                    atleast(act, summed, u.count(0))
                    nc.scalar.activation(ysum[:, :], pY[:, :], ACT.Copy).then_inc(y_copied, 1)
                    act.wait_ge(xd_made, u.count(1))
                    atleast(act, rows_made, u.count(-1))
                    nc.scalar.activation(xd[b][:, :], pX[:, :], ACT.Identity, bias=c128("beta")).then_inc(xd_copied, 1)
                    act.wait_ge(halfway, u.count(1))
                    nc.scalar.activation(start[64:128, :], ys[b][0:64, COLS - 1:COLS], ACT.Copy).then_inc(crossed, 1)
                    act.wait_ge(summed, u.count(1))
                    nc.scalar.activation(start[0:64, :], ys[b][64:128, COLS - 1:COLS], ACT.Copy).then_inc(crossed, 1)

                def y_made_of(u):
                    return z_used

                def elu_parts(u):
                    b = u.off % 2
                    act.wait_ge(summed, u.count(1))
                    atleast(act, g_made, u.count(0))
                    nc.scalar.activation(ex[:, :], ys[b][:, :], ACT.Exp, bias=c0[:, :])
                    nc.scalar.activation(rl[:, :], ys[b][:, :], ACT.Relu, bias=c0[:, :]).then_inc(e_made, 1)

                def square(u):
                    act.wait_ge(hc_made, u.count(1))
                    atleast(act, rows_made, u.count(0))
                    nc.scalar.activation(sq[:, :], pH[:, :], ACT.Square, bias=ncbeta[:, :])
                    nc.scalar.activation(hc[:, :], pH[:, :], ACT.Identity, bias=ncbeta[:, :]).then_inc(sq_made, 1)

                def square_y(u):
                    act.wait_ge(yc_made, u.count(1))
                    atleast(act, s_made, u.count(0))
                    nc.scalar.activation(q2[:, :, :], yc[:, :, :], ACT.Square, scale=F ** -0.5).then_inc(squared, 1)

                def slot(u):
                    if u.back(1).valid(PAIRS):
                        elu_parts(u.back(1))
                        square(u.back(1))
                        square_y(u.back(1))
                    if u.valid(PAIRS):
                        copies(u)

                slots(act, PAIRS, 3, slot)

            @block.vector
            def _(dve):
                def products(u):
                    for n in range(2 * H):
                        s = n // H
                        dve.wait_ge(spread_made, u.count(0) * (2 * H) + (n + 1))
                        atleast(dve, z_used, u.count(0) * (2 * H) + (n - 1))
                        nc.vector.tensor_tensor(zb[n % 2][:, :], pB[n % 2][:, :], XT[:, columns(u, s)], ALU.mult)\
                            .then_inc(z_made, 1)

                def segment_sums(u):
                    b = u.off % 2
                    dve.wait_ge(y_copied, u.count(1))
                    atleast(dve, e_made, u.count(-1))
                    atleast(dve, crossed, u.count(0) * 2)
                    nc.vector.tensor_tensor_scan(ys[b][0:64, :], mask[b][0:64, :], ysum[0:64, :], start[0:64, :],
                                                 ALU.mult, ALU.add).then_inc(halfway, 1)
                    dve.wait_ge(crossed, u.count(0) * 2 + 1)
                    nc.vector.tensor_tensor_scan(ys[b][64:128, :], mask[b][64:128, :], ysum[64:128, :], start[64:128, :],
                                                 ALU.mult, ALU.add).then_inc(summed, 1)

                def residual(u):
                    b = u.off % 2
                    dve.wait_ge(e_made, u.count(1))
                    atleast(dve, h_made, u.count(0))
                    nc.vector.scalar_tensor_tensor(gb[:, :], ex[:, :], 1.0, rl[:, :], ALU.min, ALU.add).then_inc(g_made, 1)
                    atleast(dve, hc_made, u.count(0))
                    dve.wait_ge(g_made, u.count(1))
                    dve.wait_ge(xd_copied, u.count(1))
                    nc.vector.tensor_tensor(hb[:, :], gb[:, :], xd[b][:, :], ALU.add).then_inc(h_made, 1)

                def norms(u):
                    dve.wait_ge(var_made, u.count(1))
                    nc.vector.tensor_scalar(v[:, 0:8], pR[:, 0:8], EPS, None, ALU.add).then_inc(v1_made, 1)
                    dve.wait_ge(v1_made, u.count(1))
                    inverse_roots(nc, dve, v[:, 0:8], w[:, 0:8], ta[:, 0:8], tb[:, 0:8], root_step, u.count(0) * 2, roots_made)
                    dve.wait_ge(roots_made, u.count(0) * 2 + 1)
                    dve.wait_ge(rows_made, u.count(1))
                    nc.vector.tensor_tensor(yb[:, :, :], pG[:, :].rearrange("p (r f) -> p r f", f=F),
                                            w[:, 0:8].unsqueeze(2).to_broadcast([128, 8, F]), ALU.mult).then_inc(scaled, 1)
                    dve.wait_ge(scaled, u.count(1))
                    atleast(dve, xr_made, u.count(0))
                    nc.vector.tensor_tensor(yc[:, :, :], yb[:, :, :], pC[:, :].rearrange("p (r f) -> p r f", f=F),
                                            ALU.add).then_inc(yc_made, 1)

                def finish(u):
                    b = u.off % 2
                    dve.wait_ge(squared, u.count(1))
                    nc.vector.tensor_reduce(s2[:, :], q2[:, :, :], AX.X, ALU.add).then_inc(s_made, 1)
                    dve.wait_ge(s_made, u.count(1))
                    nc.vector.tensor_scalar(v[:, 8:16], s2[:, :], EPS, None, ALU.add).then_inc(v2_made, 1)
                    dve.wait_ge(v2_made, u.count(1))
                    inverse_roots(nc, dve, v[:, 8:16], w[:, 8:16], ta[:, 8:16], tb[:, 8:16], root_step,
                                  u.count(0) * 2 + 1, roots_made)
                    dve.wait_ge(roots_made, u.count(1) * 2)
                    atleast(dve, scattered[b], u.halves(0) * 128)
                    nc.vector.tensor_tensor(xr[b][:, :, :], yc[:, :, :],
                                            w[:, 8:16].unsqueeze(2).to_broadcast([128, 8, F]), ALU.mult).then_inc(xr_made, 1)

                def slot(u):
                    if u.static() and u.count(0) == 0:
                        nc.vector.memset(start[:, :], 0.0).then_inc(cleared, 1)
                        dve.wait_ge(cleared, 1)
                    if u.back(1).valid(PAIRS):
                        residual(u.back(1))
                        norms(u.back(1))
                    if u.valid(PAIRS):
                        products(u)
                    if u.back(1).valid(PAIRS):
                        finish(u.back(1))
                    if u.valid(PAIRS):
                        segment_sums(u)

                slots(dve, PAIRS, 3, slot)

        with ExitStack() as dist:
            D = XT[:, 0:PAIRS * COLS]
            with ExitStack() as ph:
                sbp, semp = places(ph, "dist")

                ea = [sbp(f"ea{i}", [7, COLS]) for i in range(2)]
                sq = [sbp(f"sq{i}", [128, 8, F]) for i in range(2)]
                nrm = [sbp(f"nrm{i}", [128, 8, F]) for i in range(2)]
                d1 = sbp("d1", [128, COLS])
                s2 = [sbp(f"s2{i}", [128, 8]) for i in range(2)]
                v, w, ta, tb = (sbp(n, [128, 16]) for n in ("v", "w", "ta", "tb"))
                pL, pT = [bank[0], bank[1]], [bank[2], bank[3]]
                ea_in = [semp(f"ea_in{i}") for i in range(2)]
                lin, sqd, smd, vmd, rtd, nmd, tnd, gld = ([semp(f"{n}{i}") for i in range(2)] for n in (
                    "linear_made", "squares_made", "squares_summed", "v_made", "roots_made", "normed", "turned",
                    "gelu_made"))
                steps = [semp(f"root_step{i}") for i in range(2)]
                block = ph.enter_context(nc.Block())

                @block.sync
                def _(sp):
                    def slot(u):
                        if not u.valid(PAIRS):
                            return
                        atleast(sp, lin[0], u.count(-1))
                        sp.dma_start(ea[u.off % 2][:, :], ea3[:, bass.ds(u.count(0) * COLS, COLS)])\
                            .then_inc(ea_in[u.off % 2], 16)

                    slots(sp, PAIRS, 1, slot)

                @block.tensor
                def _(pe):
                    def first(u):
                        pe.wait_ge(ea_in[u.off % 2], u.halves(1) * 16)
                        atleast(pe, nmd[0], u.count(0))
                        for j in range(4):
                            c = slice(j * 128, (j + 1) * 128)
                            last = nc.tensor.matmul(pL[0][:, c], ea[u.off % 2][:, c], Wd1[:, :], start=True, stop=True)
                        last.then_inc(lin[0], 1)

                    def second(u):
                        pe.wait_ge(gld[0], u.count(1))
                        atleast(pe, nmd[1], u.count(0))
                        for j in range(4):
                            c = slice(j * 128, (j + 1) * 128)
                            nc.tensor.matmul(pL[1][:, c], d1[:, c], Wd2[:, :], start=True, stop=False)
                            last = nc.tensor.matmul(pL[1][:, c], ones[:, :], b2row[:, :], start=False, stop=True)
                        last.then_inc(lin[1], 1)

                    def turn(n, u):
                        pe.wait_ge(nmd[n], u.count(1))
                        atleast(pe, gld[n], u.count(0))
                        for j in range(4):
                            last = nc.tensor.transpose(
                                pT[n][:, j * 128:(j + 1) * 128],
                                nrm[n][:, 2 * j:2 * j + 2, :].rearrange("p r f -> p (r f)"), ident)
                        last.then_inc(tnd[n], 1)

                    def slot(u):
                        if u.valid(PAIRS):
                            first(u)
                        if u.back(1).valid(PAIRS):
                            second(u.back(1))
                        if u.valid(PAIRS):
                            turn(0, u)
                        if u.back(1).valid(PAIRS):
                            turn(1, u.back(1))

                    slots(pe, PAIRS, 1, slot)

                @block.scalar
                def _(act):
                    def square(n, u):
                        act.wait_ge(lin[n], u.count(1))
                        atleast(act, smd[n], u.count(0))
                        nc.scalar.activation(sq[n][:, :, :], pL[n][:, :].rearrange("p (r f) -> p r f", f=F), ACT.Square,
                                             scale=F ** -0.5).then_inc(sqd[n], 1)

                    def gelu(n, u):
                        act.wait_ge(tnd[n], u.count(1))
                        if n == 0:
                            atleast(act, lin[1], u.count(0))
                            nc.scalar.activation(d1[:, :], pT[0][:, :], ACT.Gelu, bias=c128("b1"), scale=c128("g1"))\
                                .then_inc(gld[0], 1)
                        else:
                            nc.scalar.activation(D[:, bass.ds(u.count(0) * COLS, COLS)], pT[1][:, :], ACT.Gelu,
                                                 bias=c128("b2"), scale=c128("g2")).then_inc(gld[1], 1)

                    def slot(u):
                        if u.valid(PAIRS):
                            square(0, u)
                        if u.back(1).valid(PAIRS):
                            square(1, u.back(1))
                        if u.valid(PAIRS):
                            gelu(0, u)
                        if u.back(1).valid(PAIRS):
                            gelu(1, u.back(1))

                    slots(act, PAIRS, 1, slot)

                @block.vector
                def _(dve):
                    def norm(n, u):
                        h = slice(8 * n, 8 * n + 8)
                        dve.wait_ge(sqd[n], u.count(1))
                        nc.vector.tensor_reduce(s2[n][:, :], sq[n][:, :, :], AX.X, ALU.add).then_inc(smd[n], 1)
                        dve.wait_ge(smd[n], u.count(1))
                        nc.vector.tensor_scalar(v[:, h], s2[n][:, :], EPS, None, ALU.add).then_inc(vmd[n], 1)
                        dve.wait_ge(vmd[n], u.count(1))
                        inverse_roots(nc, dve, v[:, h], w[:, h], ta[:, h], tb[:, h], steps[n], u.count(0), rtd[n])
                        dve.wait_ge(rtd[n], u.count(1))
                        atleast(dve, tnd[n], u.count(0))
                        nc.vector.tensor_tensor(nrm[n][:, :, :], pL[n][:, :].rearrange("p (r f) -> p r f", f=F),
                                                w[:, h].unsqueeze(2).to_broadcast([128, 8, F]), ALU.mult).then_inc(nmd[n], 1)

                    def slot(u):
                        if u.valid(PAIRS):
                            norm(0, u)
                        if u.back(1).valid(PAIRS):
                            norm(1, u.back(1))

                    slots(dve, PAIRS, 1, slot)

            with ExitStack() as ph:
                sbp, semp = places(ph, "second")

                stage = [sbp(f"stage{i}", [128, 12], i32) for i in range(2)]
                pairs = [sbp(f"pairs{i}", [128, 4, 2 * F]) for i in range(4)]
                mask = [sbp(f"mask{i}", [128, COLS], bf16) for i in range(2)]
                xe = [sbp(f"xe{i}", [128, COLS]) for i in range(2)]
                top = [sbp(f"top{i}", [128, COLS + 1]) for i in range(2)]
                fall, below = sbp("fall", [128, COLS]), sbp("below", [128, COLS])
                fell = sbp("fell", [128, COLS])
                decay = [sbp(f"decay{i}", [128, COLS]) for i in range(2)]
                term = [sbp(f"term{i}", [128, COLS]) for i in range(2)]
                sums = [sbp(f"sums{i}", [128, COLS]) for i in range(2)]
                inv, quo = sbp("inv", [128, 4, F]), sbp("quo", [128, 4, F])
                res, cen, sqr = sbp("res", [128, 4, F]), sbp("cen", [128, 4, F]), sbp("sqr", [128, 4, F])
                orow = [sbp(f"orow{i}", [128, 4, F]) for i in range(2)]
                mean, nmean, s2 = sbp("mean", [128, 4]), sbp("nmean", [128, 4]), sbp("s2", [128, 4])
                v, w, ta, tb = (sbp(n, [128, 4]) for n in ("v", "w", "ta", "tb"))
                pA, pL, pW, pS = bank[0], [bank[1], bank[2]], [bank[3], bank[4]], [bank[5], bank[6]]

                gathered = [semp(f"gathered{i}") for i in range(2)]
                scattered = [semp(f"scattered{i}") for i in range(2)]
                mask_in = [semp(f"mask_in{i}") for i in range(2)]
                (s_staged, t_staged, o_staged, turned, copied, linear, topped, carried, fall_made, fell_made, below_made,
                 exps_made, term_made, summed, rows_made, inv_made, quo_made, res_made, mean_made, nmean_made, cen_made,
                 sqr_made, s2_made, v_made, root_step, roots_made, out_made, cleared) = (semp(n) for n in (
                     "s_staged", "t_staged", "o_staged", "turned", "copied", "linear", "topped", "carried", "fall_made",
                     "fell_made", "below_made", "exps_made", "term_made", "summed", "rows_made", "inv_made", "quo_made",
                     "res_made", "mean_made", "nmean_made", "cen_made", "sqr_made", "s2_made", "v_made", "root_step",
                     "roots_made", "out_made", "cleared"))
                block = ph.enter_context(nc.Block())

                @block.sync
                def _(sp):
                    def slot(u):
                        if not u.valid(UNITS):
                            return
                        b = u.off % 2
                        atleast(sp, fell_made, u.count(-1))
                        sp.dma_start(mask[b][:, :], mask_rows[1:2, bass.ds(u.count(0) * COLS, COLS)].to_broadcast([128, COLS]))\
                            .then_inc(mask_in[b], 16)

                    slots(sp, UNITS, 1, slot)

                @block.gpsimd
                def _(pool):
                    last_row = pool.alloc_register("last_out_row")
                    pool.reg_mov(last_row, N - 1)

                    def stage_gather(u, k, staged):
                        if u.valid(UNITS):
                            atleast(pool, gathered[u.off % 2], u.halves(0) * 128)
                            nc.gpsimd.tensor_copy(stage[u.off % 2][:, k:k + 4], gix[:, bass.ds(u.count(0) * 8 + k, 4)])\
                                .then_inc(staged, 1)

                    def stage_scatter(u):
                        if u.valid(UNITS):
                            atleast(pool, scattered[u.off % 2], u.halves(0) * 64)
                            nc.gpsimd.tensor_copy(stage[u.off % 2][:, 8:12], scatter_rows[:, bass.ds(u.count(0) * 4, 4)])\
                                .then_inc(o_staged, 1)

                    def gather(u, js):
                        a = u.off % 2
                        for j in js:
                            pool.indirect_dma_start(
                                out=pairs[u.off % 4][:, j % 4, F * (j // 4):F * (j // 4) + F], out_offset=None, in_=x1,
                                in_offset=bass.IndirectOffsetOnAxis(ap=stage[a][:, j:j + 1], axis=0))\
                                .then_inc(gathered[a], 16)

                    def scatter(u):
                        a = u.off % 2
                        for j in range(4):
                            pool.indirect_dma_start(
                                out=out, out_offset=bass.IndirectOffsetOnAxis(ap=stage[a][:, 8 + j:9 + j], axis=0),
                                in_=orow[a][:, j, :], in_offset=None, bounds_check=last_row, oob_is_err=False)\
                                .then_inc(scattered[a], 16)

                    def slot(u):
                        if u.static() and u.count(0) == 0:
                            stage_gather(u, 0, s_staged)
                        if u.valid(UNITS):
                            atleast(pool, res_made, u.count(-3))
                            pool.wait_ge(s_staged, u.count(1))
                            stage_gather(u, 4, t_staged)
                            gather(u, range(4))
                            pool.wait_ge(t_staged, u.count(1))
                        o = u.back(3)
                        if u.valid(UNITS):
                            if o.valid(UNITS):
                                stage_scatter(o)
                            else:
                                stage_gather(u.back(-1), 0, s_staged)
                            gather(u, range(4, 8))
                        elif o.valid(UNITS):
                            stage_scatter(o)
                        if o.valid(UNITS):
                            pool.wait_ge(out_made, o.count(1))
                            pool.wait_ge(o_staged, o.count(1))
                            if u.valid(UNITS):
                                stage_gather(u.back(-1), 0, s_staged)
                            scatter(o)

                    slots(pool, UNITS, 4, slot)
                    for b in range(2):
                        pool.wait_ge(scattered[b], 64 * (UNITS // 2))

                @block.tensor
                def _(pe):
                    def turn(u):
                        pe.wait_ge(gathered[u.off % 2], u.halves(1) * 128)
                        atleast(pe, copied, u.count(0))
                        for j in range(4):
                            last = nc.tensor.transpose(pA[:, j * 128:(j + 1) * 128], pairs[u.off % 4][:, j, :], ident)
                        last.then_inc(turned, 1)

                    def logits(u):
                        b = u.off % 2
                        pe.wait_ge(copied, u.count(1))
                        atleast(pe, term_made, u.count(-1))
                        d = D[:, bass.ds(u.halves(0) * COLS, COLS)]
                        sel = c128("dA") if b == 0 else c128("dB")
                        nc.tensor.matmul(pL[b][:, :], c128("Wqq"), xe[b][:, :], start=True, stop=False)
                        nc.tensor.matmul(pL[b][:, :], sel, d, start=False, stop=True)
                        nc.tensor.matmul(pW[b][:, :], c128("Wv"), xe[b][:, :], start=True, stop=False)
                        nc.tensor.matmul(pW[b][:, :], sel, d, start=False, stop=True).then_inc(linear, 1)

                    def turn_sums(u):
                        b = u.off % 2
                        pe.wait_ge(summed, u.count(1))
                        atleast(pe, quo_made, u.count(-1))
                        for j in range(4):
                            last = nc.tensor.transpose(pS[b][:, j * 128:(j + 1) * 128], sums[b][:, j * 128:(j + 1) * 128], ident)
                        last.then_inc(rows_made, 1)

                    def slot(u):
                        if u.valid(UNITS):
                            turn(u)
                            logits(u)
                        if u.back(1).valid(UNITS):
                            turn_sums(u.back(1))

                    slots(pe, UNITS, 4, slot)

                @block.scalar
                def _(act):
                    def copy(u):
                        b = u.off % 2
                        act.wait_ge(turned, u.count(1))
                        atleast(act, linear, u.count(-1))
                        nc.scalar.activation(xe[b][:, :], pA[:, :], ACT.Copy).then_inc(copied, 1)

                    def exps(u):
                        b = u.off % 2
                        act.wait_ge(below_made, u.count(1))
                        act.wait_ge(fell_made, u.count(1))
                        atleast(act, summed, u.count(-1))
                        nc.scalar.activation(decay[b][:, :], fell[:, :], ACT.Exp)
                        nc.scalar.activation(term[b][:, :], below[:, :], ACT.Exp).then_inc(exps_made, 1)

                    def square(u):
                        act.wait_ge(cen_made, u.count(1))
                        nc.scalar.activation(sqr[:, :, :], cen[:, :, :], ACT.Square, scale=F ** -0.5).then_inc(sqr_made, 1)

                    def slot(u):
                        if u.valid(UNITS):
                            copy(u)
                        if u.back(2).valid(UNITS):
                            square(u.back(2))
                        if u.back(1).valid(UNITS):
                            exps(u.back(1))

                    slots(act, UNITS, 4, slot)

                @block.vector
                def _(dve):
                    def maxima(u):
                        b = u.off % 2
                        before = top[1 - b][:, COLS:COLS + 1]
                        dve.wait_ge(linear, u.count(1))
                        dve.wait_ge(mask_in[b], u.halves(1) * 16)
                        atleast(dve, topped, u.count(0))
                        atleast(dve, fall_made, u.count(-1))
                        nc.vector.tensor_copy(top[b][:, 0:1], before).then_inc(carried, 1)
                        nc.vector.tensor_tensor_scan(top[b][:, 1:], mask[b][:, :], pL[b][:, :], before, ALU.add, ALU.max)\
                            .then_inc(topped, 1)
                        dve.wait_ge(carried, u.count(1))
                        dve.wait_ge(topped, u.count(1))
                        atleast(dve, fell_made, u.count(0))
                        nc.vector.tensor_tensor(fall[:, :], top[b][:, 0:COLS], top[b][:, 1:], ALU.subtract).then_inc(fall_made, 1)
                        atleast(dve, exps_made, u.count(0))
                        nc.vector.tensor_tensor(below[:, :], pL[b][:, :], top[b][:, 1:], ALU.subtract).then_inc(below_made, 1)
                        dve.wait_ge(fall_made, u.count(1))
                        nc.vector.tensor_tensor(fell[:, :], fall[:, :], mask[b][:, :], ALU.add).then_inc(fell_made, 1)

                    def segment_sums(u):
                        b = u.off % 2
                        dve.wait_ge(exps_made, u.count(1))
                        nc.vector.tensor_tensor(term[b][64:128, :], term[b][64:128, :], pW[b][64:128, :], ALU.mult)\
                            .then_inc(term_made, 1)
                        dve.wait_ge(term_made, u.count(1))
                        atleast(dve, summed, u.count(0))
                        atleast(dve, rows_made, u.count(-1))
                        nc.vector.tensor_tensor_scan(sums[b][:, :], decay[b][:, :], term[b][:, :],
                                                     sums[1 - b][:, COLS - 1:COLS], ALU.mult, ALU.add).then_inc(summed, 1)

                    def result(u):
                        b = u.off % 2
                        dve.wait_ge(rows_made, u.count(1))
                        r = pS[b][:, :].rearrange("p (t s f) -> p t s f", t=4, s=2)
                        atleast(dve, quo_made, u.count(0))
                        nc.vector.reciprocal(inv[:, :, :], r[:, :, 0, :]).then_inc(inv_made, 1)
                        dve.wait_ge(inv_made, u.count(1))
                        atleast(dve, res_made, u.count(0))
                        nc.vector.tensor_tensor(quo[:, :, :], r[:, :, 1, :], inv[:, :, :], ALU.mult).then_inc(quo_made, 1)
                        dve.wait_ge(quo_made, u.count(1))
                        atleast(dve, cen_made, u.count(0))
                        nc.vector.tensor_tensor(res[:, :, :], quo[:, :, :], pairs[u.off % 4][:, :, F:2 * F], ALU.add).then_inc(res_made, 1)
                        dve.wait_ge(res_made, u.count(1))
                        nc.vector.tensor_reduce(mean[:, :], res[:, :, :], AX.X, ALU.add).then_inc(mean_made, 1)
                        dve.wait_ge(mean_made, u.count(1))
                        nc.vector.tensor_scalar(nmean[:, :], mean[:, :], -1.0 / F, None, ALU.mult).then_inc(nmean_made, 1)
                        dve.wait_ge(nmean_made, u.count(1))
                        atleast(dve, out_made, u.count(0))
                        nc.vector.tensor_tensor(cen[:, :, :], res[:, :, :], nmean[:, :].unsqueeze(2).to_broadcast([128, 4, F]),
                                                ALU.add).then_inc(cen_made, 1)

                    def norm(u):
                        b = u.off % 2
                        dve.wait_ge(sqr_made, u.count(1))
                        nc.vector.tensor_reduce(s2[:, :], sqr[:, :, :], AX.X, ALU.add).then_inc(s2_made, 1)
                        dve.wait_ge(s2_made, u.count(1))
                        nc.vector.tensor_scalar(v[:, :], s2[:, :], EPS, None, ALU.add).then_inc(v_made, 1)
                        dve.wait_ge(v_made, u.count(1))
                        inverse_roots(nc, dve, v[:, :], w[:, :], ta[:, :], tb[:, :], root_step, u.count(0), roots_made)
                        dve.wait_ge(roots_made, u.count(1))
                        atleast(dve, scattered[b], u.halves(0) * 64)
                        nc.vector.tensor_tensor(orow[b][:, :, :], cen[:, :, :], w[:, :].unsqueeze(2).to_broadcast([128, 4, F]),
                                                ALU.mult).then_inc(out_made, 1)

                    def slot(u):
                        if u.static() and u.count(0) == 0:
                            nc.vector.memset(top[1][:, COLS:COLS + 1], -BIG)
                            nc.vector.memset(sums[1][:, COLS - 1:COLS], 0.0).then_inc(cleared, 1)
                            dve.wait_ge(cleared, 1)
                        if u.back(2).valid(UNITS):
                            result(u.back(2))
                        if u.back(1).valid(UNITS):
                            maxima(u.back(1))
                        if u.back(2).valid(UNITS):
                            norm(u.back(2))
                        if u.back(1).valid(UNITS):
                            segment_sums(u.back(1))

                    slots(dve, UNITS, 4, slot)


def _layout(a):
    import numpy as np
    src, dst = a["src"], a["dst"]
    pad = EP - E

    def rows(v):
        return np.ascontiguousarray(v.reshape(TILES, 128).T)

    def blocks(v):
        return np.ascontiguousarray(v.reshape(2, QR, 128).transpose(1, 0, 2))

    zero = np.zeros(pad, np.int32)
    s_rows, d_rows = rows(np.concatenate([src, zero])), rows(np.concatenate([dst, zero]))
    gidx = np.stack([s_rows.reshape(128, UNITS, 4), d_rows.reshape(128, UNITS, 4)], axis=2)
    own = np.arange(N, N + pad, dtype=np.int32)
    d = np.concatenate([dst, own])
    edge = np.array([-1], np.int32)
    before, after = np.concatenate([edge, d[:-1]]), np.concatenate([d[1:], edge])
    dblk = np.stack([blocks(before), blocks(d), blocks(after)], axis=1)
    drow = np.stack([rows(d), rows(after)], axis=1)
    eaT = np.concatenate([a["edge_attr_16"].T, np.zeros((16, pad), np.float32)], axis=1)
    e3 = np.concatenate([a["edge_attr_3"].T, np.zeros((3, pad), np.float32)], axis=1)
    ea3 = e3.reshape(3, PAIRS, 2, COLS).transpose(2, 0, 1, 3).reshape(6, PAIRS * COLS)
    ea3 = np.concatenate([ea3, np.ones((1, PAIRS * COLS), np.float32)], axis=0)

    def twice(v):
        return np.concatenate([v, v], axis=-1)

    W, Wp, We = a["L0_gnn_W"], a["L0_gnn_Wp"], a["L0_gnn_W_edge"]
    p64 = np.concatenate([
        twice(W.reshape(F, H, F).transpose(2, 1, 0)).reshape(F, -1),
        twice(Wp.reshape(H, F, F).transpose(1, 0, 2)).reshape(F, -1),
        We.reshape(16, H, F).transpose(2, 1, 0).reshape(F, -1),
        a["L0_gnn_att_src"].T, a["L0_gnn_att_dst"].T, a["L0_gnn_att_edge"].T,
        a["L0_gnn_bias"].reshape(H, F).T], axis=1)

    def col(n):
        return twice(a[n])[:, None]

    def diag(w):
        o = np.zeros((128, 2 * w.shape[1]), np.float32)
        o[:F, :w.shape[1]] = w
        o[F:, w.shape[1]:] = w
        return o

    k, m = np.arange(128)[:, None], np.arange(128)[None, :]
    same = (k // F == m // F).astype(np.float32)
    eye = np.eye(128, dtype=np.float32)
    r = np.arange(24)[:, None]
    head = np.zeros((128, H * 128), np.float32)
    for h in range(H):
        head[:24, h * 128:(h + 1) * 128] = r % 8 == h + 4 * (m // F)
    p128 = np.concatenate([
        col("L0_gnn_bp"), col("L0_gnn_gamma"), col("L0_gnn_beta"), col("L1_gnn_g1"), col("L1_gnn_b1"),
        col("L1_gnn_bd2"), col("L1_gnn_g2"), col("L1_gnn_b2"),
        diag(a["L1_gnn_Wd1"].T), col("L1_gnn_bd1"), diag(a["L1_gnn_Wd2"].T),
        np.concatenate([twice(a["L1_gnn_W2"]), twice(a["L1_gnn_W1"])], axis=0),
        np.pad(a["L1_gnn_W3"], ((0, F), (F, 0))),
        eye, eye - same / F, same / F, (k // F == np.arange(2)[None, :]).astype(np.float32) / F,
        (k == m + F).astype(np.float32), (k == m).astype(np.float32) * (m >= F),
        (k == m % F).astype(np.float32), (k == F + m % F).astype(np.float32), head], axis=1)
    return {"x": a["x"], "gidx": gidx.reshape(128, -1), "drow": drow.reshape(128, -1),
            "dblk": dblk.reshape(QR, -1), "eaT": eaT, "ea3": ea3, "p64": p64.astype(np.float32),
            "p128": p128.astype(np.float32)}


def kernel(**inputs):
    import numpy as _np
    import concourse.bacc as _bacc
    from concourse import mybir as _mybir
    from concourse.bass_utils import run_bass_kernel_spmd as _run

    nc = _bacc.Bacc("TRN2", target_bir_lowering=False, num_devices=1)
    arrays, args = {}, []
    for name, a in _layout({n: _np.asarray(v) for n, v in inputs.items()}).items():
        a = _np.ascontiguousarray(a)
        arrays[f"in_{name}_dram"] = a
        args.append(nc.dram_tensor(f"in_{name}_dram", a.shape, _mybir.dt.from_np(a.dtype), kind="ExternalInput").ap())
    out = nc.dram_tensor("out_0_dram", (N, F), _mybir.dt.float32, kind="ExternalOutput").ap()
    gnn(nc, *args, out)
    r = _run(nc, [arrays], core_ids=[0])
    return r.results[0]["out_0_dram"]
```

```python
import concourse.bass as bass
from concourse import mybir
from contextlib import ExitStack

N, E, F, H = 100000, 25000, 64, 4
EPS = 1e-5
BIG = 1.0e30
SKIP = 8388608.0
COLS = 512
NODES = 2 * COLS
DENSE = -(-N // NODES)
UNITS = 50
TILES = 4 * UNITS
EP = UNITS * COLS
QR = TILES // 2
PAIRS = UNITS // 2
CH = 12
ALU = mybir.AluOpType
ACT = mybir.ActivationFunctionType
AX = mybir.AxisListType
fp32, bf16, i32 = mybir.dt.float32, mybir.dt.bfloat16, mybir.dt.int32

P64 = {}
_at = 0
for _n, _w in (("WT", H * 128), ("Wp", H * 128), ("WeT", H * 16), ("aS", H), ("aD", H), ("aE", H), ("bias", H)):
    P64[_n] = (_at, _at + _w)
    _at += _w
W64 = _at
P128 = {}
_at = 0
for _n, _w in (("bp", 1), ("gamma", 1), ("beta", 1), ("g1", 1), ("b1", 1), ("bd2", 1), ("g2", 1), ("b2", 1),
               ("Wd1T", 7), ("Wd2T", 128), ("Wqq", 128), ("Wv", 128), ("ident", 128), ("C", 128),
               ("J", 128), ("ind", 2), ("dA", 128), ("dB", 128), ("head", H * 128)):
    P128[_n] = (_at, _at + _w)
    _at += _w
W128 = _at


class Unit:

    def __init__(self, i, off):
        self.i, self.off = i, off

    def back(self, n):
        return Unit(self.i, self.off - n)

    def count(self, n=1):
        return self.i * 4 + (self.off + n)

    def halves(self, n=0):
        return self.i * 2 + (self.off // 2 + n)

    def quarters(self, n=0):
        return self.i + (self.off // 4 + n)

    def edge(self, n):
        return EdgeUnit(self.i, (self.off - 1) // 2 - n)

    def static(self):
        return isinstance(self.i, int)

    def valid(self, n):
        return not self.static() or 0 <= self.count(0) < n


class EdgeUnit:

    def __init__(self, i, off):
        self.i, self.off = i, off

    def count(self, n=1):
        return self.i * 2 + (self.off + n)

    def halves(self, n=0):
        return self.i + (self.off // 2 + n)

    def next(self):
        return EdgeUnit(self.i, self.off + 1)

    def valid(self, n):
        return not isinstance(self.i, int) or 0 <= self.count(0) < n


def atleast(eng, sem, value):
    if not isinstance(value, int) or value > 0:
        eng.wait_ge(sem, value)


MAGIC = float(0x5F1FFFF9)


def root_step(nc, dve, k, v, w, ta, tb, step, before, made):
    c1, c2 = 0.703952253, 0.703952253 * 2.38924456
    if k > 1:
        dve.wait_ge(step, (ROOT_STEPS - 1) * before + (k - 1))
    if k == 1:
        nc.vector.tensor_scalar(ta.bitcast(i32), v.bitcast(i32), 1, None, ALU.arith_shift_right).then_inc(step, 1)
    if k == 2:
        nc.vector.tensor_scalar(tb.bitcast(i32), ta.bitcast(i32), -1.0, MAGIC, ALU.mult, ALU.add).then_inc(step, 1)
    if k == 3:
        nc.vector.scalar_tensor_tensor(ta, tb, -c1, tb, ALU.mult, ALU.mult).then_inc(step, 1)
    if k == 4:
        nc.vector.tensor_tensor(ta, ta, v, ALU.mult).then_inc(step, 1)
    if k == 5:
        nc.vector.scalar_tensor_tensor(tb, ta, c2, tb, ALU.add, ALU.mult).then_inc(step, 1)
    if k == 6:
        nc.vector.scalar_tensor_tensor(ta, tb, -0.5, tb, ALU.mult, ALU.mult).then_inc(step, 1)
    if k == 7:
        nc.vector.tensor_tensor(ta, ta, v, ALU.mult).then_inc(step, 1)
    if k == 8:
        nc.vector.scalar_tensor_tensor(w, ta, 1.5, tb, ALU.add, ALU.mult).then_inc(made, 1)


ROOT_STEPS = 8


def inverse_roots(nc, dve, v, w, ta, tb, step, before, made):
    for k in range(1, ROOT_STEPS + 1):
        root_step(nc, dve, k, v, w, ta, tb, step, before, made)


def slots(eng, total, skew, body, ahead=0):
    loops = (total - ahead) // 4
    for k in range(8):
        body(Unit(0, k))
    with eng.Fori(2, loops) as i:
        for k in range(4):
            body(Unit(i, k))
    for k in range(4 * loops, total + skew):
        body(Unit(0, k))


def gnn(nc, x, gidx, drow, dblk, eaT, ea3, p64, p128, out):
    x1 = nc.dram_tensor("x1_table", [N, F], fp32, kind="Internal").ap()
    logit_rows = nc.dram_tensor("logit_rows", [CH, EP], fp32, kind="Internal").ap()

    weight_rows = nc.dram_tensor("weight_rows", [24, EP], bf16, kind="Internal").ap()
    mask_rows = nc.dram_tensor("mask_rows", [2, EP], bf16, kind="Internal").ap()

    with ExitStack() as ctx:
        def sb(name, shape, dt=fp32):
            return ctx.enter_context(nc.sbuf_tensor(name, shape, dt))

        def sem(name):
            return ctx.enter_context(nc.semaphore(name))

        def places(ph, phase):
            def buffer(name, shape, dt=fp32):
                return ph.enter_context(nc.sbuf_tensor(f"{phase}_{name}", shape, dt))

            def semaphore(name):
                return ph.enter_context(nc.semaphore(f"{phase}_{name}"))

            return buffer, semaphore

        bank = [ctx.enter_context(nc.psum_tensor(f"bank{i}", [128, COLS], fp32)) for i in range(8)]
        prm64 = sb("prm64", [64, W64])
        prm = sb("prm", [128, W128])
        gix = sb("gix", [128, UNITS * 8], i32)
        XT = sb("XT", [128, EP])

        def c64(n):
            return prm64[:, P64[n][0]:P64[n][1]]

        def c128(n):
            return prm[:, P128[n][0]:P128[n][1]]

        ident, Cm, Jm = c128("ident"), c128("C"), c128("J")
        Mstack = sb("Mstack", [128, H, F])
        Mblk = sb("Mblk", [128, 128])
        Wal = sb("Wal", [128, CH])
        WalE = sb("WalE", [16, CH])
        c0 = sb("c0", [128, 1])
        c0x = sb("c0x", [128, 1])
        ncbeta = sb("ncbeta", [128, 1])
        CG = sb("CG", [128, 128])
        Wd1 = sb("Wd1", [7, 128])
        b2row = sb("b2row", [1, 128])
        ones = sb("ones", [1, 128])
        Wd2 = sb("Wd2", [128, 128])
        headsel = sb("headsel", [24, H, 128], bf16)

        s_prm, s_pe0, s_ev0, s_pe1, s_z0, s_gix = (sem(n) for n in (
            "params_loaded", "products_made", "products_copied", "beta_projected", "zeroed", "indices_loaded"))
        with nc.Block() as block:
            @block.sync
            def _(sp):
                sp.dma_start(prm64[:, :], p64).then_inc(s_prm, 16)
                sp.dma_start(prm[:, :], p128).then_inc(s_prm, 16)
                sp.dma_start(gix[:, :], gidx).then_inc(s_gix, 16)
                sp.wait_ge(s_gix, 16)

            @block.tensor
            def _(pe):
                pe.wait_ge(s_prm, 32)
                WT, Wp, WeT = (c64(n).rearrange("c (h k) -> c h k", h=H) for n in ("WT", "Wp", "WeT"))
                for h in range(H):
                    nc.tensor.matmul(bank[0][:, h * F:(h + 1) * F], WT[:, h, :], Wp[:, h, 0:F],
                                     start=True, stop=True)
                    nc.tensor.matmul(bank[1][:, 0:F], WT[:, h, :], Wp[:, h, 0:F], start=(h == 0), stop=(h == H - 1))
                for h in range(H):
                    nc.tensor.matmul(bank[2][:, h:h + 1], WT[:, h, :], c64("aS")[:, h:h + 1], start=True, stop=True)
                    nc.tensor.matmul(bank[2][:, 4 + h:5 + h], WT[:, h, :], c64("aD")[:, h:h + 1], start=True, stop=True)
                    nc.tensor.matmul(bank[3][0:16, h:h + 1], WeT[:, h, :], c64("aE")[:, h:h + 1], start=True, stop=True)
                for h in range(H):
                    nc.tensor.matmul(bank[4][:, 0:1], Wp[:, h, :], c64("bias")[:, h:h + 1],
                                     start=(h == 0), stop=(h == H - 1))
                nc.tensor.matmul(bank[5][:, 0:1], Cm, c128("beta"), start=True, stop=True)
                nc.tensor.matmul(bank[0][0:1, 256:384], c128("bd2"), Cm, start=True, stop=True)
                nc.tensor.matmul(bank[6][0:7, 0:128], c128("Wd1T"), Cm, start=True, stop=True)
                nc.tensor.matmul(bank[7][:, 0:128], c128("Wd2T"), Cm, start=True, stop=True).then_inc(s_pe0, 1)
                pe.wait_ge(s_ev0, 2)
                nc.tensor.matmul(bank[5][:, 3:4], Mblk[:, :], c128("beta"), start=True, stop=True).then_inc(s_pe1, 1)

            @block.vector
            def _(dve):
                nc.vector.memset(Mblk[:, :], 0.0)
                nc.vector.memset(Wal[:, :], 0.0)
                nc.vector.memset(WalE[:, :], 0.0).then_inc(s_z0, 1)
                dve.wait_ge(s_z0, 1)
                dve.wait_ge(s_prm, 32)
                nc.vector.tensor_copy(headsel[:, :, :], c128("head")[0:24, :].rearrange("r (h m) -> r h m", h=H))
                dve.wait_ge(s_pe0, 1)
                nc.vector.tensor_copy(Mstack[:, :, :], bank[0][:, 0:H * F].rearrange("p (h f) -> p h f", h=H))
                nc.vector.tensor_copy(Mblk[0:64, 0:64], bank[1][0:64, 0:F])
                nc.vector.tensor_copy(Mblk[64:128, 64:128], bank[1][64:128, 0:F])
                nc.vector.tensor_copy(Wal[0:64, 0:4], bank[2][0:64, 0:4])
                nc.vector.tensor_copy(Wal[64:128, 0:4], bank[2][64:128, 4:8])
                nc.vector.tensor_copy(Wal[64:128, 8:12], bank[2][64:128, 0:4]).then_inc(s_ev0, 1)
                dve.wait_ge(s_ev0, 1)
                nc.vector.tensor_tensor(Wal[64:128, 8:12], Wal[64:128, 8:12], bank[2][64:128, 4:8], ALU.add)
                nc.vector.tensor_copy(WalE[:, 0:4], bank[3][0:16, 0:4])
                nc.vector.tensor_copy(WalE[:, 4:8], bank[3][0:16, 0:4])
                nc.vector.tensor_tensor(c0[:, :], bank[4][:, 0:1], c128("bp"), ALU.add)
                nc.vector.tensor_scalar(ncbeta[:, :], bank[5][:, 0:1], -1.0, None, ALU.mult)
                nc.vector.tensor_scalar(CG[:, :], Cm, c128("gamma"), None, ALU.mult)
                nc.vector.memset(ones[:, :], 1.0)
                nc.vector.tensor_copy(b2row[:, :], bank[0][0:1, 256:384])
                nc.vector.tensor_copy(Wd1[:, :], bank[6][0:7, 0:128])
                nc.vector.tensor_copy(Wd2[:, :], bank[7][:, 0:128])
                nc.vector.tensor_scalar(c128("Wqq")[0:64, :], c128("Wqq")[0:64, :], -1.0, None, ALU.mult).then_inc(s_ev0, 1)
                dve.wait_ge(s_ev0, 2)
                dve.wait_ge(s_pe1, 1)
                nc.vector.tensor_tensor(c0x[:, :], c0[:, :], bank[5][:, 3:4], ALU.subtract)

        with ExitStack() as ph:
            sbp, semp = places(ph, "dense")

            rows = [sbp(f"rows{i}", [128, 8 * F]) for i in range(4)]
            xT = [sbp(f"xT{i}", [128, COLS]) for i in range(4)]
            ex = [sbp(f"ex{i}", [128, COLS]) for i in range(2)]
            rl = [sbp(f"rl{i}", [128, COLS]) for i in range(2)]
            gb = sbp("gb", [128, COLS])
            hb = [sbp(f"hb{i}", [128, COLS]) for i in range(2)]
            sq = [sbp(f"sq{i}", [128, COLS]) for i in range(2)]
            hc = [sbp(f"hc{i}", [128, COLS]) for i in range(2)]
            yb = sbp("yb", [128, 8, F])
            yc = [sbp(f"yc{i}", [128, 8, F]) for i in range(4)]
            q2 = [sbp(f"q2{i}", [128, 8, F]) for i in range(2)]
            s2 = sbp("s2", [128, 8])
            v, w, ta, tb = (sbp(n, [128, 24]) for n in ("v", "w", "ta", "tb"))
            xr = [sbp(f"xr{i}", [128, 8, F]) for i in range(2)]
            orow = [sbp(f"orow{i}", [128, 8, F]) for i in range(2)]
            stage = [sbp(f"stage{i}", [128, 8], i32) for i in range(2)]
            pairs = [sbp(f"pairs{i}", [128, 4, 2 * F]) for i in range(2)]
            eab = [sbp(f"eab{i}", [16, COLS]) for i in range(2)]
            lrow = [sbp(f"lrow{i}", [CH, COLS]) for i in range(2)]
            pT, pH, pR, pA = bank[0], bank[1], bank[2], bank[3]
            pG, pX, pP = [bank[4], bank[5]], bank[6], bank[7]

            x_loaded = [semp(f"x_loaded{i}") for i in range(4)]
            stored = [semp(f"stored{i}") for i in range(2)]
            (xt_made, x_copied, p_made, e_made, g_made, h_made, hc_made, sq_made, var_made, g_rows_made, v1_made,
             scaled, y_made, y_squared, y_summed, v2_made, out_made) = (semp(n) for n in (
                 "xt_made", "x_copied", "p_made", "e_made", "g_made", "h_made", "hc_made", "sq_made", "var_made",
                 "g_rows_made", "v1_made", "scaled", "y_made", "y_squared", "y_summed", "v2_made", "out_made"))
            v_cleared, root_steps, roots_made = semp("v_cleared"), semp("root_steps"), semp("roots_made")
            gathered = [semp(f"gathered{i}") for i in range(2)]
            ea_loaded = [semp(f"ea_loaded{i}") for i in range(2)]
            l_stored = [semp(f"l_stored{i}") for i in range(2)]
            sources_staged, targets_staged, pair_turned, pair_copied, l_made, l_copied = (semp(n) for n in (
                "sources_staged", "targets_staged", "pair_turned", "pair_copied", "l_made", "l_copied"))

            def node_rows(table, u):
                if u.static():
                    n0 = min(u.count(0) * NODES, N - NODES)
                    t = table[n0:n0 + NODES, :]
                else:
                    t = table[bass.ds(u.count(0) * NODES, NODES), :]
                return t.rearrange("(p r) f -> p (r f)", p=128)

            block = ph.enter_context(nc.Block())

            @block.sync
            def _(sp):
                def load(u):
                    atleast(sp, xt_made, u.count(-3))
                    sp.dma_start(rows[u.off % 4][:, :], node_rows(x, u)).then_inc(x_loaded[u.off % 4], 16)

                def store(u):
                    b = u.off % 2
                    sp.wait_ge(out_made, u.count(1))
                    if u.static() and u.count(0) == DENSE - 1:
                        sp.wait_ge(stored[1 - b], 32 * ((DENSE - 2) // 2 + 1))
                    sp.dma_start(node_rows(x1, u), xr[b][:, :, :].rearrange("p r f -> p (r f)")).then_inc(stored[b], 16)
                    sp.dma_start(node_rows(out, u), orow[b][:, :, :].rearrange("p r f -> p (r f)")).then_inc(stored[b], 16)

                def load_attributes(e):
                    atleast(sp, l_made, e.count(-1))
                    sp.dma_start(eab[e.off % 2][:, :], eaT[:, bass.ds(e.count(0) * COLS, COLS)])\
                        .then_inc(ea_loaded[e.off % 2], 16)

                def store_logits(e):
                    sp.wait_ge(l_copied, e.count(1))
                    sp.dma_start(logit_rows[:, bass.ds(e.count(0) * COLS, COLS)], lrow[e.off % 2][:, :])\
                        .then_inc(l_stored[e.off % 2], 16)

                def slot(u):
                    if u.static() and u.count(0) == 0:
                        for ahead in range(3):
                            load(Unit(0, ahead))
                    if u.back(-3).valid(DENSE):
                        load(u.back(-3))
                    if u.off % 2 == 1:
                        if u.edge(0).valid(UNITS):
                            load_attributes(u.edge(0))
                        if u.edge(2).valid(UNITS):
                            store_logits(u.edge(2))
                    if u.back(5).valid(DENSE):
                        store(u.back(5))

                slots(sp, DENSE, 6, slot, ahead=4)
                for b in range(2):
                    sp.wait_ge(stored[b], 32 * (DENSE // 2))
                    sp.wait_ge(l_stored[b], 16 * (UNITS // 2))

            @block.gpsimd
            def _(pool):
                def stage_sources(e):
                    if e.valid(UNITS):
                        atleast(pool, gathered[e.off % 2], e.halves(0) * 128)
                        nc.gpsimd.tensor_copy(stage[e.off % 2][:, 0:4], gix[:, bass.ds(e.count(0) * 8, 4)])\
                            .then_inc(sources_staged, 1)

                def stage_targets(e):
                    nc.gpsimd.tensor_copy(stage[e.off % 2][:, 4:8], gix[:, bass.ds(e.count(0) * 8 + 4, 4)])\
                        .then_inc(targets_staged, 1)

                def gather(e, js):
                    a = e.off % 2
                    for j in js:
                        pool.indirect_dma_start(
                            out=pairs[a][:, j % 4, F * (j // 4):F * (j // 4) + F], out_offset=None, in_=x,
                            in_offset=bass.IndirectOffsetOnAxis(ap=stage[a][:, j:j + 1], axis=0))\
                            .then_inc(gathered[a], 16)

                def edge_unit(e):
                    atleast(pool, pair_turned, e.count(-1))
                    pool.wait_ge(sources_staged, e.count(1))
                    stage_targets(e)
                    gather(e, range(4))
                    pool.wait_ge(targets_staged, e.count(1))
                    stage_sources(e.next())
                    gather(e, range(4, 8))

                def slot(u):
                    if u.static() and u.count(0) == 0:
                        stage_sources(EdgeUnit(0, 0))
                    if u.off % 2 == 1 and u.edge(0).valid(UNITS):
                        edge_unit(u.edge(0))

                slots(pool, DENSE, 6, slot)

            @block.tensor
            def _(pe):
                def turn_rows(u):
                    pe.wait_ge(x_loaded[u.off % 4], u.quarters(1) * 16)
                    atleast(pe, x_copied, u.count(0))
                    for j in range(4):
                        last = nc.tensor.transpose(pT[:, j * 128:(j + 1) * 128],
                                                   rows[u.off % 4][:, j * 128:(j + 1) * 128], ident)
                    last.then_inc(xt_made, 1)

                def project(u):
                    pe.wait_ge(x_copied, u.count(1))
                    atleast(pe, e_made, u.count(0))
                    nc.tensor.matmul(pP[:, :], Mblk[:, :], xT[u.off % 4][:, :], start=True, stop=True).then_inc(p_made, 1)

                def centre(u):
                    pe.wait_ge(h_made, u.count(1))
                    atleast(pe, sq_made, u.count(0))
                    nc.tensor.matmul(pH[:, :], Cm, hb[u.off % 2][:, :], start=True, stop=True).then_inc(hc_made, 1)

                def variance(u):
                    b = u.off % 2
                    pe.wait_ge(sq_made, u.count(1))
                    atleast(pe, v1_made, u.count(0))
                    for j in range(4):
                        last = nc.tensor.matmul(pR[:, 2 * j:2 * j + 2], sq[b][:, j * 128:(j + 1) * 128], c128("ind"),
                                                start=True, stop=True)
                    last.then_inc(var_made, 1)

                def to_rows(u):
                    b = u.off % 2
                    atleast(pe, scaled, u.count(-1))
                    for j in range(4):
                        c = slice(j * 128, (j + 1) * 128)
                        nc.tensor.matmul(pG[b][:, c], hc[b][:, c], CG[:, :], start=True, stop=True)

                def x_to_rows(u):
                    atleast(pe, y_made, u.count(0))
                    for j in range(4):
                        c = slice(j * 128, (j + 1) * 128)
                        last = nc.tensor.matmul(pX[:, c], xT[u.off % 4][:, c], Cm, start=True, stop=True)
                    last.then_inc(g_rows_made, 1)

                def turn_pairs(e):
                    a = e.off % 2
                    pe.wait_ge(gathered[a], e.halves(1) * 128)
                    atleast(pe, l_copied, e.count(0))
                    for j in range(4):
                        last = nc.tensor.transpose(pA[:, j * 128:(j + 1) * 128], pairs[a][:, j, :], ident)
                    last.then_inc(pair_turned, 1)

                def logits(e):
                    a = e.off % 2
                    pe.wait_ge(pair_copied, e.count(1))
                    pe.wait_ge(ea_loaded[a], e.halves(1) * 16)
                    nc.tensor.matmul(pA[0:CH, :], Wal[:, :], XT[:, bass.ds(e.count(0) * COLS, COLS)],
                                     start=True, stop=False)
                    nc.tensor.matmul(pA[0:CH, :], WalE[:, :], eab[a][:, :], start=False, stop=True).then_inc(l_made, 1)

                def slot(u):
                    if u.valid(DENSE):
                        turn_rows(u)
                    if u.back(2).valid(DENSE):
                        variance(u.back(2))
                        to_rows(u.back(2))
                    if u.valid(DENSE):
                        project(u)
                    if u.back(1).valid(DENSE):
                        centre(u.back(1))
                    if u.back(2).valid(DENSE):
                        x_to_rows(u.back(2))
                    if u.off % 2 == 1 and u.edge(1).valid(UNITS):
                        turn_pairs(u.edge(1))
                    if u.off % 2 == 0 and u.edge(1).valid(UNITS):
                        logits(u.edge(1))

                slots(pe, DENSE, 6, slot)

            @block.scalar
            def _(act):
                def copy_x(u):
                    act.wait_ge(xt_made, u.count(1))
                    atleast(act, g_rows_made, u.count(-3))
                    nc.scalar.activation(xT[u.off % 4][:, :], pT[:, :], ACT.Identity, bias=c128("beta")).then_inc(x_copied, 1)

                def elu_parts(u):
                    b = u.off % 2
                    act.wait_ge(p_made, u.count(1))
                    atleast(act, g_made, u.count(-1))
                    nc.scalar.activation(ex[b][:, :], pP[:, :], ACT.Exp, bias=c0x[:, :])
                    nc.scalar.activation(rl[b][:, :], pP[:, :], ACT.Relu, bias=c0x[:, :]).then_inc(e_made, 1)

                def square(u):
                    b = u.off % 2
                    act.wait_ge(hc_made, u.count(1))
                    atleast(act, g_rows_made, u.count(-1))
                    nc.scalar.activation(sq[b][:, :], pH[:, :], ACT.Square, bias=ncbeta[:, :])
                    nc.scalar.activation(hc[b][:, :], pH[:, :], ACT.Identity, bias=ncbeta[:, :]).then_inc(sq_made, 1)

                def square_y(u):
                    b = u.off % 2
                    act.wait_ge(y_made, u.count(1))
                    atleast(act, y_summed, u.count(-1))
                    nc.scalar.activation(q2[b][:, :, :], yc[u.off % 4][:, :, :], ACT.Square, scale=F ** -0.5).then_inc(y_squared, 1)

                def copy_pairs(e):
                    act.wait_ge(pair_turned, e.count(1))
                    nc.scalar.activation(XT[:, bass.ds(e.count(0) * COLS, COLS)], pA[:, :], ACT.Copy).then_inc(pair_copied, 1)

                def copy_logits(e):
                    a = e.off % 2
                    act.wait_ge(l_made, e.count(1))
                    atleast(act, l_stored[a], e.halves(0) * 16)
                    nc.scalar.activation(lrow[a][:, :], pA[0:CH, :], ACT.Copy).then_inc(l_copied, 1)

                def slot(u):
                    if u.valid(DENSE):
                        copy_x(u)
                    if u.back(3).valid(DENSE):
                        square_y(u.back(3))
                    if u.valid(DENSE):
                        elu_parts(u)
                    if u.back(1).valid(DENSE):
                        square(u.back(1))
                    if u.off % 2 == 1 and u.edge(1).valid(UNITS):
                        copy_pairs(u.edge(1))
                    if u.off % 2 == 0 and u.edge(1).valid(UNITS):
                        copy_logits(u.edge(1))

                slots(act, DENSE, 6, slot)

            @block.vector
            def _(dve):
                def elu(u):
                    b = u.off % 2
                    dve.wait_ge(e_made, u.count(1))
                    atleast(dve, h_made, u.count(0))
                    nc.vector.scalar_tensor_tensor(gb[:, :], ex[b][:, :], 1.0, rl[b][:, :], ALU.min, ALU.add).then_inc(g_made, 1)

                def residual(u):
                    b = u.off % 2
                    atleast(dve, hc_made, u.count(-1))
                    dve.wait_ge(g_made, u.count(1))
                    nc.vector.tensor_tensor(hb[b][:, :], gb[:, :], xT[u.off % 4][:, :], ALU.add).then_inc(h_made, 1)

                def add_eps(u):
                    dve.wait_ge(var_made, u.count(1))
                    atleast(dve, roots_made, u.count(0))
                    nc.vector.tensor_scalar(v[:, 0:8], pR[:, 0:8], EPS, None, ALU.add).then_inc(v1_made, 1)

                def root(u, k):
                    if k == 1:
                        if u.valid(DENSE):
                            dve.wait_ge(v1_made, u.count(1))
                        atleast(dve, v2_made, u.count(-1))
                    if k == ROOT_STEPS:
                        atleast(dve, out_made, u.count(-2) if u.valid(DENSE) else min(u.count(-2), DENSE))
                        atleast(dve, scaled, u.count(0) if u.valid(DENSE) else DENSE)
                    root_step(nc, dve, k, v[:, :], w[:, :], ta[:, :], tb[:, :], root_steps, u.count(0), roots_made)

                def scale(u):
                    b = u.off % 2
                    dve.wait_ge(roots_made, u.count(1))
                    dve.wait_ge(g_rows_made, u.count(1))
                    atleast(dve, y_made, u.count(0))
                    nc.vector.tensor_tensor(yb[:, :, :], pG[b][:, :].rearrange("p (r f) -> p r f", f=F),
                                            w[:, 0:8].unsqueeze(2).to_broadcast([128, 8, F]), ALU.mult).then_inc(scaled, 1)

                def add_scaled(u):
                    dve.wait_ge(scaled, u.count(1))
                    atleast(dve, out_made, u.count(-3))
                    nc.vector.tensor_tensor(yc[u.off % 4][:, :, :], yb[:, :, :], pX[:, :].rearrange("p (r f) -> p r f", f=F),
                                            ALU.add).then_inc(y_made, 1)

                def sum_squares(u):
                    b = u.off % 2
                    dve.wait_ge(y_squared, u.count(1))
                    atleast(dve, v2_made, u.count(0))
                    nc.vector.tensor_reduce(s2[:, :], q2[b][:, :, :], AX.X, ALU.add).then_inc(y_summed, 1)

                def keep_sums(u):
                    dve.wait_ge(y_summed, u.count(1))
                    dve.wait_ge(roots_made, u.count(2))
                    nc.vector.tensor_scalar(v[:, 8:16], s2[:, :], EPS, None, ALU.add)
                    nc.vector.tensor_scalar(v[:, 16:24], s2[:, :], 1.0 + EPS, EPS * EPS, ALU.mult, ALU.add)\
                        .then_inc(v2_made, 1)

                def finish_x1(u):
                    b = u.off % 2
                    dve.wait_ge(roots_made, u.count(3))
                    atleast(dve, stored[b], u.halves(0) * 32)
                    nc.vector.tensor_tensor(xr[b][:, :, :], yc[u.off % 4][:, :, :],
                                            w[:, 8:16].unsqueeze(2).to_broadcast([128, 8, F]), ALU.mult)

                def finish_out(u):
                    nc.vector.tensor_tensor(orow[u.off % 2][:, :, :], yc[u.off % 4][:, :, :],
                                            w[:, 16:24].unsqueeze(2).to_broadcast([128, 8, F]), ALU.mult)\
                        .then_inc(out_made, 1)

                def slot(u):
                    if u.static() and u.count(0) == 0:
                        nc.vector.memset(v[:, :], 1.0).then_inc(v_cleared, 1)
                        dve.wait_ge(v_cleared, 1)
                    has_roots = u.back(2).valid(DENSE + 2)
                    if u.back(1).valid(DENSE):
                        elu(u.back(1))
                    if u.back(2).valid(DENSE):
                        add_eps(u.back(2))
                    if has_roots:
                        root(u.back(2), 1)
                    if u.back(1).valid(DENSE):
                        residual(u.back(1))
                    if has_roots:
                        root(u.back(2), 2)
                    if u.back(5).valid(DENSE):
                        finish_x1(u.back(5))
                    if has_roots:
                        root(u.back(2), 3)
                    if u.back(5).valid(DENSE):
                        finish_out(u.back(5))
                    if has_roots:
                        root(u.back(2), 4)
                    if u.back(3).valid(DENSE):
                        sum_squares(u.back(3))
                    if has_roots:
                        for k in range(5, ROOT_STEPS + 1):
                            root(u.back(2), k)
                    if u.back(2).valid(DENSE):
                        scale(u.back(2))
                    if u.back(3).valid(DENSE):
                        keep_sums(u.back(3))
                    if u.back(2).valid(DENSE):
                        add_scaled(u.back(2))

                slots(dve, DENSE, 6, slot)

        scatter_rows = sb("scatter_rows", [128, TILES], i32)
        with ExitStack() as ph:
            sbp, semp = places(ph, "weigh")

            ids = sbp("ids", [QR, 3, 2, 128], i32)
            idf = sbp("idf", [QR, 3, 2, 128])
            rid = sbp("rid", [128, 2, TILES], i32)
            rif = sbp("rif", [128, 2, TILES])
            lg = sbp("lg", [QR, 2, CH, 128])
            goes_on = sbp("goes_on", [QR, 2, 128])
            lasts = sbp("lasts", [QR, 2, 128])
            stays = sbp("stays", [QR, 2, 128])
            drop = sbp("drop", [QR, 2, 128])
            narrow = sbp("narrow", [QR, 2, 2, 128], bf16)
            val = sbp("val", [QR, 2, 9, 128])
            pre = sbp("pre", [QR, 2, 9, 128])
            tot = sbp("tot", [QR, 2, 9, 128])
            loop = sbp("loop", [QR, 2, 4, 128])
            tmp = sbp("tmp", [QR, 2, 4, 128])
            peak = sbp("peak", [QR, 2, 4, 128])
            weight, rest = tot[:, :, 0:8, :], pre[:, :, 0:8, :]
            part = sbp("part", [QR, 3, 2, 8, 128], bf16)
            keep = sbp("keep", [QR, 4, 2])
            ends = sbp("ends", [QR, 2, 2, 9])
            rowT = sbp("rowT", [9, 2, 2, 2 * QR])
            chain = sbp("chain", [9, 2, 2 * QR + 1])
            carry = sbp("carry", [QR, 2, 9])

            loaded, ends_made, turned, chained, back, stepped, weights_done, exps_asked, exps_made, saved = (
                semp(n) for n in ("loaded", "ends_made", "turned", "chained", "back", "stepped", "weights_done",
                                  "exps_asked", "exps_made", "saved"))
            ROUNDS = [(0, 9, True, 4), (0, 9, False, 0), (0, 4, True, 0), (0, 4, False, 0)]
            block = ph.enter_context(nc.Block())

            @block.sync
            def _(sp):
                sp.dma_start(ids[:, :, :, :].rearrange("q a h j -> q (a h j)"), dblk).then_inc(loaded, 16)
                sp.dma_start(rid[:, :, :].rearrange("p a t -> p (a t)"), drow).then_inc(loaded, 16)
                for h in range(2):
                    sp.dma_start(lg[:, h, :, :],
                                 logit_rows[:, h * QR * 128:(h + 1) * QR * 128].rearrange("c (q j) -> q c j", j=128))\
                        .then_inc(loaded, 16)
                sp.wait_ge(weights_done, 1)
                for h in range(2):
                    span = slice(h * QR * 128, (h + 1) * QR * 128)
                    for a in range(3):
                        sp.dma_start(weight_rows[8 * a:8 * a + 8, span].rearrange("c (q j) -> q c j", j=128),
                                     part[:, a, h, :, :]).then_inc(saved, 16)
                    for a in range(2):
                        sp.dma_start(mask_rows[a, span].rearrange("(q j) -> q j", j=128), narrow[:, a, h, :])\
                            .then_inc(saved, 16)
                sp.wait_ge(saved, 16 * 10)

            @block.tensor
            def _(pe):
                for n, (c0_, c1_, forward, maxima) in enumerate(ROUNDS):
                    groups = [(c0_, maxima), (maxima, c1_)] if maxima else [(c0_, c1_)]
                    pe.wait_ge(ends_made, n + 1)
                    for g, (a, b) in enumerate(groups):
                        for k in range(2):
                            for h in range(2):
                                last = nc.tensor.transpose(bank[2 * g + k][0:b - a, h * QR:(h + 1) * QR],
                                                           ends[:, k, h, a:b], ident[0:QR, 0:QR])
                    last.then_inc(turned, 1)
                    pe.wait_ge(chained, n + 1)
                    for g, (a, b) in enumerate(groups):
                        for h in range(2):
                            first = h * QR + (0 if forward else 1)
                            last = nc.tensor.transpose(bank[4 + h][0:QR, a:b], chain[0:b - a, g, first:first + QR],
                                                       ident[0:b - a, 0:b - a])
                    last.then_inc(back, 1)

            @block.scalar
            def _(act):
                act.wait_ge(exps_asked, 1)
                nc.scalar.activation(val[:, :, 0:4, :], peak[:, :, :, :], ACT.Exp)
                nc.scalar.activation(loop[:, :, :, :], tmp[:, :, :, :], ACT.Exp).then_inc(exps_made, 1)

            @block.vector
            def _(dve):
                count = [0]

                def step(ins):
                    count[0] += 1
                    ins.then_inc(stepped, 1)
                    dve.wait_ge(stepped, count[0])

                def spread(t, n):
                    return t.unsqueeze(2).to_broadcast([QR, 2, n, 128])

                def scans(n, out_, from_, initial):
                    c0_, c1_, forward, maxima = ROUNDS[n]
                    for h in range(2):
                        for c in range(c0_, c1_):
                            o, f = out_[:, h, c, :], from_[:, h, c, :]
                            if forward and c < maxima:
                                last = nc.vector.tensor_tensor_scan(o, drop[:, h, :], f, initial(h, c), ALU.add, ALU.max)
                            elif forward:
                                last = nc.vector.tensor_tensor_scan(o, goes_on[:, h, :], f, initial(h, c), ALU.mult, ALU.add)
                            else:
                                last = nc.vector.tensor_tensor_scan(o[:, ::-1], stays[:, h, ::-1], f[:, ::-1],
                                                                    initial(h, c), ALU.mult, ALU.add)
                    return last

                def segment_scan(n, out_, from_):
                    c0_, c1_, forward, maxima = ROUNDS[n]
                    step(scans(n, out_, from_, lambda h, c: -BIG if forward and c < maxima else 0.0))
                    edge = 127 if forward else 0
                    nc.vector.tensor_copy(ends[:, 0, :, c0_:c1_], out_[:, :, c0_:c1_, edge])
                    if maxima:
                        nc.vector.tensor_copy(ends[:, 1, :, 0:maxima], keep[:, 2, :].unsqueeze(2).to_broadcast([QR, 2, maxima]))
                    nc.vector.tensor_copy(ends[:, 1, :, maxima:c1_],
                                          keep[:, 0 if forward else 1, :].unsqueeze(2).to_broadcast([QR, 2, c1_ - maxima]))\
                        .then_inc(ends_made, 1)
                    groups = [(c0_, maxima), (maxima, c1_)] if maxima else [(c0_, c1_)]
                    dve.wait_ge(turned, n + 1)
                    for g, (a, b) in enumerate(groups):
                        for k in range(2):
                            last = nc.vector.tensor_copy(rowT[0:b - a, g, k, :], bank[2 * g + k][0:b - a, 0:2 * QR])
                        start = -BIG if maxima and g == 0 else 0.0
                        first = 0 if forward else 2 * QR
                        last = nc.vector.memset(chain[0:b - a, g, first:first + 1], start)
                    step(last)
                    for g, (a, b) in enumerate(groups):
                        m = b - a
                        start = -BIG if maxima and g == 0 else 0.0
                        if forward:
                            ops = (ALU.add, ALU.max) if maxima and g == 0 else (ALU.mult, ALU.add)
                            last = nc.vector.tensor_tensor_scan(chain[0:m, g, 1:], rowT[0:m, g, 1, :], rowT[0:m, g, 0, :],
                                                                start, *ops)
                        else:
                            o = chain[0:m, g, 0:2 * QR]
                            last = nc.vector.tensor_tensor_scan(o[:, ::-1], rowT[0:m, g, 1, ::-1], rowT[0:m, g, 0, ::-1],
                                                                start, ALU.mult, ALU.add)
                    last.then_inc(chained, 1)
                    dve.wait_ge(back, n + 1)
                    for h in range(2):
                        last = nc.vector.tensor_copy(carry[:, h, c0_:c1_], bank[4 + h][0:QR, c0_:c1_])
                    step(last)
                    step(scans(n, out_, from_, lambda h, c: carry[:, h, c:c + 1]))

                dve.wait_ge(loaded, 64)
                nc.vector.tensor_copy(rif[:, :, :], rid[:, :, :])
                step(nc.vector.tensor_copy(idf[:, :, :, :], ids[:, :, :, :]))
                nc.vector.tensor_tensor(goes_on[:, :, :], idf[:, 0, :, :], idf[:, 1, :, :], ALU.is_equal)
                nc.vector.tensor_tensor(lasts[:, :, :], idf[:, 1, :, :], idf[:, 2, :, :], ALU.not_equal)
                nc.vector.tensor_tensor(stays[:, :, :], idf[:, 1, :, :], idf[:, 2, :, :], ALU.is_equal)
                step(nc.vector.tensor_tensor(rif[:, 1, :], rif[:, 0, :], rif[:, 1, :], ALU.is_equal))
                nc.vector.tensor_scalar(drop[:, :, :], goes_on[:, :, :], 1.0, BIG, ALU.subtract, ALU.mult)
                nc.vector.tensor_copy(narrow[:, 0, :, :], goes_on[:, :, :])
                nc.vector.tensor_reduce(keep[:, 0, :], goes_on[:, :, :], AX.X, ALU.min)
                nc.vector.tensor_reduce(keep[:, 1, :], stays[:, :, :], AX.X, ALU.min)
                step(nc.vector.scalar_tensor_tensor(rif[:, 0, :], rif[:, 1, :], SKIP, rif[:, 0, :], ALU.mult, ALU.max))
                nc.vector.tensor_copy(scatter_rows[:, :], rif[:, 0, :])
                nc.vector.tensor_copy(narrow[:, 1, :, :], drop[:, :, :])
                nc.vector.tensor_scalar(keep[:, 2, :], keep[:, 0, :], 1.0, BIG, ALU.subtract, ALU.mult)
                nc.vector.scalar_tensor_tensor(val[:, :, 0:4, :], lg[:, :, 0:4, :], 0.2, lg[:, :, 0:4, :], ALU.mult, ALU.max)
                nc.vector.tensor_copy(val[:, :, 4:8, :], lg[:, :, 4:8, :])
                step(nc.vector.memset(val[:, :, 8, :], 1.0))
                segment_scan(0, pre, val)
                step(nc.vector.tensor_tensor(pre[:, :, :, :], pre[:, :, :, :], spread(lasts[:, :, :], 9), ALU.mult))
                segment_scan(1, tot, pre)
                step(nc.vector.reciprocal(tot[:, :, 8, :], tot[:, :, 8, :]))
                step(nc.vector.tensor_tensor(loop[:, :, :, :], tot[:, :, 4:8, :], spread(tot[:, :, 8, :], 4), ALU.mult))
                step(nc.vector.tensor_tensor(tmp[:, :, :, :], loop[:, :, :, :], lg[:, :, 8:12, :], ALU.add))
                step(nc.vector.scalar_tensor_tensor(loop[:, :, :, :], tmp[:, :, :, :], 0.2, tmp[:, :, :, :], ALU.mult, ALU.max))
                step(nc.vector.tensor_tensor(rest[:, :, 0:4, :], loop[:, :, :, :], tot[:, :, 0:4, :], ALU.max))
                nc.vector.tensor_tensor(peak[:, :, :, :], val[:, :, 0:4, :], rest[:, :, 0:4, :], ALU.subtract)
                nc.vector.tensor_tensor(tmp[:, :, :, :], loop[:, :, :, :], rest[:, :, 0:4, :], ALU.subtract)\
                    .then_inc(exps_asked, 1)
                dve.wait_ge(exps_made, 1)
                segment_scan(2, pre, val)
                step(nc.vector.tensor_tensor(pre[:, :, 0:4, :], pre[:, :, 0:4, :], spread(lasts[:, :, :], 4), ALU.mult))
                segment_scan(3, tot, pre)
                step(nc.vector.tensor_tensor(peak[:, :, :, :], tot[:, :, 0:4, :], loop[:, :, :, :], ALU.add))
                step(nc.vector.reciprocal(tmp[:, :, :, :], peak[:, :, :, :]))
                nc.vector.tensor_tensor(weight[:, :, 0:4, :], val[:, :, 0:4, :], tmp[:, :, :, :], ALU.mult)
                step(nc.vector.tensor_tensor(peak[:, :, :, :], loop[:, :, :, :], tmp[:, :, :, :], ALU.mult))
                step(nc.vector.tensor_tensor(weight[:, :, 4:8, :], peak[:, :, :, :], spread(lasts[:, :, :], 4), ALU.mult))
                step(nc.vector.tensor_copy(part[:, 0, :, :, :], weight[:, :, :, :]))
                step(nc.vector.tensor_tensor(rest[:, :, :, :], weight[:, :, :, :], part[:, 0, :, :, :], ALU.subtract))
                step(nc.vector.tensor_copy(part[:, 1, :, :, :], rest[:, :, :, :]))
                step(nc.vector.tensor_tensor(weight[:, :, :, :], rest[:, :, :, :], part[:, 1, :, :, :], ALU.subtract))
                nc.vector.tensor_copy(part[:, 2, :, :, :], weight[:, :, :, :]).then_inc(weights_done, 1)

        with ExitStack() as ph:
            sbp, semp = places(ph, "first")

            wt = [sbp(f"wt{i}", [24, 2 * COLS], bf16) for i in range(2)]
            mask = [sbp(f"mask{i}", [128, COLS], bf16) for i in range(2)]
            zb = [sbp(f"zb{i}", [128, COLS]) for i in range(2)]
            ys = [sbp(f"ys{i}", [128, COLS]) for i in range(2)]
            start = sbp("start", [128, 1])
            xd = [sbp(f"xd{i}", [128, COLS]) for i in range(4)]
            ex, rl, gb, hb, sq, hc = (sbp(n, [128, COLS]) for n in ("ex", "rl", "gb", "hb", "sq", "hc"))
            yb, q2 = sbp("yb", [128, 8, F]), sbp("q2", [128, 8, F])
            yc = [sbp(f"yc{i}", [128, 8, F]) for i in range(2)]
            xr = [sbp(f"xr{i}", [128, 8, F]) for i in range(2)]
            s2 = sbp("s2", [128, 8])
            v, w, ta, tb = (sbp(n, [128, 16]) for n in ("v", "w", "ta", "tb"))
            stage = [sbp(f"stage{i}", [128, 8], i32) for i in range(2)]
            pB, pY, pH, pR, pG = [bank[0], bank[1]], bank[2], bank[4], bank[5], bank[6]
            pC = bank[7]

            w_loaded = [semp(f"w_loaded{i}") for i in range(2)]
            scattered = [semp(f"scattered{i}") for i in range(2)]
            (spread_made, z_made, z_used, halfway, crossed, summed, xd_copied,
             e_made, g_made, h_made, hc_made, sq_made, var_made, rows_made, v1_made, roots_made, root_steps, scaled,
             yc_made, squared, s_made, v2_made, xr_made, a_staged, b_staged, cleared) = (semp(n) for n in (
                 "spread_made", "z_made", "z_used", "halfway", "crossed", "summed",
                 "xd_copied", "e_made", "g_made", "h_made", "hc_made", "sq_made", "var_made", "rows_made",
                 "v1_made", "roots_made", "root_steps", "scaled", "yc_made", "squared", "s_made", "v2_made", "xr_made",
                 "a_staged", "b_staged", "cleared"))
            block = ph.enter_context(nc.Block())

            def columns(u, s):
                return bass.ds(u.count(0) * (2 * COLS) + s * COLS, COLS)

            @block.sync
            def _(sp):
                def load(u):
                    b = u.off % 2
                    atleast(sp, summed, u.count(-1))
                    sp.dma_start(wt[b][:, :], weight_rows[:, bass.ds(u.count(0) * 2 * COLS, 2 * COLS)])\
                        .then_inc(w_loaded[b], 16)
                    for s in range(2):
                        sp.dma_start(mask[b][64 * s:64 * s + 64, :],
                                     mask_rows[0:1, columns(u, s)].to_broadcast([64, COLS])).then_inc(w_loaded[b], 16)

                def slot(u):
                    if u.static() and u.count(0) == 0:
                        load(u)
                    if u.back(-1).valid(PAIRS):
                        load(u.back(-1))

                slots(sp, PAIRS, 4, slot)

            @block.gpsimd
            def _(pool):
                def stage_part(u, s, staged):
                    if not u.valid(PAIRS):
                        return
                    atleast(pool, scattered[u.off % 2], u.halves(0) * 128)
                    nc.gpsimd.tensor_copy(stage[u.off % 2][:, 4 * s:4 * s + 4],
                                          scatter_rows[:, bass.ds(u.count(0) * 8 + 4 * s, 4)]).then_inc(staged, 1)

                def scatter(u, s):
                    b = u.off % 2
                    for j in range(4):
                        pool.indirect_dma_start(
                            out=x1, out_offset=bass.IndirectOffsetOnAxis(ap=stage[b][:, 4 * s + j:4 * s + j + 1], axis=0),
                            in_=xr[b][:, 2 * j + s, :], in_offset=None, bounds_check=last_row, oob_is_err=False)\
                            .then_inc(scattered[b], 16)

                last_row = pool.alloc_register("last_row")
                pool.reg_mov(last_row, N - 1)

                def slot(u):
                    if u.static() and u.count(0) == 0:
                        stage_part(u, 0, a_staged)
                    u = u.back(3)
                    if not u.valid(PAIRS):
                        return
                    pool.wait_ge(xr_made, u.count(1))
                    pool.wait_ge(a_staged, u.count(1))
                    stage_part(u, 1, b_staged)
                    scatter(u, 0)
                    pool.wait_ge(b_staged, u.count(1))
                    stage_part(u.back(-1), 0, a_staged)
                    scatter(u, 1)

                slots(pool, PAIRS, 4, slot)
                for b in range(2):
                    pool.wait_ge(scattered[b], 128 * ((PAIRS + 1 - b) // 2))

            @block.tensor
            def _(pe):
                def sums(u, n):
                    b = u.off % 2
                    if n == 0:
                        pe.wait_ge(w_loaded[b], u.halves(1) * 48)
                    if n < 2 * H:
                        s, h = n // H, n % H
                        atleast(pe, z_made, u.count(0) * (2 * H) + (n - 1))
                        nc.tensor.matmul(pB[n % 2][:, :], headsel[:, h, :], wt[b][:, s * COLS:(s + 1) * COLS],
                                         start=True, stop=True).then_inc(spread_made, 1)
                    if n:
                        s, h = (n - 1) // H, (n - 1) % H
                        if h == 0:
                            atleast(pe, summed if s else halfway, u.count(0))
                        pe.wait_ge(z_made, u.count(0) * (2 * H) + n)
                        nc.tensor.matmul(pY[64 * s:64 * s + 64, :], Mstack[:, h, :], zb[(n - 1) % 2][:, :],
                                         start=(h == 0), stop=(h == H - 1)).then_inc(z_used, 1)

                def centre(u):
                    pe.wait_ge(h_made, u.count(1))
                    atleast(pe, sq_made, u.count(0))
                    nc.tensor.matmul(pH[:, :], Cm, hb[:, :], start=True, stop=True).then_inc(hc_made, 1)

                def variance(u):
                    pe.wait_ge(sq_made, u.count(1))
                    atleast(pe, v1_made, u.count(0))
                    for j in range(4):
                        last = nc.tensor.matmul(pR[:, 2 * j:2 * j + 2], sq[:, j * 128:(j + 1) * 128], c128("ind"),
                                                start=True, stop=True)
                    last.then_inc(var_made, 1)

                def to_rows(u):
                    atleast(pe, yc_made, u.count(0))
                    for j in range(4):
                        c = slice(j * 128, (j + 1) * 128)
                        nc.tensor.matmul(pG[:, c], hc[:, c], CG[:, :], start=True, stop=True)
                        last = nc.tensor.matmul(pC[:, c], xd[u.off % 4][:, c], Cm, start=True, stop=True)
                    last.then_inc(rows_made, 1)

                def slot(u):
                    for n in range(2 * H + 1):
                        if u.valid(PAIRS):
                            sums(u, n)
                        if n == 0 and u.back(2).valid(PAIRS):
                            variance(u.back(2))
                        if n == 3 and u.back(2).valid(PAIRS):
                            to_rows(u.back(2))
                        if n == 5 and u.back(1).valid(PAIRS):
                            centre(u.back(1))

                slots(pe, PAIRS, 4, slot)

            @block.scalar
            def _(act):
                def copy_targets(u):
                    atleast(act, rows_made, u.count(-3))
                    nc.scalar.activation(xd[u.off % 4][0:64, :], XT[64:128, columns(u, 0)], ACT.Identity,
                                         bias=c128("beta")[64:128, :])
                    nc.scalar.activation(xd[u.off % 4][64:128, :], XT[64:128, columns(u, 1)], ACT.Identity,
                                         bias=c128("beta")[64:128, :]).then_inc(xd_copied, 1)

                def elu_parts(u):
                    b = u.off % 2
                    act.wait_ge(summed, u.count(1))
                    atleast(act, g_made, u.count(0))
                    nc.scalar.activation(ex[:, :], ys[b][:, :], ACT.Exp, bias=c0[:, :])
                    nc.scalar.activation(rl[:, :], ys[b][:, :], ACT.Relu, bias=c0[:, :]).then_inc(e_made, 1)

                def square(u):
                    act.wait_ge(hc_made, u.count(1))
                    atleast(act, rows_made, u.count(0))
                    nc.scalar.activation(sq[:, :], pH[:, :], ACT.Square, bias=ncbeta[:, :])
                    nc.scalar.activation(hc[:, :], pH[:, :], ACT.Identity, bias=ncbeta[:, :]).then_inc(sq_made, 1)

                def square_y(u):
                    act.wait_ge(yc_made, u.count(1))
                    atleast(act, s_made, u.count(0))
                    nc.scalar.activation(q2[:, :, :], yc[u.off % 2][:, :, :], ACT.Square, scale=F ** -0.5).then_inc(squared, 1)

                def slot(u):
                    if u.back(1).valid(PAIRS):
                        elu_parts(u.back(1))
                    if u.back(3).valid(PAIRS):
                        square_y(u.back(3))
                    if u.valid(PAIRS):
                        copy_targets(u)
                    if u.back(1).valid(PAIRS):
                        square(u.back(1))

                slots(act, PAIRS, 4, slot)

            @block.vector
            def _(dve):
                def product(u, n):
                    dve.wait_ge(spread_made, u.count(0) * (2 * H) + (n + 1))
                    atleast(dve, z_used, u.count(0) * (2 * H) + (n - 1))
                    nc.vector.tensor_tensor(zb[n % 2][:, :], pB[n % 2][:, :], XT[:, columns(u, n // H)], ALU.mult)\
                        .then_inc(z_made, 1)

                def scan(u, s):
                    b, half = u.off % 2, slice(64 * s, 64 * s + 64)
                    dve.wait_ge(z_used, u.count(0) * (2 * H) + (s + 1) * H)
                    atleast(dve, e_made, u.count(-1))
                    atleast(dve, crossed, u.count(0) * 2 + s)
                    nc.vector.tensor_tensor_scan(ys[b][half, :], mask[b][half, :], pY[half, :], start[half, :],
                                                 ALU.mult, ALU.add).then_inc(summed if s else halfway, 1)

                def cross(u, s):
                    b = u.off % 2
                    dve.wait_ge(summed if s else halfway, u.count(1))
                    nc.vector.tensor_copy(start[64 - 64 * s:128 - 64 * s, :], ys[b][64 * s:64 * s + 64, COLS - 1:COLS])\
                        .then_inc(crossed, 1)

                def elu(u):
                    dve.wait_ge(e_made, u.count(1))
                    atleast(dve, h_made, u.count(0))
                    nc.vector.scalar_tensor_tensor(gb[:, :], ex[:, :], 1.0, rl[:, :], ALU.min, ALU.add).then_inc(g_made, 1)

                def residual(u):
                    atleast(dve, hc_made, u.count(0))
                    dve.wait_ge(g_made, u.count(1))
                    dve.wait_ge(xd_copied, u.count(1))
                    nc.vector.tensor_tensor(hb[:, :], gb[:, :], xd[u.off % 4][:, :], ALU.add).then_inc(h_made, 1)

                def add_eps(u):
                    dve.wait_ge(var_made, u.count(1))
                    atleast(dve, roots_made, u.count(0))
                    nc.vector.tensor_scalar(v[:, 0:8], pR[:, 0:8], EPS, None, ALU.add).then_inc(v1_made, 1)

                def sum_squares(u):
                    dve.wait_ge(squared, u.count(1))
                    atleast(dve, v2_made, u.count(0))
                    nc.vector.tensor_reduce(s2[:, :], q2[:, :, :], AX.X, ALU.add).then_inc(s_made, 1)
                    dve.wait_ge(s_made, u.count(1))
                    dve.wait_ge(roots_made, u.count(1))
                    nc.vector.tensor_scalar(v[:, 8:16], s2[:, :], EPS, None, ALU.add).then_inc(v2_made, 1)

                def root(u, k):
                    if k == 1:
                        if u.valid(PAIRS):
                            dve.wait_ge(v1_made, u.count(1))
                        atleast(dve, v2_made, u.count(0))
                    if k == ROOT_STEPS:
                        atleast(dve, xr_made, u.count(-1))
                        atleast(dve, scaled, u.count(0))
                    root_step(nc, dve, k, v[:, :], w[:, :], ta[:, :], tb[:, :], root_steps, u.count(0), roots_made)

                def scale(u):
                    dve.wait_ge(roots_made, u.count(1))
                    dve.wait_ge(rows_made, u.count(1))
                    atleast(dve, yc_made, u.count(0))
                    nc.vector.tensor_tensor(yb[:, :, :], pG[:, :].rearrange("p (r f) -> p r f", f=F),
                                            w[:, 0:8].unsqueeze(2).to_broadcast([128, 8, F]), ALU.mult).then_inc(scaled, 1)

                def add_scaled(u):
                    dve.wait_ge(scaled, u.count(1))
                    atleast(dve, xr_made, u.count(-1))
                    nc.vector.tensor_tensor(yc[u.off % 2][:, :, :], yb[:, :, :], pC[:, :].rearrange("p (r f) -> p r f", f=F),
                                            ALU.add).then_inc(yc_made, 1)

                def finish(u):
                    b = u.off % 2
                    dve.wait_ge(roots_made, u.count(2))
                    atleast(dve, scattered[b], u.halves(0) * 128)
                    nc.vector.tensor_tensor(xr[b][:, :, :], yc[b][:, :, :],
                                            w[:, 8:16].unsqueeze(2).to_broadcast([128, 8, F]), ALU.mult).then_inc(xr_made, 1)

                def slot(u):
                    if u.static() and u.count(0) == 0:
                        nc.vector.memset(v[:, :], 1.0)
                        nc.vector.memset(start[:, :], 0.0).then_inc(cleared, 1)
                        dve.wait_ge(cleared, 1)
                    has_roots = u.back(2).valid(PAIRS + 1)
                    for n in range(2 * H):
                        if u.valid(PAIRS):
                            product(u, n)
                        if n == 1 and u.back(1).valid(PAIRS):
                            elu(u.back(1))
                        if n == 2 and u.back(1).valid(PAIRS):
                            residual(u.back(1))
                        if n == 3:
                            if u.back(3).valid(PAIRS):
                                sum_squares(u.back(3))
                            if u.back(2).valid(PAIRS):
                                add_eps(u.back(2))
                        if n == 4 and u.valid(PAIRS):
                            scan(u, 0)
                        if n >= 4 and has_roots:
                            root(u.back(2), 2 * n - 7)
                        if n == 4 and u.valid(PAIRS):
                            cross(u, 0)
                        if n >= 4 and has_roots:
                            root(u.back(2), 2 * n - 6)
                    if u.back(2).valid(PAIRS):
                        scale(u.back(2))
                    if u.valid(PAIRS):
                        scan(u, 1)
                    if u.back(2).valid(PAIRS):
                        add_scaled(u.back(2))
                    if u.valid(PAIRS):
                        cross(u, 1)
                    if u.back(3).valid(PAIRS):
                        finish(u.back(3))

                slots(dve, PAIRS, 4, slot)

        with ExitStack() as dist:
            D = XT[:, 0:PAIRS * COLS]
            with ExitStack() as ph:
                sbp, semp = places(ph, "dist")

                ea = [sbp(f"ea{i}", [7, COLS]) for i in range(2)]
                sq = [sbp(f"sq{i}", [128, 8, F]) for i in range(2)]
                nrm = [sbp(f"nrm{i}", [128, 8, F]) for i in range(2)]
                d1 = sbp("d1", [128, COLS])
                s2 = [sbp(f"s2{i}", [128, 8]) for i in range(2)]
                v, w, ta, tb = (sbp(n, [128, 16]) for n in ("v", "w", "ta", "tb"))
                pL, pT = [bank[0], bank[1]], [bank[2], bank[3]]
                ea_in = [semp(f"ea_in{i}") for i in range(2)]
                lin, sqd, smd, vmd, rtd, nmd, tnd, gld = ([semp(f"{n}{i}") for i in range(2)] for n in (
                    "linear_made", "squares_made", "squares_summed", "v_made", "roots_made", "normed", "turned",
                    "gelu_made"))
                steps = [semp(f"root_steps{i}") for i in range(2)]
                block = ph.enter_context(nc.Block())

                @block.sync
                def _(sp):
                    def slot(u):
                        if not u.valid(PAIRS):
                            return
                        atleast(sp, lin[0], u.count(-1))
                        sp.dma_start(ea[u.off % 2][:, :], ea3[:, bass.ds(u.count(0) * COLS, COLS)])\
                            .then_inc(ea_in[u.off % 2], 16)

                    slots(sp, PAIRS, 1, slot)

                @block.tensor
                def _(pe):
                    def first(u):
                        pe.wait_ge(ea_in[u.off % 2], u.halves(1) * 16)
                        atleast(pe, nmd[0], u.count(0))
                        for j in range(4):
                            c = slice(j * 128, (j + 1) * 128)
                            last = nc.tensor.matmul(pL[0][:, c], ea[u.off % 2][:, c], Wd1[:, :], start=True, stop=True)
                        last.then_inc(lin[0], 1)

                    def second(u):
                        pe.wait_ge(gld[0], u.count(1))
                        atleast(pe, nmd[1], u.count(0))
                        for j in range(4):
                            c = slice(j * 128, (j + 1) * 128)
                            nc.tensor.matmul(pL[1][:, c], d1[:, c], Wd2[:, :], start=True, stop=False)
                            last = nc.tensor.matmul(pL[1][:, c], ones[:, :], b2row[:, :], start=False, stop=True)
                        last.then_inc(lin[1], 1)

                    def turn(n, u):
                        pe.wait_ge(nmd[n], u.count(1))
                        atleast(pe, gld[n], u.count(0))
                        for j in range(4):
                            last = nc.tensor.transpose(
                                pT[n][:, j * 128:(j + 1) * 128],
                                nrm[n][:, 2 * j:2 * j + 2, :].rearrange("p r f -> p (r f)"), ident)
                        last.then_inc(tnd[n], 1)

                    def slot(u):
                        if u.valid(PAIRS):
                            first(u)
                        if u.back(1).valid(PAIRS):
                            second(u.back(1))
                        if u.valid(PAIRS):
                            turn(0, u)
                        if u.back(1).valid(PAIRS):
                            turn(1, u.back(1))

                    slots(pe, PAIRS, 1, slot)

                @block.scalar
                def _(act):
                    def square(n, u):
                        act.wait_ge(lin[n], u.count(1))
                        atleast(act, smd[n], u.count(0))
                        nc.scalar.activation(sq[n][:, :, :], pL[n][:, :].rearrange("p (r f) -> p r f", f=F), ACT.Square,
                                             scale=F ** -0.5).then_inc(sqd[n], 1)

                    def gelu(n, u):
                        act.wait_ge(tnd[n], u.count(1))
                        if n == 0:
                            atleast(act, lin[1], u.count(0))
                            nc.scalar.activation(d1[:, :], pT[0][:, :], ACT.Gelu, bias=c128("b1"), scale=c128("g1"))\
                                .then_inc(gld[0], 1)
                        else:
                            nc.scalar.activation(D[:, bass.ds(u.count(0) * COLS, COLS)], pT[1][:, :], ACT.Gelu,
                                                 bias=c128("b2"), scale=c128("g2")).then_inc(gld[1], 1)

                    def slot(u):
                        if u.valid(PAIRS):
                            square(0, u)
                        if u.back(1).valid(PAIRS):
                            square(1, u.back(1))
                        if u.valid(PAIRS):
                            gelu(0, u)
                        if u.back(1).valid(PAIRS):
                            gelu(1, u.back(1))

                    slots(act, PAIRS, 1, slot)

                @block.vector
                def _(dve):
                    def norm(n, u):
                        h = slice(8 * n, 8 * n + 8)
                        dve.wait_ge(sqd[n], u.count(1))
                        nc.vector.tensor_reduce(s2[n][:, :], sq[n][:, :, :], AX.X, ALU.add).then_inc(smd[n], 1)
                        dve.wait_ge(smd[n], u.count(1))
                        nc.vector.tensor_scalar(v[:, h], s2[n][:, :], EPS, None, ALU.add).then_inc(vmd[n], 1)
                        dve.wait_ge(vmd[n], u.count(1))
                        inverse_roots(nc, dve, v[:, h], w[:, h], ta[:, h], tb[:, h], steps[n], u.count(0), rtd[n])
                        dve.wait_ge(rtd[n], u.count(1))
                        atleast(dve, tnd[n], u.count(0))
                        nc.vector.tensor_tensor(nrm[n][:, :, :], pL[n][:, :].rearrange("p (r f) -> p r f", f=F),
                                                w[:, h].unsqueeze(2).to_broadcast([128, 8, F]), ALU.mult).then_inc(nmd[n], 1)

                    def slot(u):
                        if u.valid(PAIRS):
                            norm(0, u)
                        if u.back(1).valid(PAIRS):
                            norm(1, u.back(1))

                    slots(dve, PAIRS, 1, slot)

            with ExitStack() as ph:
                sbp, semp = places(ph, "second")

                stage = [sbp(f"stage{i}", [128, 12], i32) for i in range(2)]
                pairs = [sbp(f"pairs{i}", [128, 4, 2 * F]) for i in range(4)]
                mask = [sbp(f"mask{i}", [128, COLS], bf16) for i in range(2)]
                xe = [sbp(f"xe{i}", [128, COLS]) for i in range(2)]
                top = [sbp(f"top{i}", [128, COLS + 1]) for i in range(2)]
                fall, below = sbp("fall", [128, COLS]), sbp("below", [128, COLS])
                fell = sbp("fell", [128, COLS])
                decay = [sbp(f"decay{i}", [128, COLS]) for i in range(2)]
                term = [sbp(f"term{i}", [128, COLS]) for i in range(2)]
                sums = [sbp(f"sums{i}", [128, COLS]) for i in range(2)]
                inv, quo = sbp("inv", [128, 4, F]), sbp("quo", [128, 4, F])
                res, cen, sqr = sbp("res", [128, 4, F]), sbp("cen", [128, 4, F]), sbp("sqr", [128, 4, F])
                orow = [sbp(f"orow{i}", [128, 4, F]) for i in range(2)]
                mean, nmean, s2 = sbp("mean", [128, 4]), sbp("nmean", [128, 4]), sbp("s2", [128, 4])
                v, w, ta, tb = (sbp(n, [128, 4]) for n in ("v", "w", "ta", "tb"))
                pA, pL, pW, pS = bank[0], [bank[1], bank[2]], [bank[3], bank[4]], [bank[5], bank[6]]

                gathered = [semp(f"gathered{i}") for i in range(2)]
                scattered = [semp(f"scattered{i}") for i in range(2)]
                mask_in = [semp(f"mask_in{i}") for i in range(2)]
                (s_staged, t_staged, o_staged, turned, copied, linear, topped, carried, fall_made, fell_made, below_made,
                 exps_made, term_made, summed, rows_made, inv_made, quo_made, res_made, mean_made, nmean_made, cen_made,
                 sqr_made, s2_made, v_made, root_steps, roots_made, out_made, cleared) = (semp(n) for n in (
                     "s_staged", "t_staged", "o_staged", "turned", "copied", "linear", "topped", "carried", "fall_made",
                     "fell_made", "below_made", "exps_made", "term_made", "summed", "rows_made", "inv_made", "quo_made",
                     "res_made", "mean_made", "nmean_made", "cen_made", "sqr_made", "s2_made", "v_made", "root_steps",
                     "roots_made", "out_made", "cleared"))
                block = ph.enter_context(nc.Block())

                @block.sync
                def _(sp):
                    def slot(u):
                        if not u.valid(UNITS):
                            return
                        b = u.off % 2
                        atleast(sp, fell_made, u.count(-1))
                        sp.dma_start(mask[b][:, :], mask_rows[1:2, bass.ds(u.count(0) * COLS, COLS)].to_broadcast([128, COLS]))\
                            .then_inc(mask_in[b], 16)

                    slots(sp, UNITS, 1, slot)

                @block.gpsimd
                def _(pool):
                    last_row = pool.alloc_register("last_out_row")
                    pool.reg_mov(last_row, N - 1)

                    def stage_gather(u, k, staged):
                        if u.valid(UNITS):
                            atleast(pool, gathered[u.off % 2], u.halves(0) * 128)
                            nc.gpsimd.tensor_copy(stage[u.off % 2][:, k:k + 4], gix[:, bass.ds(u.count(0) * 8 + k, 4)])\
                                .then_inc(staged, 1)

                    def stage_scatter(u):
                        if u.valid(UNITS):
                            atleast(pool, scattered[u.off % 2], u.halves(0) * 64)
                            nc.gpsimd.tensor_copy(stage[u.off % 2][:, 8:12], scatter_rows[:, bass.ds(u.count(0) * 4, 4)])\
                                .then_inc(o_staged, 1)

                    def gather(u, js):
                        a = u.off % 2
                        for j in js:
                            pool.indirect_dma_start(
                                out=pairs[u.off % 4][:, j % 4, F * (j // 4):F * (j // 4) + F], out_offset=None, in_=x1,
                                in_offset=bass.IndirectOffsetOnAxis(ap=stage[a][:, j:j + 1], axis=0))\
                                .then_inc(gathered[a], 16)

                    def scatter(u):
                        a = u.off % 2
                        for j in range(4):
                            pool.indirect_dma_start(
                                out=out, out_offset=bass.IndirectOffsetOnAxis(ap=stage[a][:, 8 + j:9 + j], axis=0),
                                in_=orow[a][:, j, :], in_offset=None, bounds_check=last_row, oob_is_err=False)\
                                .then_inc(scattered[a], 16)

                    def slot(u):
                        if u.static() and u.count(0) == 0:
                            stage_gather(u, 0, s_staged)
                        if u.valid(UNITS):
                            atleast(pool, res_made, u.count(-3))
                            pool.wait_ge(s_staged, u.count(1))
                            stage_gather(u, 4, t_staged)
                            gather(u, range(4))
                            pool.wait_ge(t_staged, u.count(1))
                        o = u.back(3)
                        if u.valid(UNITS):
                            if o.valid(UNITS):
                                stage_scatter(o)
                            else:
                                stage_gather(u.back(-1), 0, s_staged)
                            gather(u, range(4, 8))
                        elif o.valid(UNITS):
                            stage_scatter(o)
                        if o.valid(UNITS):
                            pool.wait_ge(out_made, o.count(1))
                            pool.wait_ge(o_staged, o.count(1))
                            if u.valid(UNITS):
                                stage_gather(u.back(-1), 0, s_staged)
                            scatter(o)

                    slots(pool, UNITS, 4, slot)
                    for b in range(2):
                        pool.wait_ge(scattered[b], 64 * (UNITS // 2))

                @block.tensor
                def _(pe):
                    def turn(u):
                        pe.wait_ge(gathered[u.off % 2], u.halves(1) * 128)
                        atleast(pe, copied, u.count(0))
                        for j in range(4):
                            last = nc.tensor.transpose(pA[:, j * 128:(j + 1) * 128], pairs[u.off % 4][:, j, :], ident)
                        last.then_inc(turned, 1)

                    def logits(u):
                        b = u.off % 2
                        pe.wait_ge(copied, u.count(1))
                        atleast(pe, term_made, u.count(-1))
                        d = D[:, bass.ds(u.halves(0) * COLS, COLS)]
                        sel = c128("dA") if b == 0 else c128("dB")
                        nc.tensor.matmul(pL[b][:, :], c128("Wqq"), xe[b][:, :], start=True, stop=False)
                        nc.tensor.matmul(pL[b][:, :], sel, d, start=False, stop=True)
                        nc.tensor.matmul(pW[b][:, :], c128("Wv"), xe[b][:, :], start=True, stop=False)
                        nc.tensor.matmul(pW[b][:, :], sel, d, start=False, stop=True).then_inc(linear, 1)

                    def turn_sums(u):
                        b = u.off % 2
                        pe.wait_ge(summed, u.count(1))
                        atleast(pe, quo_made, u.count(-1))
                        for j in range(4):
                            last = nc.tensor.transpose(pS[b][:, j * 128:(j + 1) * 128], sums[b][:, j * 128:(j + 1) * 128], ident)
                        last.then_inc(rows_made, 1)

                    def slot(u):
                        if u.valid(UNITS):
                            turn(u)
                            logits(u)
                        if u.back(1).valid(UNITS):
                            turn_sums(u.back(1))

                    slots(pe, UNITS, 4, slot)

                @block.scalar
                def _(act):
                    def copy(u):
                        b = u.off % 2
                        act.wait_ge(turned, u.count(1))
                        atleast(act, linear, u.count(-1))
                        nc.scalar.activation(xe[b][:, :], pA[:, :], ACT.Copy).then_inc(copied, 1)

                    def exps(u):
                        b = u.off % 2
                        act.wait_ge(below_made, u.count(1))
                        act.wait_ge(fell_made, u.count(1))
                        atleast(act, summed, u.count(-1))
                        nc.scalar.activation(decay[b][:, :], fell[:, :], ACT.Exp)
                        nc.scalar.activation(term[b][:, :], below[:, :], ACT.Exp).then_inc(exps_made, 1)

                    def square(u):
                        act.wait_ge(cen_made, u.count(1))
                        nc.scalar.activation(sqr[:, :, :], cen[:, :, :], ACT.Square, scale=F ** -0.5).then_inc(sqr_made, 1)

                    def slot(u):
                        if u.valid(UNITS):
                            copy(u)
                        if u.back(2).valid(UNITS):
                            square(u.back(2))
                        if u.back(1).valid(UNITS):
                            exps(u.back(1))

                    slots(act, UNITS, 4, slot)

                @block.vector
                def _(dve):
                    def maxima(u):
                        b = u.off % 2
                        before = top[1 - b][:, COLS:COLS + 1]
                        dve.wait_ge(linear, u.count(1))
                        dve.wait_ge(mask_in[b], u.halves(1) * 16)
                        atleast(dve, topped, u.count(0))
                        atleast(dve, fall_made, u.count(-1))
                        nc.vector.tensor_copy(top[b][:, 0:1], before).then_inc(carried, 1)
                        nc.vector.tensor_tensor_scan(top[b][:, 1:], mask[b][:, :], pL[b][:, :], before, ALU.add, ALU.max)\
                            .then_inc(topped, 1)
                        dve.wait_ge(carried, u.count(1))
                        dve.wait_ge(topped, u.count(1))
                        atleast(dve, fell_made, u.count(0))
                        nc.vector.tensor_tensor(fall[:, :], top[b][:, 0:COLS], top[b][:, 1:], ALU.subtract).then_inc(fall_made, 1)
                        atleast(dve, exps_made, u.count(0))
                        nc.vector.tensor_tensor(below[:, :], pL[b][:, :], top[b][:, 1:], ALU.subtract).then_inc(below_made, 1)
                        dve.wait_ge(fall_made, u.count(1))
                        nc.vector.tensor_tensor(fell[:, :], fall[:, :], mask[b][:, :], ALU.add).then_inc(fell_made, 1)

                    def segment_sums(u):
                        b = u.off % 2
                        dve.wait_ge(exps_made, u.count(1))
                        nc.vector.tensor_tensor(term[b][64:128, :], term[b][64:128, :], pW[b][64:128, :], ALU.mult)\
                            .then_inc(term_made, 1)
                        dve.wait_ge(term_made, u.count(1))
                        atleast(dve, summed, u.count(0))
                        atleast(dve, rows_made, u.count(-1))
                        nc.vector.tensor_tensor_scan(sums[b][:, :], decay[b][:, :], term[b][:, :],
                                                     sums[1 - b][:, COLS - 1:COLS], ALU.mult, ALU.add).then_inc(summed, 1)

                    def result(u):
                        b = u.off % 2
                        dve.wait_ge(rows_made, u.count(1))
                        r = pS[b][:, :].rearrange("p (t s f) -> p t s f", t=4, s=2)
                        atleast(dve, quo_made, u.count(0))
                        nc.vector.reciprocal(inv[:, :, :], r[:, :, 0, :]).then_inc(inv_made, 1)
                        dve.wait_ge(inv_made, u.count(1))
                        atleast(dve, res_made, u.count(0))
                        nc.vector.tensor_tensor(quo[:, :, :], r[:, :, 1, :], inv[:, :, :], ALU.mult).then_inc(quo_made, 1)
                        dve.wait_ge(quo_made, u.count(1))
                        atleast(dve, cen_made, u.count(0))
                        nc.vector.tensor_tensor(res[:, :, :], quo[:, :, :], pairs[u.off % 4][:, :, F:2 * F], ALU.add).then_inc(res_made, 1)
                        dve.wait_ge(res_made, u.count(1))
                        nc.vector.tensor_reduce(mean[:, :], res[:, :, :], AX.X, ALU.add).then_inc(mean_made, 1)
                        dve.wait_ge(mean_made, u.count(1))
                        nc.vector.tensor_scalar(nmean[:, :], mean[:, :], -1.0 / F, None, ALU.mult).then_inc(nmean_made, 1)
                        dve.wait_ge(nmean_made, u.count(1))
                        atleast(dve, out_made, u.count(0))
                        nc.vector.tensor_tensor(cen[:, :, :], res[:, :, :], nmean[:, :].unsqueeze(2).to_broadcast([128, 4, F]),
                                                ALU.add).then_inc(cen_made, 1)

                    def norm(u):
                        b = u.off % 2
                        dve.wait_ge(sqr_made, u.count(1))
                        nc.vector.tensor_reduce(s2[:, :], sqr[:, :, :], AX.X, ALU.add).then_inc(s2_made, 1)
                        dve.wait_ge(s2_made, u.count(1))
                        nc.vector.tensor_scalar(v[:, :], s2[:, :], EPS, None, ALU.add).then_inc(v_made, 1)
                        dve.wait_ge(v_made, u.count(1))
                        inverse_roots(nc, dve, v[:, :], w[:, :], ta[:, :], tb[:, :], root_steps, u.count(0), roots_made)
                        dve.wait_ge(roots_made, u.count(1))
                        atleast(dve, scattered[b], u.halves(0) * 64)
                        nc.vector.tensor_tensor(orow[b][:, :, :], cen[:, :, :], w[:, :].unsqueeze(2).to_broadcast([128, 4, F]),
                                                ALU.mult).then_inc(out_made, 1)

                    def slot(u):
                        if u.static() and u.count(0) == 0:
                            nc.vector.memset(top[1][:, COLS:COLS + 1], -BIG)
                            nc.vector.memset(sums[1][:, COLS - 1:COLS], 0.0).then_inc(cleared, 1)
                            dve.wait_ge(cleared, 1)
                        if u.back(2).valid(UNITS):
                            result(u.back(2))
                        if u.back(1).valid(UNITS):
                            maxima(u.back(1))
                        if u.back(2).valid(UNITS):
                            norm(u.back(2))
                        if u.back(1).valid(UNITS):
                            segment_sums(u.back(1))

                    slots(dve, UNITS, 4, slot)


def _layout(a):
    import numpy as np
    src, dst = a["src"], a["dst"]
    pad = EP - E

    def rows(v):
        return np.ascontiguousarray(v.reshape(TILES, 128).T)

    def blocks(v):
        return np.ascontiguousarray(v.reshape(2, QR, 128).transpose(1, 0, 2))

    zero = np.zeros(pad, np.int32)
    s_rows, d_rows = rows(np.concatenate([src, zero])), rows(np.concatenate([dst, zero]))
    gidx = np.stack([s_rows.reshape(128, UNITS, 4), d_rows.reshape(128, UNITS, 4)], axis=2)
    own = np.arange(N, N + pad, dtype=np.int32)
    d = np.concatenate([dst, own])
    edge = np.array([-1], np.int32)
    before, after = np.concatenate([edge, d[:-1]]), np.concatenate([d[1:], edge])
    dblk = np.stack([blocks(before), blocks(d), blocks(after)], axis=1)
    drow = np.stack([rows(d), rows(after)], axis=1)
    eaT = np.concatenate([a["edge_attr_16"].T, np.zeros((16, pad), np.float32)], axis=1)
    e3 = np.concatenate([a["edge_attr_3"].T, np.zeros((3, pad), np.float32)], axis=1)
    ea3 = e3.reshape(3, PAIRS, 2, COLS).transpose(2, 0, 1, 3).reshape(6, PAIRS * COLS)
    ea3 = np.concatenate([ea3, np.ones((1, PAIRS * COLS), np.float32)], axis=0)

    def twice(v):
        return np.concatenate([v, v], axis=-1)

    W, Wp, We = a["L0_gnn_W"], a["L0_gnn_Wp"], a["L0_gnn_W_edge"]
    p64 = np.concatenate([
        twice(W.reshape(F, H, F).transpose(2, 1, 0)).reshape(F, -1),
        twice(Wp.reshape(H, F, F).transpose(1, 0, 2)).reshape(F, -1),
        We.reshape(16, H, F).transpose(2, 1, 0).reshape(F, -1),
        a["L0_gnn_att_src"].T, a["L0_gnn_att_dst"].T, a["L0_gnn_att_edge"].T,
        a["L0_gnn_bias"].reshape(H, F).T], axis=1)

    def col(n):
        return twice(a[n])[:, None]

    def diag(w):
        o = np.zeros((128, 2 * w.shape[1]), np.float32)
        o[:F, :w.shape[1]] = w
        o[F:, w.shape[1]:] = w
        return o

    k, m = np.arange(128)[:, None], np.arange(128)[None, :]
    same = (k // F == m // F).astype(np.float32)
    eye = np.eye(128, dtype=np.float32)
    r = np.arange(24)[:, None]
    head = np.zeros((128, H * 128), np.float32)
    for h in range(H):
        head[:24, h * 128:(h + 1) * 128] = r % 8 == h + 4 * (m // F)
    p128 = np.concatenate([
        col("L0_gnn_bp"), col("L0_gnn_gamma"), col("L0_gnn_beta"), col("L1_gnn_g1"), col("L1_gnn_b1"),
        col("L1_gnn_bd2"), col("L1_gnn_g2"), col("L1_gnn_b2"),
        diag(a["L1_gnn_Wd1"].T), col("L1_gnn_bd1"), diag(a["L1_gnn_Wd2"].T),
        np.concatenate([twice(a["L1_gnn_W2"]), twice(a["L1_gnn_W1"])], axis=0),
        np.pad(a["L1_gnn_W3"], ((0, F), (F, 0))),
        eye, eye - same / F, same / F, (k // F == np.arange(2)[None, :]).astype(np.float32) / F,
        (k == m % F).astype(np.float32), (k == F + m % F).astype(np.float32), head], axis=1)
    return {"x": a["x"], "gidx": gidx.reshape(128, -1), "drow": drow.reshape(128, -1),
            "dblk": dblk.reshape(QR, -1), "eaT": eaT, "ea3": ea3, "p64": p64.astype(np.float32),
            "p128": p128.astype(np.float32)}


def kernel(**inputs):
    import numpy as _np
    import concourse.bacc as _bacc
    from concourse import mybir as _mybir
    from concourse.bass_utils import run_bass_kernel_spmd as _run

    nc = _bacc.Bacc("TRN2", target_bir_lowering=False, num_devices=1)
    arrays, args = {}, []
    for name, a in _layout({n: _np.asarray(v) for n, v in inputs.items()}).items():
        a = _np.ascontiguousarray(a)
        arrays[f"in_{name}_dram"] = a
        args.append(nc.dram_tensor(f"in_{name}_dram", a.shape, _mybir.dt.from_np(a.dtype), kind="ExternalInput").ap())
    out = nc.dram_tensor("out_0_dram", (N, F), _mybir.dt.float32, kind="ExternalOutput").ap()
    gnn(nc, *args, out)
    r = _run(nc, [arrays], core_ids=[0])
    return r.results[0]["out_0_dram"]
```

```python
import concourse.bass as bass
from concourse import mybir
from contextlib import ExitStack

N, E, F, H = 100000, 25000, 64, 4
EPS = 1e-5
BIG = 1.0e30
SKIP = 8388608.0
COLS = 512
NODES = 2 * COLS
DENSE = -(-N // NODES)
UNITS = 50
TILES = 4 * UNITS
EP = UNITS * COLS
QR = TILES // 2
PAIRS = UNITS // 2
CH = 12
ALU = mybir.AluOpType
ACT = mybir.ActivationFunctionType
AX = mybir.AxisListType
fp32, bf16, i32 = mybir.dt.float32, mybir.dt.bfloat16, mybir.dt.int32

P64 = {}
_at = 0
for _n, _w in (("WT", H * 128), ("Wp", H * 128), ("WeT", H * 16), ("aS", H), ("aD", H), ("aE", H), ("bias", H)):
    P64[_n] = (_at, _at + _w)
    _at += _w
W64 = _at
P128 = {}
_at = 0
for _n, _w in (("bp", 1), ("gamma", 1), ("beta", 1), ("g1", 1), ("b1", 1), ("bd2", 1), ("g2", 1), ("b2", 1),
               ("Wd1T", 7), ("Wd2T", 128), ("Wqq", 128), ("Wv", 128), ("ident", 128), ("C", 128),
               ("ind", 2), ("dA", 128), ("dB", 128), ("head", H * 128)):
    P128[_n] = (_at, _at + _w)
    _at += _w
W128 = _at


class Unit:

    def __init__(self, i, off):
        self.i, self.off = i, off

    def back(self, n):
        return Unit(self.i, self.off - n)

    def count(self, n=1):
        return self.i * 4 + (self.off + n)

    def halves(self, n=0):
        return self.i * 2 + (self.off // 2 + n)

    def quarters(self, n=0):
        return self.i + (self.off // 4 + n)

    def edge(self, n):
        return EdgeUnit(self.i, (self.off - 1) // 2 - n)

    def static(self):
        return isinstance(self.i, int)

    def valid(self, n):
        return not self.static() or 0 <= self.count(0) < n


class EdgeUnit:

    def __init__(self, i, off):
        self.i, self.off = i, off

    def count(self, n=1):
        return self.i * 2 + (self.off + n)

    def halves(self, n=0):
        return self.i + (self.off // 2 + n)

    def next(self):
        return EdgeUnit(self.i, self.off + 1)

    def valid(self, n):
        return not isinstance(self.i, int) or 0 <= self.count(0) < n


def atleast(eng, sem, value):
    if not isinstance(value, int) or value > 0:
        eng.wait_ge(sem, value)


MAGIC = float(0x5F1FFFF9)


def root_step(nc, dve, k, v, w, ta, tb, step, before, made):
    c1, c2 = 0.703952253, 0.703952253 * 2.38924456
    if k > 1:
        dve.wait_ge(step, (ROOT_STEPS - 1) * before + (k - 1))
    if k == 1:
        nc.vector.tensor_scalar(ta.bitcast(i32), v.bitcast(i32), 1, None, ALU.arith_shift_right).then_inc(step, 1)
    if k == 2:
        nc.vector.tensor_scalar(tb.bitcast(i32), ta.bitcast(i32), -1.0, MAGIC, ALU.mult, ALU.add).then_inc(step, 1)
    if k == 3:
        nc.vector.scalar_tensor_tensor(ta, tb, -c1, tb, ALU.mult, ALU.mult).then_inc(step, 1)
    if k == 4:
        nc.vector.tensor_tensor(ta, ta, v, ALU.mult).then_inc(step, 1)
    if k == 5:
        nc.vector.scalar_tensor_tensor(tb, ta, c2, tb, ALU.add, ALU.mult).then_inc(step, 1)
    if k == 6:
        nc.vector.scalar_tensor_tensor(ta, tb, -0.5, tb, ALU.mult, ALU.mult).then_inc(step, 1)
    if k == 7:
        nc.vector.tensor_tensor(ta, ta, v, ALU.mult).then_inc(step, 1)
    if k == 8:
        nc.vector.scalar_tensor_tensor(w, ta, 1.5, tb, ALU.add, ALU.mult).then_inc(made, 1)


ROOT_STEPS = 8


def slots(eng, total, skew, body, ahead=0):
    loops = (total - ahead) // 4
    for k in range(8):
        body(Unit(0, k))
    with eng.Fori(2, loops) as i:
        for k in range(4):
            body(Unit(i, k))
    for k in range(4 * loops, total + skew):
        body(Unit(0, k))


def gnn(nc, x, gidx, drow, dblk, eaT, ea3, p64, p128, out):
    x1 = nc.dram_tensor("x1_table", [N, F], fp32, kind="Internal").ap()
    logit_rows = nc.dram_tensor("logit_rows", [CH, EP], fp32, kind="Internal").ap()
    weight_rows = nc.dram_tensor("weight_rows", [24, EP], bf16, kind="Internal").ap()
    mask_rows = nc.dram_tensor("mask_rows", [3, EP], bf16, kind="Internal").ap()
    target_rows = nc.dram_tensor("target_rows", [128, TILES * F], fp32, kind="Internal").ap()

    with ExitStack() as ctx:
        def sb(name, shape, dt=fp32):
            return ctx.enter_context(nc.sbuf_tensor(name, shape, dt))

        def sem(name):
            return ctx.enter_context(nc.semaphore(name))

        def places(ph, phase):
            def buffer(name, shape, dt=fp32):
                return ph.enter_context(nc.sbuf_tensor(f"{phase}_{name}", shape, dt))

            def semaphore(name):
                return ph.enter_context(nc.semaphore(f"{phase}_{name}"))

            return buffer, semaphore

        bank = [ctx.enter_context(nc.psum_tensor(f"bank{i}", [128, COLS], fp32)) for i in range(8)]
        prm64 = sb("prm64", [64, W64])
        prm = sb("prm", [128, W128])
        gix = sb("gix", [128, UNITS * 8], i32)
        XT = sb("XT", [128, EP])

        def c64(n):
            return prm64[:, P64[n][0]:P64[n][1]]

        def c128(n):
            return prm[:, P128[n][0]:P128[n][1]]

        ident, Cm = c128("ident"), c128("C")
        Mstack = sb("Mstack", [128, H, F])
        Mblk = sb("Mblk", [128, 128])
        Wal = sb("Wal", [128, CH])
        WalE = sb("WalE", [16, CH])
        c0 = sb("c0", [128, 1])
        c0x = sb("c0x", [128, 1])
        ncbeta = sb("ncbeta", [128, 1])
        CG = sb("CG", [128, 128])
        Wd1 = sb("Wd1", [7, 128])
        b2row = sb("b2row", [1, 128])
        b2part = sb("b2part", [1, 128], bf16)
        b2rest = sb("b2rest", [1, 128])
        b2parts = sb("b2parts", [96, 4, 128], bf16)
        ones = sb("ones", [96, 128], bf16)
        Wd2 = sb("Wd2", [128, 128])
        headsel = sb("headsel", [24, H, 128], bf16)
        minus = sb("minus", [128, 128])

        s_b2 = sem("bias_split")
        s_prm, s_pe0, s_ev0, s_pe1, s_z0, s_gix = (sem(n) for n in (
            "params_loaded", "products_made", "products_copied", "beta_projected", "zeroed", "indices_loaded"))
        with nc.Block() as block:
            @block.sync
            def _(sp):
                sp.dma_start(prm64[:, :], p64).then_inc(s_prm, 16)
                sp.dma_start(prm[:, :], p128).then_inc(s_prm, 16)
                sp.dma_start(gix[:, :], gidx).then_inc(s_gix, 16)
                sp.wait_ge(s_gix, 16)

            @block.tensor
            def _(pe):
                pe.wait_ge(s_prm, 32)
                WT, Wp, WeT = (c64(n).rearrange("c (h k) -> c h k", h=H) for n in ("WT", "Wp", "WeT"))
                for h in range(H):
                    nc.tensor.matmul(bank[0][:, h * F:(h + 1) * F], WT[:, h, :], Wp[:, h, 0:F],
                                     start=True, stop=True)
                    nc.tensor.matmul(bank[1][:, 0:F], WT[:, h, :], Wp[:, h, 0:F], start=(h == 0), stop=(h == H - 1))
                for h in range(H):
                    nc.tensor.matmul(bank[2][:, h:h + 1], WT[:, h, :], c64("aS")[:, h:h + 1], start=True, stop=True)
                    nc.tensor.matmul(bank[2][:, 4 + h:5 + h], WT[:, h, :], c64("aD")[:, h:h + 1], start=True, stop=True)
                    nc.tensor.matmul(bank[3][0:16, h:h + 1], WeT[:, h, :], c64("aE")[:, h:h + 1], start=True, stop=True)
                for h in range(H):
                    nc.tensor.matmul(bank[4][:, 0:1], Wp[:, h, :], c64("bias")[:, h:h + 1],
                                     start=(h == 0), stop=(h == H - 1))
                nc.tensor.matmul(bank[5][:, 0:1], Cm, c128("beta"), start=True, stop=True)
                nc.tensor.matmul(bank[0][0:1, 256:384], c128("bd2"), Cm, start=True, stop=True)
                nc.tensor.matmul(bank[6][0:7, 0:128], c128("Wd1T"), Cm, start=True, stop=True)
                nc.tensor.matmul(bank[7][:, 0:128], c128("Wd2T"), Cm, start=True, stop=True).then_inc(s_pe0, 1)
                pe.wait_ge(s_ev0, 2)
                nc.tensor.matmul(bank[5][:, 3:4], Mblk[:, :], c128("beta"), start=True, stop=True).then_inc(s_pe1, 1)

            @block.vector
            def _(dve):
                nc.vector.memset(Mblk[:, :], 0.0)
                nc.vector.memset(b2parts[:, :, :], 0.0)
                nc.vector.memset(Wal[:, :], 0.0)
                nc.vector.memset(WalE[:, :], 0.0).then_inc(s_z0, 1)
                dve.wait_ge(s_z0, 1)
                dve.wait_ge(s_prm, 32)
                nc.vector.tensor_copy(headsel[:, :, :], c128("head")[0:24, :].rearrange("r (h m) -> r h m", h=H))
                dve.wait_ge(s_pe0, 1)
                nc.vector.tensor_copy(Mstack[:, :, :], bank[0][:, 0:H * F].rearrange("p (h f) -> p h f", h=H))
                nc.vector.tensor_copy(Mblk[0:64, 0:64], bank[1][0:64, 0:F])
                nc.vector.tensor_copy(Mblk[64:128, 64:128], bank[1][64:128, 0:F])
                nc.vector.tensor_copy(Wal[0:64, 0:4], bank[2][0:64, 0:4])
                nc.vector.tensor_copy(Wal[64:128, 0:4], bank[2][64:128, 4:8])
                nc.vector.tensor_copy(Wal[64:128, 8:12], bank[2][64:128, 0:4]).then_inc(s_ev0, 1)
                dve.wait_ge(s_ev0, 1)
                nc.vector.tensor_tensor(Wal[64:128, 8:12], Wal[64:128, 8:12], bank[2][64:128, 4:8], ALU.add)
                nc.vector.tensor_copy(WalE[:, 0:4], bank[3][0:16, 0:4])
                nc.vector.tensor_copy(WalE[:, 4:8], bank[3][0:16, 0:4])
                nc.vector.tensor_tensor(c0[:, :], bank[4][:, 0:1], c128("bp"), ALU.add)
                nc.vector.tensor_scalar(ncbeta[:, :], bank[5][:, 0:1], -1.0, None, ALU.mult)
                nc.vector.tensor_scalar(minus[:, :], ident, -1.0, None, ALU.mult)
                nc.vector.tensor_scalar(CG[:, :], Cm, c128("gamma"), None, ALU.mult)
                nc.vector.memset(ones[:, :], 1.0)
                nc.vector.tensor_copy(Wd1[:, :], bank[6][0:7, 0:128])
                nc.vector.tensor_copy(Wd2[:, :], bank[7][:, 0:128])
                nc.vector.tensor_scalar(c128("Wqq")[0:64, :], c128("Wqq")[0:64, :], -1.0, None, ALU.mult).then_inc(s_ev0, 1)
                for k in range(3):
                    src = b2row if k % 2 == 0 else b2rest
                    if k == 0:
                        nc.vector.tensor_copy(b2row[:, :], bank[0][0:1, 256:384]).then_inc(s_b2, 1)
                        dve.wait_ge(s_b2, 1)
                    spread = src[:, :].unsqueeze(1).to_broadcast([1, 4, 128])
                    nc.vector.tensor_copy(b2parts[32 * k:32 * k + 1, :, :], spread)
                    if k < 2:
                        left = b2rest if k % 2 == 0 else b2row
                        nc.vector.tensor_copy(b2part[:, :], src[:, :]).then_inc(s_b2, 1)
                        dve.wait_ge(s_b2, 2 * k + 2)
                        nc.vector.tensor_tensor(left[:, :], src[:, :], b2part[:, :], ALU.subtract).then_inc(s_b2, 1)
                        dve.wait_ge(s_b2, 2 * k + 3)
                dve.wait_ge(s_ev0, 2)
                dve.wait_ge(s_pe1, 1)
                nc.vector.tensor_tensor(c0x[:, :], c0[:, :], bank[5][:, 3:4], ALU.subtract)

        with ExitStack() as ph:
            sbp, semp = places(ph, "dense")

            rows = [sbp(f"rows{i}", [128, 8 * F]) for i in range(4)]
            xT = [sbp(f"xT{i}", [128, COLS]) for i in range(4)]
            ex = [sbp(f"ex{i}", [128, COLS]) for i in range(2)]
            rl = [sbp(f"rl{i}", [128, COLS]) for i in range(2)]
            gb = sbp("gb", [128, COLS])
            hb = [sbp(f"hb{i}", [128, COLS]) for i in range(2)]
            sq = [sbp(f"sq{i}", [128, COLS]) for i in range(2)]
            hc = [sbp(f"hc{i}", [128, COLS]) for i in range(2)]
            yb = sbp("yb", [128, 8, F])
            yc = [sbp(f"yc{i}", [128, 8, F]) for i in range(4)]
            q2 = [sbp(f"q2{i}", [128, 8, F]) for i in range(2)]
            s2 = sbp("s2", [128, 8])
            v, w, ta, tb = (sbp(n, [128, 24]) for n in ("v", "w", "ta", "tb"))
            xr = [sbp(f"xr{i}", [128, 8, F]) for i in range(2)]
            orow = [sbp(f"orow{i}", [128, 8, F]) for i in range(2)]
            stage = [sbp(f"stage{i}", [128, 8], i32) for i in range(2)]
            pairs = [sbp(f"pairs{i}", [128, 4, 2 * F]) for i in range(2)]
            eab = [sbp(f"eab{i}", [16, COLS]) for i in range(2)]
            lrow = [sbp(f"lrow{i}", [CH, COLS]) for i in range(2)]
            pT, pH, pR, pA = bank[0], bank[1], bank[2], bank[3]
            pG, pX, pP = [bank[4], bank[5]], bank[6], bank[7]

            x_loaded = [semp(f"x_loaded{i}") for i in range(4)]
            stored = [semp(f"stored{i}") for i in range(2)]
            (xt_made, x_copied, p_made, e_made, g_made, h_made, hc_made, sq_made, var_made, g_rows_made, v1_made,
             scaled, y_made, y_squared, y_summed, v2_made, out_made) = (semp(n) for n in (
                 "xt_made", "x_copied", "p_made", "e_made", "g_made", "h_made", "hc_made", "sq_made", "var_made",
                 "g_rows_made", "v1_made", "scaled", "y_made", "y_squared", "y_summed", "v2_made", "out_made"))
            v_cleared, root_steps, roots_made = semp("v_cleared"), semp("root_steps"), semp("roots_made")
            gathered = [semp(f"gathered{i}") for i in range(2)]
            ea_loaded = [semp(f"ea_loaded{i}") for i in range(2)]
            l_stored = [semp(f"l_stored{i}") for i in range(2)]
            sources_staged, targets_staged, pair_turned, pair_copied, l_made, l_copied = (semp(n) for n in (
                "sources_staged", "targets_staged", "pair_turned", "pair_copied", "l_made", "l_copied"))

            def node_rows(table, u):
                if u.static():
                    n0 = min(u.count(0) * NODES, N - NODES)
                    t = table[n0:n0 + NODES, :]
                else:
                    t = table[bass.ds(u.count(0) * NODES, NODES), :]
                return t.rearrange("(p r) f -> p (r f)", p=128)

            block = ph.enter_context(nc.Block())

            @block.sync
            def _(sp):
                def load(u):
                    atleast(sp, xt_made, u.count(-3))
                    sp.dma_start(rows[u.off % 4][:, :], node_rows(x, u)).then_inc(x_loaded[u.off % 4], 16)

                def store(u):
                    b = u.off % 2
                    sp.wait_ge(out_made, u.count(1))
                    if u.static() and u.count(0) == DENSE - 1:
                        sp.wait_ge(stored[1 - b], 32 * ((DENSE - 2) // 2 + 1))
                    sp.dma_start(node_rows(x1, u), xr[b][:, :, :].rearrange("p r f -> p (r f)")).then_inc(stored[b], 16)
                    sp.dma_start(node_rows(out, u), orow[b][:, :, :].rearrange("p r f -> p (r f)")).then_inc(stored[b], 16)

                def load_attributes(e):
                    atleast(sp, l_made, e.count(-1))
                    sp.dma_start(eab[e.off % 2][:, :], eaT[:, bass.ds(e.count(0) * COLS, COLS)])\
                        .then_inc(ea_loaded[e.off % 2], 16)

                def store_logits(e):
                    sp.wait_ge(l_copied, e.count(1))
                    sp.dma_start(logit_rows[:, bass.ds(e.count(0) * COLS, COLS)], lrow[e.off % 2][:, :])\
                        .then_inc(l_stored[e.off % 2], 16)

                def slot(u):
                    if u.static() and u.count(0) == 0:
                        for ahead in range(3):
                            load(Unit(0, ahead))
                    if u.back(-3).valid(DENSE):
                        load(u.back(-3))
                    if u.off % 2 == 1:
                        if u.edge(0).valid(UNITS):
                            load_attributes(u.edge(0))
                        if u.edge(2).valid(UNITS):
                            store_logits(u.edge(2))
                    if u.back(5).valid(DENSE):
                        store(u.back(5))

                slots(sp, DENSE, 6, slot, ahead=4)
                for b in range(2):
                    sp.wait_ge(stored[b], 32 * (DENSE // 2))
                    sp.wait_ge(l_stored[b], 16 * (UNITS // 2))

            @block.gpsimd
            def _(pool):
                def stage_sources(e):
                    if e.valid(UNITS):
                        atleast(pool, gathered[e.off % 2], e.halves(0) * 128)
                        nc.gpsimd.tensor_copy(stage[e.off % 2][:, 0:4], gix[:, bass.ds(e.count(0) * 8, 4)])\
                            .then_inc(sources_staged, 1)

                def stage_targets(e):
                    nc.gpsimd.tensor_copy(stage[e.off % 2][:, 4:8], gix[:, bass.ds(e.count(0) * 8 + 4, 4)])\
                        .then_inc(targets_staged, 1)

                def gather(e, js):
                    a = e.off % 2
                    for j in js:
                        pool.indirect_dma_start(
                            out=pairs[a][:, j % 4, F * (j // 4):F * (j // 4) + F], out_offset=None, in_=x,
                            in_offset=bass.IndirectOffsetOnAxis(ap=stage[a][:, j:j + 1], axis=0))\
                            .then_inc(gathered[a], 16)

                def edge_unit(e):
                    atleast(pool, pair_turned, e.count(-1))
                    pool.wait_ge(sources_staged, e.count(1))
                    stage_targets(e)
                    gather(e, range(4))
                    pool.wait_ge(targets_staged, e.count(1))
                    stage_sources(e.next())
                    gather(e, range(4, 8))

                def slot(u):
                    if u.static() and u.count(0) == 0:
                        stage_sources(EdgeUnit(0, 0))
                    if u.off % 2 == 1 and u.edge(0).valid(UNITS):
                        edge_unit(u.edge(0))

                slots(pool, DENSE, 6, slot)

            @block.tensor
            def _(pe):
                def turn_rows(u):
                    pe.wait_ge(x_loaded[u.off % 4], u.quarters(1) * 16)
                    atleast(pe, x_copied, u.count(0))
                    for j in range(4):
                        last = nc.tensor.transpose(pT[:, j * 128:(j + 1) * 128],
                                                   rows[u.off % 4][:, j * 128:(j + 1) * 128], ident)
                    last.then_inc(xt_made, 1)

                def project(u):
                    pe.wait_ge(x_copied, u.count(1))
                    atleast(pe, e_made, u.count(0))
                    nc.tensor.matmul(pP[:, :], Mblk[:, :], xT[u.off % 4][:, :], start=True, stop=True).then_inc(p_made, 1)

                def centre(u):
                    pe.wait_ge(h_made, u.count(1))
                    atleast(pe, sq_made, u.count(0))
                    nc.tensor.matmul(pH[:, :], Cm, hb[u.off % 2][:, :], start=True, stop=True).then_inc(hc_made, 1)

                def variance(u):
                    b = u.off % 2
                    pe.wait_ge(sq_made, u.count(1))
                    atleast(pe, v1_made, u.count(0))
                    for j in range(4):
                        last = nc.tensor.matmul(pR[:, 2 * j:2 * j + 2], sq[b][:, j * 128:(j + 1) * 128], c128("ind"),
                                                start=True, stop=True)
                    last.then_inc(var_made, 1)

                def to_rows(u):
                    b = u.off % 2
                    atleast(pe, scaled, u.count(-1))
                    for j in range(4):
                        c = slice(j * 128, (j + 1) * 128)
                        nc.tensor.matmul(pG[b][:, c], hc[b][:, c], CG[:, :], start=True, stop=True)

                def x_to_rows(u):
                    atleast(pe, y_made, u.count(0))
                    for j in range(4):
                        c = slice(j * 128, (j + 1) * 128)
                        last = nc.tensor.matmul(pX[:, c], xT[u.off % 4][:, c], Cm, start=True, stop=True)
                    last.then_inc(g_rows_made, 1)

                def turn_pairs(e):
                    a = e.off % 2
                    pe.wait_ge(gathered[a], e.halves(1) * 128)
                    atleast(pe, l_copied, e.count(0))
                    for j in range(4):
                        last = nc.tensor.transpose(pA[:, j * 128:(j + 1) * 128], pairs[a][:, j, :], ident)
                    last.then_inc(pair_turned, 1)

                def logits(e):
                    a = e.off % 2
                    pe.wait_ge(pair_copied, e.count(1))
                    pe.wait_ge(ea_loaded[a], e.halves(1) * 16)
                    nc.tensor.matmul(pA[0:CH, :], Wal[:, :], XT[:, bass.ds(e.count(0) * COLS, COLS)],
                                     start=True, stop=False)
                    nc.tensor.matmul(pA[0:CH, :], WalE[:, :], eab[a][:, :], start=False, stop=True).then_inc(l_made, 1)

                def slot(u):
                    if u.valid(DENSE):
                        turn_rows(u)
                    if u.back(2).valid(DENSE):
                        variance(u.back(2))
                        to_rows(u.back(2))
                    if u.valid(DENSE):
                        project(u)
                    if u.back(1).valid(DENSE):
                        centre(u.back(1))
                    if u.back(2).valid(DENSE):
                        x_to_rows(u.back(2))
                    if u.off % 2 == 1 and u.edge(1).valid(UNITS):
                        turn_pairs(u.edge(1))
                    if u.off % 2 == 0 and u.edge(1).valid(UNITS):
                        logits(u.edge(1))

                slots(pe, DENSE, 6, slot)

            @block.scalar
            def _(act):
                def copy_x(u):
                    act.wait_ge(xt_made, u.count(1))
                    atleast(act, g_rows_made, u.count(-3))
                    nc.scalar.activation(xT[u.off % 4][:, :], pT[:, :], ACT.Identity, bias=c128("beta")).then_inc(x_copied, 1)

                def elu_parts(u):
                    b = u.off % 2
                    act.wait_ge(p_made, u.count(1))
                    atleast(act, g_made, u.count(-1))
                    nc.scalar.activation(ex[b][:, :], pP[:, :], ACT.Exp, bias=c0x[:, :])
                    nc.scalar.activation(rl[b][:, :], pP[:, :], ACT.Relu, bias=c0x[:, :]).then_inc(e_made, 1)

                def square(u):
                    b = u.off % 2
                    act.wait_ge(hc_made, u.count(1))
                    atleast(act, g_rows_made, u.count(-1))
                    nc.scalar.activation(sq[b][:, :], pH[:, :], ACT.Square, bias=ncbeta[:, :])
                    nc.scalar.activation(hc[b][:, :], pH[:, :], ACT.Identity, bias=ncbeta[:, :]).then_inc(sq_made, 1)

                def square_y(u):
                    b = u.off % 2
                    act.wait_ge(y_made, u.count(1))
                    atleast(act, y_summed, u.count(-1))
                    nc.scalar.activation(q2[b][:, :, :], yc[u.off % 4][:, :, :], ACT.Square, scale=F ** -0.5).then_inc(y_squared, 1)

                def copy_pairs(e):
                    act.wait_ge(pair_turned, e.count(1))
                    nc.scalar.activation(XT[:, bass.ds(e.count(0) * COLS, COLS)], pA[:, :], ACT.Copy).then_inc(pair_copied, 1)

                def copy_logits(e):
                    a = e.off % 2
                    act.wait_ge(l_made, e.count(1))
                    atleast(act, l_stored[a], e.halves(0) * 16)
                    nc.scalar.activation(lrow[a][:, :], pA[0:CH, :], ACT.Copy).then_inc(l_copied, 1)

                def slot(u):
                    if u.valid(DENSE):
                        copy_x(u)
                    if u.back(3).valid(DENSE):
                        square_y(u.back(3))
                    if u.valid(DENSE):
                        elu_parts(u)
                    if u.back(1).valid(DENSE):
                        square(u.back(1))
                    if u.off % 2 == 1 and u.edge(1).valid(UNITS):
                        copy_pairs(u.edge(1))
                    if u.off % 2 == 0 and u.edge(1).valid(UNITS):
                        copy_logits(u.edge(1))

                slots(act, DENSE, 6, slot)

            @block.vector
            def _(dve):
                def elu(u):
                    b = u.off % 2
                    dve.wait_ge(e_made, u.count(1))
                    atleast(dve, h_made, u.count(0))
                    nc.vector.scalar_tensor_tensor(gb[:, :], ex[b][:, :], 1.0, rl[b][:, :], ALU.min, ALU.add).then_inc(g_made, 1)

                def residual(u):
                    b = u.off % 2
                    atleast(dve, hc_made, u.count(-1))
                    dve.wait_ge(g_made, u.count(1))
                    nc.vector.tensor_tensor(hb[b][:, :], gb[:, :], xT[u.off % 4][:, :], ALU.add).then_inc(h_made, 1)

                def add_eps(u):
                    dve.wait_ge(var_made, u.count(1))
                    atleast(dve, roots_made, u.count(0))
                    nc.vector.tensor_scalar(v[:, 0:8], pR[:, 0:8], EPS, None, ALU.add).then_inc(v1_made, 1)

                def root(u, k):
                    if k == 1:
                        if u.valid(DENSE):
                            dve.wait_ge(v1_made, u.count(1))
                        atleast(dve, v2_made, u.count(-1))
                    if k == ROOT_STEPS:
                        atleast(dve, out_made, u.count(-2) if u.valid(DENSE) else min(u.count(-2), DENSE))
                        atleast(dve, scaled, u.count(0) if u.valid(DENSE) else DENSE)
                    root_step(nc, dve, k, v[:, :], w[:, :], ta[:, :], tb[:, :], root_steps, u.count(0), roots_made)

                def scale(u):
                    b = u.off % 2
                    dve.wait_ge(roots_made, u.count(1))
                    dve.wait_ge(g_rows_made, u.count(1))
                    atleast(dve, y_made, u.count(0))
                    nc.vector.tensor_tensor(yb[:, :, :], pG[b][:, :].rearrange("p (r f) -> p r f", f=F),
                                            w[:, 0:8].unsqueeze(2).to_broadcast([128, 8, F]), ALU.mult).then_inc(scaled, 1)

                def add_scaled(u):
                    dve.wait_ge(scaled, u.count(1))
                    atleast(dve, out_made, u.count(-3))
                    nc.vector.tensor_tensor(yc[u.off % 4][:, :, :], yb[:, :, :], pX[:, :].rearrange("p (r f) -> p r f", f=F),
                                            ALU.add).then_inc(y_made, 1)

                def sum_squares(u):
                    b = u.off % 2
                    dve.wait_ge(y_squared, u.count(1))
                    atleast(dve, v2_made, u.count(0))
                    nc.vector.tensor_reduce(s2[:, :], q2[b][:, :, :], AX.X, ALU.add).then_inc(y_summed, 1)

                def keep_sums(u):
                    dve.wait_ge(y_summed, u.count(1))
                    dve.wait_ge(roots_made, u.count(2))
                    nc.vector.tensor_scalar(v[:, 8:16], s2[:, :], EPS, None, ALU.add)
                    nc.vector.tensor_scalar(v[:, 16:24], s2[:, :], 1.0 + EPS, EPS * EPS, ALU.mult, ALU.add)\
                        .then_inc(v2_made, 1)

                def finish_x1(u):
                    b = u.off % 2
                    dve.wait_ge(roots_made, u.count(3))
                    atleast(dve, stored[b], u.halves(0) * 32)
                    nc.vector.tensor_tensor(xr[b][:, :, :], yc[u.off % 4][:, :, :],
                                            w[:, 8:16].unsqueeze(2).to_broadcast([128, 8, F]), ALU.mult)

                def finish_out(u):
                    nc.vector.tensor_tensor(orow[u.off % 2][:, :, :], yc[u.off % 4][:, :, :],
                                            w[:, 16:24].unsqueeze(2).to_broadcast([128, 8, F]), ALU.mult)\
                        .then_inc(out_made, 1)

                def slot(u):
                    if u.static() and u.count(0) == 0:
                        nc.vector.memset(v[:, :], 1.0).then_inc(v_cleared, 1)
                        dve.wait_ge(v_cleared, 1)
                    has_roots = u.back(2).valid(DENSE + 2)
                    if u.back(1).valid(DENSE):
                        elu(u.back(1))
                    if u.back(2).valid(DENSE):
                        add_eps(u.back(2))
                    if has_roots:
                        root(u.back(2), 1)
                    if u.back(1).valid(DENSE):
                        residual(u.back(1))
                    if has_roots:
                        root(u.back(2), 2)
                    if u.back(5).valid(DENSE):
                        finish_x1(u.back(5))
                    if has_roots:
                        root(u.back(2), 3)
                    if u.back(5).valid(DENSE):
                        finish_out(u.back(5))
                    if has_roots:
                        root(u.back(2), 4)
                    if u.back(3).valid(DENSE):
                        sum_squares(u.back(3))
                    if has_roots:
                        for k in range(5, ROOT_STEPS + 1):
                            root(u.back(2), k)
                    if u.back(2).valid(DENSE):
                        scale(u.back(2))
                    if u.back(3).valid(DENSE):
                        keep_sums(u.back(3))
                    if u.back(2).valid(DENSE):
                        add_scaled(u.back(2))

                slots(dve, DENSE, 6, slot)

        last_rows = sb("last_rows", [128, TILES], i32)
        first_rows = sb("first_rows", [128, TILES], i32)
        firsts = sb("firsts", [128, TILES])
        with ExitStack() as ph:
            sbp, semp = places(ph, "weigh")

            ids = sbp("ids", [QR, 3, 2, 128], i32)
            idf = sbp("idf", [QR, 3, 2, 128])
            rid = sbp("rid", [128, 3, TILES], i32)
            rif = sbp("rif", [128, 4, TILES])
            lg = sbp("lg", [QR, 2, CH, 128])
            goes_on = sbp("goes_on", [QR, 2, 128])
            lasts = sbp("lasts", [QR, 2, 128])
            stays = sbp("stays", [QR, 2, 128])
            drop = sbp("drop", [QR, 2, 128])
            narrow = sbp("narrow", [QR, 3, 2, 128], bf16)
            val = sbp("val", [QR, 2, 9, 128])
            pre = sbp("pre", [QR, 2, 9, 128])
            tot = sbp("tot", [QR, 2, 9, 128])
            loop = sbp("loop", [QR, 2, 4, 128])
            tmp = sbp("tmp", [QR, 2, 4, 128])
            peak = sbp("peak", [QR, 2, 4, 128])
            weight, rest = tot[:, :, 0:8, :], pre[:, :, 0:8, :]
            part = sbp("part", [QR, 3, 2, 8, 128], bf16)
            keep = sbp("keep", [QR, 4, 2])
            ends = sbp("ends", [QR, 2, 2, 9])
            rowT = sbp("rowT", [9, 2, 2, 2 * QR])
            chain = sbp("chain", [9, 2, 2 * QR + 1])
            carry = sbp("carry", [QR, 2, 9])

            ids_loaded, masks_made = semp("ids_loaded"), semp("masks_made")
            loaded, ends_made, turned, chained, back, stepped, weights_done, exps_asked, exps_made, saved = (
                semp(n) for n in ("loaded", "ends_made", "turned", "chained", "back", "stepped", "weights_done",
                                  "exps_asked", "exps_made", "saved"))
            ROUNDS = [(0, 9, True, 4), (0, 9, False, 0), (0, 4, True, 0), (0, 4, False, 0)]
            block = ph.enter_context(nc.Block())

            @block.sync
            def _(sp):
                sp.dma_start(ids[:, :, :, :].rearrange("q a h j -> q (a h j)"), dblk).then_inc(ids_loaded, 16)
                sp.dma_start(rid[:, :, :].rearrange("p a t -> p (a t)"), drow).then_inc(ids_loaded, 16)
                for h in range(2):
                    sp.dma_start(lg[:, h, :, :],
                                 logit_rows[:, h * QR * 128:(h + 1) * QR * 128].rearrange("c (q j) -> q c j", j=128))\
                        .then_inc(loaded, 16)
                sp.wait_ge(masks_made, 1)
                for h in range(2):
                    for a in range(3):
                        sp.dma_start(mask_rows[a, h * QR * 128:(h + 1) * QR * 128].rearrange("(q j) -> q j", j=128),
                                     narrow[:, a, h, :]).then_inc(saved, 16)
                sp.wait_ge(weights_done, 1)
                for h in range(2):
                    span = slice(h * QR * 128, (h + 1) * QR * 128)
                    for a in range(3):
                        sp.dma_start(weight_rows[8 * a:8 * a + 8, span].rearrange("c (q j) -> q c j", j=128),
                                     part[:, a, h, :, :]).then_inc(saved, 16)
                sp.wait_ge(saved, 16 * 12)

            @block.tensor
            def _(pe):
                for n, (c0_, c1_, forward, maxima) in enumerate(ROUNDS):
                    groups = [(c0_, maxima), (maxima, c1_)] if maxima else [(c0_, c1_)]
                    pe.wait_ge(ends_made, n + 1)
                    for g, (a, b) in enumerate(groups):
                        for k in range(2):
                            for h in range(2):
                                last = nc.tensor.transpose(bank[2 * g + k][0:b - a, h * QR:(h + 1) * QR],
                                                           ends[:, k, h, a:b], ident[0:QR, 0:QR])
                    last.then_inc(turned, 1)
                    pe.wait_ge(chained, n + 1)
                    for g, (a, b) in enumerate(groups):
                        for h in range(2):
                            first = h * QR + (0 if forward else 1)
                            last = nc.tensor.transpose(bank[4 + h][0:QR, a:b], chain[0:b - a, g, first:first + QR],
                                                       ident[0:b - a, 0:b - a])
                    last.then_inc(back, 1)

            @block.scalar
            def _(act):
                act.wait_ge(exps_asked, 1)
                nc.scalar.activation(val[:, :, 0:4, :], peak[:, :, :, :], ACT.Exp)
                nc.scalar.activation(loop[:, :, :, :], tmp[:, :, :, :], ACT.Exp).then_inc(exps_made, 1)

            @block.vector
            def _(dve):
                count = [0]

                def step(ins):
                    count[0] += 1
                    ins.then_inc(stepped, 1)
                    dve.wait_ge(stepped, count[0])

                def spread(t, n):
                    return t.unsqueeze(2).to_broadcast([QR, 2, n, 128])

                def scans(n, out_, from_, initial):
                    c0_, c1_, forward, maxima = ROUNDS[n]
                    for h in range(2):
                        for c in range(c0_, c1_):
                            o, f = out_[:, h, c, :], from_[:, h, c, :]
                            if forward and c < maxima:
                                last = nc.vector.tensor_tensor_scan(o, drop[:, h, :], f, initial(h, c), ALU.add, ALU.max)
                            elif forward:
                                last = nc.vector.tensor_tensor_scan(o, goes_on[:, h, :], f, initial(h, c), ALU.mult, ALU.add)
                            else:
                                last = nc.vector.tensor_tensor_scan(o[:, ::-1], stays[:, h, ::-1], f[:, ::-1],
                                                                    initial(h, c), ALU.mult, ALU.add)
                    return last

                def segment_scan(n, out_, from_):
                    c0_, c1_, forward, maxima = ROUNDS[n]
                    step(scans(n, out_, from_, lambda h, c: -BIG if forward and c < maxima else 0.0))
                    edge = 127 if forward else 0
                    nc.vector.tensor_copy(ends[:, 0, :, c0_:c1_], out_[:, :, c0_:c1_, edge])
                    if maxima:
                        nc.vector.tensor_copy(ends[:, 1, :, 0:maxima], keep[:, 2, :].unsqueeze(2).to_broadcast([QR, 2, maxima]))
                    nc.vector.tensor_copy(ends[:, 1, :, maxima:c1_],
                                          keep[:, 0 if forward else 1, :].unsqueeze(2).to_broadcast([QR, 2, c1_ - maxima]))\
                        .then_inc(ends_made, 1)
                    groups = [(c0_, maxima), (maxima, c1_)] if maxima else [(c0_, c1_)]
                    dve.wait_ge(turned, n + 1)
                    for g, (a, b) in enumerate(groups):
                        for k in range(2):
                            last = nc.vector.tensor_copy(rowT[0:b - a, g, k, :], bank[2 * g + k][0:b - a, 0:2 * QR])
                        start = -BIG if maxima and g == 0 else 0.0
                        first = 0 if forward else 2 * QR
                        last = nc.vector.memset(chain[0:b - a, g, first:first + 1], start)
                    step(last)
                    for g, (a, b) in enumerate(groups):
                        m = b - a
                        start = -BIG if maxima and g == 0 else 0.0
                        if forward:
                            ops = (ALU.add, ALU.max) if maxima and g == 0 else (ALU.mult, ALU.add)
                            last = nc.vector.tensor_tensor_scan(chain[0:m, g, 1:], rowT[0:m, g, 1, :], rowT[0:m, g, 0, :],
                                                                start, *ops)
                        else:
                            o = chain[0:m, g, 0:2 * QR]
                            last = nc.vector.tensor_tensor_scan(o[:, ::-1], rowT[0:m, g, 1, ::-1], rowT[0:m, g, 0, ::-1],
                                                                start, ALU.mult, ALU.add)
                    last.then_inc(chained, 1)
                    dve.wait_ge(back, n + 1)
                    for h in range(2):
                        last = nc.vector.tensor_copy(carry[:, h, c0_:c1_], bank[4 + h][0:QR, c0_:c1_])
                    step(last)
                    step(scans(n, out_, from_, lambda h, c: carry[:, h, c:c + 1]))

                dve.wait_ge(ids_loaded, 32)
                nc.vector.tensor_copy(rif[:, 0:3, :], rid[:, :, :])
                step(nc.vector.tensor_copy(idf[:, :, :, :], ids[:, :, :, :]))
                nc.vector.tensor_tensor(goes_on[:, :, :], idf[:, 0, :, :], idf[:, 1, :, :], ALU.is_equal)
                nc.vector.tensor_tensor(lasts[:, :, :], idf[:, 1, :, :], idf[:, 2, :, :], ALU.not_equal)
                nc.vector.tensor_tensor(stays[:, :, :], idf[:, 1, :, :], idf[:, 2, :, :], ALU.is_equal)
                nc.vector.tensor_tensor(firsts[:, :], rif[:, 0, :], rif[:, 2, :], ALU.not_equal)
                nc.vector.tensor_tensor(rif[:, 3, :], rif[:, 0, :], rif[:, 2, :], ALU.is_equal)
                step(nc.vector.tensor_tensor(rif[:, 1, :], rif[:, 0, :], rif[:, 1, :], ALU.is_equal))
                nc.vector.tensor_scalar(drop[:, :, :], goes_on[:, :, :], 1.0, BIG, ALU.subtract, ALU.mult)
                nc.vector.tensor_copy(narrow[:, 0, :, :], goes_on[:, :, :])
                nc.vector.tensor_copy(narrow[:, 2, :, :], stays[:, :, :])
                nc.vector.tensor_reduce(keep[:, 0, :], goes_on[:, :, :], AX.X, ALU.min)
                nc.vector.tensor_reduce(keep[:, 1, :], stays[:, :, :], AX.X, ALU.min)
                nc.vector.scalar_tensor_tensor(rif[:, 3, :], rif[:, 3, :], SKIP, rif[:, 0, :], ALU.mult, ALU.max)
                step(nc.vector.scalar_tensor_tensor(rif[:, 1, :], rif[:, 1, :], SKIP, rif[:, 0, :], ALU.mult, ALU.max))
                nc.vector.tensor_copy(last_rows[:, :], rif[:, 1, :])
                nc.vector.tensor_copy(first_rows[:, :], rif[:, 3, :])
                nc.vector.tensor_copy(narrow[:, 1, :, :], drop[:, :, :]).then_inc(masks_made, 1)
                nc.vector.tensor_scalar(keep[:, 2, :], keep[:, 0, :], 1.0, BIG, ALU.subtract, ALU.mult)
                dve.wait_ge(loaded, 32)
                nc.vector.scalar_tensor_tensor(val[:, :, 0:4, :], lg[:, :, 0:4, :], 0.2, lg[:, :, 0:4, :], ALU.mult, ALU.max)
                nc.vector.tensor_copy(val[:, :, 4:8, :], lg[:, :, 4:8, :])
                step(nc.vector.memset(val[:, :, 8, :], 1.0))
                segment_scan(0, pre, val)
                step(nc.vector.tensor_tensor(pre[:, :, :, :], pre[:, :, :, :], spread(lasts[:, :, :], 9), ALU.mult))
                segment_scan(1, tot, pre)
                step(nc.vector.reciprocal(tot[:, :, 8, :], tot[:, :, 8, :]))
                step(nc.vector.tensor_tensor(loop[:, :, :, :], tot[:, :, 4:8, :], spread(tot[:, :, 8, :], 4), ALU.mult))
                step(nc.vector.tensor_tensor(tmp[:, :, :, :], loop[:, :, :, :], lg[:, :, 8:12, :], ALU.add))
                step(nc.vector.scalar_tensor_tensor(loop[:, :, :, :], tmp[:, :, :, :], 0.2, tmp[:, :, :, :], ALU.mult, ALU.max))
                step(nc.vector.tensor_tensor(rest[:, :, 0:4, :], loop[:, :, :, :], tot[:, :, 0:4, :], ALU.max))
                nc.vector.tensor_tensor(peak[:, :, :, :], val[:, :, 0:4, :], rest[:, :, 0:4, :], ALU.subtract)
                nc.vector.tensor_tensor(tmp[:, :, :, :], loop[:, :, :, :], rest[:, :, 0:4, :], ALU.subtract)\
                    .then_inc(exps_asked, 1)
                dve.wait_ge(exps_made, 1)
                segment_scan(2, pre, val)
                step(nc.vector.tensor_tensor(pre[:, :, 0:4, :], pre[:, :, 0:4, :], spread(lasts[:, :, :], 4), ALU.mult))
                segment_scan(3, tot, pre)
                step(nc.vector.tensor_tensor(peak[:, :, :, :], tot[:, :, 0:4, :], loop[:, :, :, :], ALU.add))
                step(nc.vector.reciprocal(tmp[:, :, :, :], peak[:, :, :, :]))
                nc.vector.tensor_tensor(weight[:, :, 0:4, :], val[:, :, 0:4, :], tmp[:, :, :, :], ALU.mult)
                step(nc.vector.tensor_tensor(peak[:, :, :, :], loop[:, :, :, :], tmp[:, :, :, :], ALU.mult))
                step(nc.vector.tensor_tensor(weight[:, :, 4:8, :], peak[:, :, :, :], spread(lasts[:, :, :], 4), ALU.mult))
                step(nc.vector.tensor_copy(part[:, 0, :, :, :], weight[:, :, :, :]))
                step(nc.vector.tensor_tensor(rest[:, :, :, :], weight[:, :, :, :], part[:, 0, :, :, :], ALU.subtract))
                step(nc.vector.tensor_copy(part[:, 1, :, :, :], rest[:, :, :, :]))
                step(nc.vector.tensor_tensor(weight[:, :, :, :], rest[:, :, :, :], part[:, 1, :, :, :], ALU.subtract))
                nc.vector.tensor_copy(part[:, 2, :, :, :], weight[:, :, :, :]).then_inc(weights_done, 1)

        with ExitStack() as ph:
            sbp, semp = places(ph, "first")

            wt = [sbp(f"wt{i}", [24, 2 * COLS], bf16) for i in range(2)]
            mask = [sbp(f"mask{i}", [128, COLS], bf16) for i in range(2)]
            zb = [sbp(f"zb{i}", [128, COLS]) for i in range(4)]
            ys = [sbp(f"ys{i}", [128, COLS]) for i in range(2)]
            start = sbp("start", [128, 1])
            xd = [sbp(f"xd{i}", [128, COLS]) for i in range(4)]
            ex, rl, gb, hb, sq, hc = (sbp(n, [128, COLS]) for n in ("ex", "rl", "gb", "hb", "sq", "hc"))
            yb, q2 = sbp("yb", [128, 8, F]), sbp("q2", [128, 8, F])
            yc = [sbp(f"yc{i}", [128, 8, F]) for i in range(2)]
            xr = [sbp(f"xr{i}", [128, 8, F]) for i in range(2)]
            s2 = sbp("s2", [128, 8])
            v, w, ta, tb = (sbp(n, [128, 16]) for n in ("v", "w", "ta", "tb"))
            wf = sbp("wf", [128, 8])
            stage = [sbp(f"stage{i}", [128, 8], i32) for i in range(2)]
            pB, pY, pH, pR, pG = [bank[0], bank[1]], bank[2], bank[4], bank[5], bank[6]
            pC = bank[7]

            w_loaded = [semp(f"w_loaded{i}") for i in range(2)]
            scattered = [semp(f"scattered{i}") for i in range(2)]
            stored = [semp(f"stored{i}") for i in range(2)]
            (spread_made, z_made, z_used, halfway, crossed, summed, xd_copied,
             e_made, g_made, h_made, hc_made, sq_made, var_made, rows_made, v1_made, roots_made, root_steps, scaled,
             yc_made, squared, s_made, v2_made, xr_made, a_staged, b_staged, cleared, flagged) = (semp(n) for n in (
                 "spread_made", "z_made", "z_used", "halfway", "crossed", "summed",
                 "xd_copied", "e_made", "g_made", "h_made", "hc_made", "sq_made", "var_made", "rows_made",
                 "v1_made", "roots_made", "root_steps", "scaled", "yc_made", "squared", "s_made", "v2_made", "xr_made",
                 "a_staged", "b_staged", "cleared", "flagged"))
            block = ph.enter_context(nc.Block())

            def columns(u, s):
                return bass.ds(u.count(0) * (-2 * COLS) + ((PAIRS - 1) * 2 * COLS + s * COLS), COLS)

            @block.sync
            def _(sp):
                def load(u):
                    b = u.off % 2
                    atleast(sp, summed, u.count(-1))
                    sp.dma_start(wt[b][:, :], weight_rows[:, bass.ds(u.count(0) * (-2 * COLS) + (PAIRS - 1) * 2 * COLS, 2 * COLS)])\
                        .then_inc(w_loaded[b], 16)
                    for s in range(2):
                        sp.dma_start(mask[b][64 * s:64 * s + 64, :],
                                     mask_rows[2:3, columns(u, s)].to_broadcast([64, COLS])).then_inc(w_loaded[b], 16)

                def store(u):
                    b = u.off % 2
                    sp.wait_ge(xr_made, u.count(1))
                    for s in range(2):
                        at = bass.ds(u.count(0) * (-8 * F) + ((PAIRS - 1) * 8 * F + s * 4 * F), 4 * F)
                        sp.dma_start(target_rows[:, at].rearrange("p (j f) -> p j f", f=F),
                                     xr[b][:, :, :].rearrange("p (j s) f -> p s j f", s=2)[:, s, :, :]).then_inc(stored[b], 16)

                def slot(u):
                    if u.static() and u.count(0) == 0:
                        load(u)
                    if u.back(-1).valid(PAIRS):
                        load(u.back(-1))
                    if u.back(4).valid(PAIRS):
                        store(u.back(4))

                slots(sp, PAIRS, 5, slot)
                for b in range(2):
                    sp.wait_ge(stored[b], 32 * ((PAIRS + 1 - b) // 2))

            @block.gpsimd
            def _(pool):
                def stage_part(u, s, staged):
                    if not u.valid(PAIRS):
                        return
                    atleast(pool, scattered[u.off % 2], u.halves(0) * 128)
                    nc.gpsimd.tensor_copy(stage[u.off % 2][:, 4 * s:4 * s + 4],
                                          first_rows[:, bass.ds(u.count(0) * -8 + ((PAIRS - 1) * 8 + 4 * s), 4)]).then_inc(staged, 1)

                def scatter(u, s):
                    b = u.off % 2
                    for j in range(4):
                        pool.indirect_dma_start(
                            out=x1, out_offset=bass.IndirectOffsetOnAxis(ap=stage[b][:, 4 * s + j:4 * s + j + 1], axis=0),
                            in_=xr[b][:, 2 * j + s, :], in_offset=None, bounds_check=last_row, oob_is_err=False)\
                            .then_inc(scattered[b], 16)

                last_row = pool.alloc_register("last_row")
                pool.reg_mov(last_row, N - 1)

                def slot(u):
                    if u.static() and u.count(0) == 0:
                        stage_part(u, 0, a_staged)
                    u = u.back(4)
                    if not u.valid(PAIRS):
                        return
                    pool.wait_ge(xr_made, u.count(1))
                    pool.wait_ge(a_staged, u.count(1))
                    stage_part(u, 1, b_staged)
                    scatter(u, 0)
                    pool.wait_ge(b_staged, u.count(1))
                    stage_part(u.back(-1), 0, a_staged)
                    scatter(u, 1)

                slots(pool, PAIRS, 5, slot)
                for b in range(2):
                    pool.wait_ge(scattered[b], 128 * ((PAIRS + 1 - b) // 2))

            @block.tensor
            def _(pe):
                def sums(u, n):
                    b = u.off % 2
                    if n == 0:
                        pe.wait_ge(w_loaded[b], u.halves(1) * 48)
                    if n < 2 * H:
                        s, h = 1 - n // H, n % H
                        atleast(pe, z_made, u.count(0) * (2 * H) + (n - 1))
                        nc.tensor.matmul(pB[n % 2][:, :], headsel[:, h, :], wt[b][:, s * COLS:(s + 1) * COLS],
                                         start=True, stop=True).then_inc(spread_made, 1)
                    if n > 1:
                        s, h = 1 - (n - 2) // H, (n - 2) % H
                        if h == 0:
                            atleast(pe, halfway if s else summed, u.count(0))
                        pe.wait_ge(z_made, u.count(0) * (2 * H) + (n - 1))
                        nc.tensor.matmul(pY[64 * s:64 * s + 64, :], Mstack[:, h, :], zb[(n - 2) % 4][:, :],
                                         start=(h == 0), stop=(h == H - 1)).then_inc(z_used, 1)

                def centre(u):
                    pe.wait_ge(h_made, u.count(1))
                    atleast(pe, sq_made, u.count(0))
                    nc.tensor.matmul(pH[:, :], Cm, hb[:, :], start=True, stop=True).then_inc(hc_made, 1)

                def variance(u):
                    pe.wait_ge(sq_made, u.count(1))
                    atleast(pe, v1_made, u.count(0))
                    for j in range(4):
                        last = nc.tensor.matmul(pR[:, 2 * j:2 * j + 2], sq[:, j * 128:(j + 1) * 128], c128("ind"),
                                                start=True, stop=True)
                    last.then_inc(var_made, 1)

                def to_rows(u, j):
                    if j == 0:
                        atleast(pe, yc_made, u.count(0))
                    c = slice(j * 128, (j + 1) * 128)
                    nc.tensor.matmul(pG[:, c], hc[:, c], CG[:, :], start=True, stop=True)
                    nc.tensor.matmul(pC[:, c], xd[u.off % 4][:, c], Cm, start=True, stop=True).then_inc(rows_made, 1)

                def slot(u):
                    for n in range(2 * H + 2):
                        if u.valid(PAIRS):
                            sums(u, n)
                        if n == 0 and u.back(2).valid(PAIRS):
                            variance(u.back(2))
                        if 1 <= n <= 4 and u.back(2).valid(PAIRS):
                            to_rows(u.back(2), n - 1)
                        if n == 5 and u.back(1).valid(PAIRS):
                            centre(u.back(1))

                slots(pe, PAIRS, 5, slot)

            @block.scalar
            def _(act):
                def copy_targets(u):
                    atleast(act, rows_made, u.count(-3) * 4)
                    nc.scalar.activation(xd[u.off % 4][0:64, :], XT[64:128, columns(u, 0)], ACT.Identity,
                                         bias=c128("beta")[64:128, :])
                    nc.scalar.activation(xd[u.off % 4][64:128, :], XT[64:128, columns(u, 1)], ACT.Identity,
                                         bias=c128("beta")[64:128, :]).then_inc(xd_copied, 1)

                def elu_parts(u):
                    b = u.off % 2
                    act.wait_ge(summed, u.count(1))
                    atleast(act, g_made, u.count(0))
                    nc.scalar.activation(ex[:, :], ys[b][:, :], ACT.Exp, bias=c0[:, :])
                    nc.scalar.activation(rl[:, :], ys[b][:, :], ACT.Relu, bias=c0[:, :]).then_inc(e_made, 1)

                def square(u):
                    act.wait_ge(hc_made, u.count(1))
                    atleast(act, rows_made, u.count(0) * 4)
                    nc.scalar.activation(sq[:, :], pH[:, :], ACT.Square, bias=ncbeta[:, :])
                    nc.scalar.activation(hc[:, :], pH[:, :], ACT.Identity, bias=ncbeta[:, :]).then_inc(sq_made, 1)

                def square_y(u):
                    act.wait_ge(yc_made, u.count(1))
                    atleast(act, s_made, u.count(0))
                    nc.scalar.activation(q2[:, :, :], yc[u.off % 2][:, :, :], ACT.Square, scale=F ** -0.5).then_inc(squared, 1)

                def slot(u):
                    if u.back(1).valid(PAIRS):
                        elu_parts(u.back(1))
                    if u.back(3).valid(PAIRS):
                        square_y(u.back(3))
                    if u.valid(PAIRS):
                        copy_targets(u)
                    if u.back(1).valid(PAIRS):
                        square(u.back(1))

                slots(act, PAIRS, 5, slot)

            @block.vector
            def _(dve):
                def product(u, n):
                    dve.wait_ge(spread_made, u.count(0) * (2 * H) + (n + 1))
                    atleast(dve, z_used, u.count(0) * (2 * H) + (n - 3))
                    nc.vector.tensor_tensor(zb[n % 4][:, :], pB[n % 2][:, :], XT[:, columns(u, 1 - n // H)], ALU.mult)\
                        .then_inc(z_made, 1)

                def scan(u, s):
                    b, half = u.off % 2, slice(64 * s, 64 * s + 64)
                    dve.wait_ge(z_used, u.count(0) * (2 * H) + (2 - s) * H)
                    atleast(dve, e_made, u.count(-1))
                    atleast(dve, crossed, u.count(0) * 2 + (1 - s))
                    nc.vector.tensor_tensor_scan(ys[b][half, ::-1], mask[b][half, ::-1], pY[half, ::-1], start[half, :],
                                                 ALU.mult, ALU.add).then_inc(halfway if s else summed, 1)

                def cross(u, s):
                    b = u.off % 2
                    dve.wait_ge(halfway if s else summed, u.count(1))
                    nc.vector.tensor_copy(start[64 - 64 * s:128 - 64 * s, :], ys[b][64 * s:64 * s + 64, 0:1])\
                        .then_inc(crossed, 1)

                def elu(u):
                    dve.wait_ge(e_made, u.count(1))
                    atleast(dve, h_made, u.count(0))
                    nc.vector.scalar_tensor_tensor(gb[:, :], ex[:, :], 1.0, rl[:, :], ALU.min, ALU.add).then_inc(g_made, 1)

                def residual(u):
                    atleast(dve, hc_made, u.count(0))
                    dve.wait_ge(g_made, u.count(1))
                    dve.wait_ge(xd_copied, u.count(1))
                    nc.vector.tensor_tensor(hb[:, :], gb[:, :], xd[u.off % 4][:, :], ALU.add).then_inc(h_made, 1)

                def add_eps(u):
                    dve.wait_ge(var_made, u.count(1))
                    atleast(dve, roots_made, u.count(0))
                    nc.vector.tensor_scalar(v[:, 0:8], pR[:, 0:8], EPS, None, ALU.add).then_inc(v1_made, 1)

                def sum_squares(u):
                    dve.wait_ge(squared, u.count(1))
                    atleast(dve, v2_made, u.count(0))
                    nc.vector.tensor_reduce(s2[:, :], q2[:, :, :], AX.X, ALU.add).then_inc(s_made, 1)
                    dve.wait_ge(s_made, u.count(1))
                    dve.wait_ge(roots_made, u.count(1))
                    nc.vector.tensor_scalar(v[:, 8:16], s2[:, :], EPS, None, ALU.add).then_inc(v2_made, 1)

                def root(u, k):
                    if k == 1:
                        if u.valid(PAIRS):
                            dve.wait_ge(v1_made, u.count(1))
                        atleast(dve, v2_made, u.count(0))
                    if k == ROOT_STEPS:
                        atleast(dve, flagged, u.count(-1))
                        atleast(dve, scaled, u.count(0))
                    root_step(nc, dve, k, v[:, :], w[:, :], ta[:, :], tb[:, :], root_steps, u.count(0), roots_made)

                def scale(u):
                    dve.wait_ge(roots_made, u.count(1))
                    dve.wait_ge(rows_made, u.count(1) * 4)
                    atleast(dve, yc_made, u.count(0))
                    nc.vector.tensor_tensor(yb[:, :, :], pG[:, :].rearrange("p (r f) -> p r f", f=F),
                                            w[:, 0:8].unsqueeze(2).to_broadcast([128, 8, F]), ALU.mult).then_inc(scaled, 1)

                def add_scaled(u):
                    dve.wait_ge(scaled, u.count(1))
                    atleast(dve, xr_made, u.count(-1))
                    nc.vector.tensor_tensor(yc[u.off % 2][:, :, :], yb[:, :, :], pC[:, :].rearrange("p (r f) -> p r f", f=F),
                                            ALU.add).then_inc(yc_made, 1)

                def finish(u):
                    b = u.off % 2
                    dve.wait_ge(flagged, u.count(1))
                    atleast(dve, scattered[b], u.halves(0) * 128)
                    atleast(dve, stored[b], u.halves(0) * 32)
                    nc.vector.tensor_tensor(xr[b][:, :, :], yc[b][:, :, :],
                                            wf[:, :].unsqueeze(2).to_broadcast([128, 8, F]), ALU.mult).then_inc(xr_made, 1)

                def flag(u):
                    dve.wait_ge(roots_made, u.count(2))
                    atleast(dve, xr_made, u.count(0))
                    at = bass.ds(u.count(0) * -8 + (PAIRS - 1) * 8, 8)
                    nc.vector.tensor_tensor(wf[:, :].rearrange("p (j s) -> p s j", s=2),
                                            w[:, 8:16].rearrange("p (j s) -> p s j", s=2),
                                            firsts[:, at].rearrange("p (s j) -> p s j", s=2), ALU.mult).then_inc(flagged, 1)

                def slot(u):
                    if u.static() and u.count(0) == 0:
                        nc.vector.memset(v[:, :], 1.0)
                        nc.vector.memset(start[:, :], 0.0).then_inc(cleared, 1)
                        dve.wait_ge(cleared, 1)
                    has_roots = u.back(2).valid(PAIRS + 1)
                    for n in range(2 * H):
                        if u.valid(PAIRS):
                            product(u, n)
                        if n == 1 and u.back(1).valid(PAIRS):
                            elu(u.back(1))
                        if n == 2 and u.back(1).valid(PAIRS):
                            residual(u.back(1))
                        if n == 3:
                            if u.back(3).valid(PAIRS):
                                sum_squares(u.back(3))
                            if u.back(2).valid(PAIRS):
                                add_eps(u.back(2))
                        if n == 4 and u.valid(PAIRS):
                            scan(u, 1)
                        if n == 5 and u.back(4).valid(PAIRS):
                            finish(u.back(4))
                        if n >= 4 and has_roots:
                            root(u.back(2), 2 * n - 7)
                        if n == 4 and u.valid(PAIRS):
                            cross(u, 1)
                        if n >= 4 and has_roots:
                            root(u.back(2), 2 * n - 6)
                    if u.back(2).valid(PAIRS):
                        scale(u.back(2))
                    if u.back(3).valid(PAIRS):
                        flag(u.back(3))
                    if u.valid(PAIRS):
                        scan(u, 0)
                    if u.back(2).valid(PAIRS):
                        add_scaled(u.back(2))
                    if u.valid(PAIRS):
                        cross(u, 0)

                slots(dve, PAIRS, 5, slot)

        with ExitStack() as dist:
            D = XT[:, 0:PAIRS * COLS]
            with ExitStack() as ph:
                sbp, semp = places(ph, "dist")

                ea = [sbp(f"ea{i}", [7, COLS]) for i in range(2)]
                sq = [sbp(f"sq{i}", [128, 8, F]) for i in range(2)]
                nrm = [sbp(f"nrm{i}", [128, 8, F]) for i in range(2)]
                d1 = sbp("d1", [128, COLS])
                s2 = [sbp(f"s2{i}", [128, 8]) for i in range(2)]
                v, w, ta, tb = (sbp(n, [128, 16]) for n in ("v", "w", "ta", "tb"))
                pL, pT = [[bank[0], bank[1]], [bank[2], bank[3]]], [bank[4], bank[5]]
                ea_in = [semp(f"ea_in{i}") for i in range(2)]
                lin, sqd, smd, vmd, nmd, tnd, gld = ([semp(f"{n}{i}") for i in range(2)] for n in (
                    "linear_made", "squares_made", "squares_summed", "v_made", "normed", "turned", "gelu_made"))
                cleared, root_steps, roots_made = semp("cleared"), semp("root_steps"), semp("roots_made")
                block = ph.enter_context(nc.Block())

                @block.sync
                def _(sp):
                    def slot(u):
                        if not u.valid(PAIRS):
                            return
                        atleast(sp, lin[0], u.count(-1))
                        sp.dma_start(ea[u.off % 2][:, :], ea3[:, bass.ds(u.count(0) * COLS, COLS)])\
                            .then_inc(ea_in[u.off % 2], 16)

                    slots(sp, PAIRS, 3, slot)

                @block.tensor
                def _(pe):
                    def first(u):
                        b = u.off % 2
                        pe.wait_ge(ea_in[b], u.halves(1) * 16)
                        atleast(pe, nmd[0], u.count(-1))
                        for j in range(4):
                            c = slice(j * 128, (j + 1) * 128)
                            last = nc.tensor.matmul(pL[0][b][:, c], ea[b][:, c], Wd1[:, :], start=True, stop=True)
                        last.then_inc(lin[0], 1)

                    def second(u):
                        b = u.off % 2
                        pe.wait_ge(gld[0], u.count(1))
                        atleast(pe, nmd[1], u.count(-1))
                        nc.tensor.matmul(pL[1][b][:, :], ones[:, :], b2parts[:, :, :].rearrange("k j m -> k (j m)"),
                                         start=True, stop=False)
                        for j in range(4):
                            c = slice(j * 128, (j + 1) * 128)
                            last = nc.tensor.matmul(pL[1][b][:, c], d1[:, c], Wd2[:, :], start=False, stop=(j == 3))
                        last.then_inc(lin[1], 1)

                    def turn(n, u):
                        pe.wait_ge(nmd[n], u.count(1))
                        atleast(pe, gld[n], u.count(0))
                        for j in range(4):
                            last = nc.tensor.transpose(
                                pT[n][:, j * 128:(j + 1) * 128],
                                nrm[n][:, 2 * j:2 * j + 2, :].rearrange("p r f -> p (r f)"), ident)
                        last.then_inc(tnd[n], 1)

                    def slot(u):
                        if u.valid(PAIRS):
                            first(u)
                        if u.back(2).valid(PAIRS):
                            second(u.back(2))
                        if u.back(1).valid(PAIRS):
                            turn(0, u.back(1))
                        if u.back(3).valid(PAIRS):
                            turn(1, u.back(3))

                    slots(pe, PAIRS, 3, slot)

                @block.scalar
                def _(act):
                    def square(n, u):
                        act.wait_ge(lin[n], u.count(1))
                        atleast(act, smd[n], u.count(0))
                        nc.scalar.activation(sq[n][:, :, :], pL[n][u.off % 2][:, :].rearrange("p (r f) -> p r f", f=F),
                                             ACT.Square, scale=F ** -0.5).then_inc(sqd[n], 1)

                    def gelu(n, u):
                        act.wait_ge(tnd[n], u.count(1))
                        if n == 0:
                            atleast(act, lin[1], u.count(0))
                            nc.scalar.activation(d1[:, :], pT[0][:, :], ACT.Gelu, bias=c128("b1"), scale=c128("g1"))\
                                .then_inc(gld[0], 1)
                        else:
                            nc.scalar.activation(D[:, bass.ds(u.count(0) * COLS, COLS)], pT[1][:, :], ACT.Gelu,
                                                 bias=c128("b2"), scale=c128("g2")).then_inc(gld[1], 1)

                    def slot(u):
                        if u.valid(PAIRS):
                            square(0, u)
                        if u.back(2).valid(PAIRS):
                            square(1, u.back(2))
                        if u.back(1).valid(PAIRS):
                            gelu(0, u.back(1))
                        if u.back(3).valid(PAIRS):
                            gelu(1, u.back(3))

                    slots(act, PAIRS, 3, slot)

                @block.vector
                def _(dve):
                    def sum_squares(n, u):
                        dve.wait_ge(sqd[n], u.count(1))
                        atleast(dve, vmd[n], u.count(0))
                        nc.vector.tensor_reduce(s2[n][:, :], sq[n][:, :, :], AX.X, ALU.add).then_inc(smd[n], 1)

                    def add_eps(n, u):
                        dve.wait_ge(smd[n], u.count(1))
                        atleast(dve, roots_made, u.count(2 * n))
                        nc.vector.tensor_scalar(v[:, 8 * n:8 * n + 8], s2[n][:, :], EPS, None, ALU.add).then_inc(vmd[n], 1)

                    def root(u, k):
                        if k == 1:
                            if u.valid(PAIRS):
                                dve.wait_ge(vmd[0], u.count(1))
                            atleast(dve, vmd[1], u.count(-1))
                        if k == ROOT_STEPS:
                            atleast(dve, nmd[0], u.count(0) if u.valid(PAIRS) else PAIRS)
                            atleast(dve, nmd[1], u.count(-2))
                        root_step(nc, dve, k, v[:, :], w[:, :], ta[:, :], tb[:, :], root_steps, u.count(0), roots_made)

                    def norm(n, u):
                        dve.wait_ge(roots_made, u.count(1 + 2 * n))
                        atleast(dve, tnd[n], u.count(0))
                        nc.vector.tensor_tensor(nrm[n][:, :, :], pL[n][u.off % 2][:, :].rearrange("p (r f) -> p r f", f=F),
                                                w[:, 8 * n:8 * n + 8].unsqueeze(2).to_broadcast([128, 8, F]), ALU.mult)\
                            .then_inc(nmd[n], 1)

                    def slot(u):
                        if u.static() and u.count(0) == 0:
                            nc.vector.memset(v[:, :], 1.0).then_inc(cleared, 1)
                            dve.wait_ge(cleared, 1)
                        for k in range(1, ROOT_STEPS + 1):
                            if u.back(1).valid(PAIRS + 2):
                                root(u.back(1), k)
                        if u.back(1).valid(PAIRS):
                            norm(0, u.back(1))
                        if u.back(3).valid(PAIRS):
                            norm(1, u.back(3))
                        if u.valid(PAIRS):
                            sum_squares(0, u)
                        if u.back(2).valid(PAIRS):
                            sum_squares(1, u.back(2))
                        if u.valid(PAIRS):
                            add_eps(0, u)
                        if u.back(2).valid(PAIRS):
                            add_eps(1, u.back(2))

                    slots(dve, PAIRS, 3, slot)

            with ExitStack() as ph:
                sbp, semp = places(ph, "second")

                stage = [sbp(f"stage{i}", [128, 8], i32) for i in range(2)]
                pairs = [sbp(f"pairs{i}", [128, 4, 2 * F]) for i in range(2)]
                mask = [sbp(f"mask{i}", [128, COLS], bf16) for i in range(2)]
                goes = [sbp(f"goes{i}", [128, COLS], bf16) for i in range(2)]
                xe = [sbp(f"xe{i}", [128, COLS]) for i in range(2)]
                top = [sbp(f"top{i}", [128, COLS + 1]) for i in range(2)]
                below = sbp("below", [128, COLS])
                decay = [sbp(f"decay{i}", [128, COLS]) for i in range(2)]
                term = [sbp(f"term{i}", [128, COLS]) for i in range(2)]
                sums = [sbp(f"sums{i}", [128, COLS]) for i in range(2)]
                inv, quo = sbp("inv", [128, 4, F]), sbp("quo", [128, 4, F])
                res, sqr = sbp("res", [128, 4, F]), sbp("sqr", [128, 4, F])
                cen = [sbp(f"cen{i}", [128, 4, F]) for i in range(2)]
                orow = [sbp(f"orow{i}", [128, 4, F]) for i in range(2)]
                mean, nmean, s2 = sbp("mean", [128, 4]), sbp("nmean", [128, 4]), sbp("s2", [128, 4])
                v, w, ta, tb = (sbp(n, [128, 4]) for n in ("v", "w", "ta", "tb"))
                pA, pL, pW, pS, pF, pD = bank[0], [bank[1], bank[2]], [bank[3], bank[4]], bank[5], bank[6], bank[7]

                gathered = [semp(f"gathered{i}") for i in range(2)]
                scattered = [semp(f"scattered{i}") for i in range(2)]
                mask_in = [semp(f"mask_in{i}") for i in range(2)]
                targets_in = [semp(f"targets_in{i}") for i in range(2)]
                (s_staged, o_staged, turned, copied, held, linear, topped, carried, fell_made, below_made,
                 exps_made, term_made, summed, rows_made, inv_made, quo_made, res_made, mean_made, nmean_made, cen_made,
                 sqr_made, s2_made, v_made, root_steps, roots_made, out_made, cleared) = (semp(n) for n in (
                     "s_staged", "o_staged", "turned", "copied", "held", "linear", "topped", "carried",
                     "fell_made", "below_made", "exps_made", "term_made", "summed", "rows_made", "inv_made", "quo_made",
                     "res_made", "mean_made", "nmean_made", "cen_made", "sqr_made", "s2_made", "v_made", "root_steps",
                     "roots_made", "out_made", "cleared"))
                block = ph.enter_context(nc.Block())

                @block.sync
                def _(sp):
                    def slot(u):
                        if not u.valid(UNITS):
                            return
                        b = u.off % 2
                        atleast(sp, turned, u.count(-1))
                        sp.dma_start(pairs[u.off % 2][:, :, F:2 * F],
                                     target_rows[:, bass.ds(u.count(0) * (4 * F), 4 * F)].rearrange("p (j f) -> p j f", f=F))\
                            .then_inc(targets_in[b], 16)
                        atleast(sp, fell_made, u.count(-1))
                        sp.dma_start(mask[b][:, :], mask_rows[1:2, bass.ds(u.count(0) * COLS, COLS)].to_broadcast([128, COLS]))\
                            .then_inc(mask_in[b], 16)
                        sp.dma_start(goes[b][64:128, :], mask_rows[0:1, bass.ds(u.count(0) * COLS, COLS)].to_broadcast([64, COLS]))\
                            .then_inc(mask_in[b], 16)

                    slots(sp, UNITS, 1, slot)

                @block.gpsimd
                def _(pool):
                    last_row = pool.alloc_register("last_out_row")
                    pool.reg_mov(last_row, N - 1)

                    def stage_gather(u):
                        if u.valid(UNITS):
                            atleast(pool, gathered[u.off % 2], u.halves(0) * 64)
                            nc.gpsimd.tensor_copy(stage[u.off % 2][:, 0:4], gix[:, bass.ds(u.count(0) * 8, 4)])\
                                .then_inc(s_staged, 1)

                    def stage_scatter(u):
                        if u.valid(UNITS):
                            atleast(pool, scattered[u.off % 2], u.halves(0) * 64)
                            nc.gpsimd.tensor_copy(stage[u.off % 2][:, 4:8], last_rows[:, bass.ds(u.count(0) * 4, 4)])\
                                .then_inc(o_staged, 1)

                    def gather(u):
                        a = u.off % 2
                        for j in range(4):
                            pool.indirect_dma_start(
                                out=pairs[u.off % 2][:, j, 0:F], out_offset=None, in_=x1,
                                in_offset=bass.IndirectOffsetOnAxis(ap=stage[a][:, j:j + 1], axis=0))\
                                .then_inc(gathered[a], 16)

                    def scatter(u):
                        a = u.off % 2
                        for j in range(4):
                            pool.indirect_dma_start(
                                out=out, out_offset=bass.IndirectOffsetOnAxis(ap=stage[a][:, 4 + j:5 + j], axis=0),
                                in_=orow[a][:, j, :], in_offset=None, bounds_check=last_row, oob_is_err=False)\
                                .then_inc(scattered[a], 16)

                    def slot(u):
                        o = u.back(5)
                        if u.static() and u.count(0) == 0:
                            stage_gather(u)
                        if u.valid(UNITS):
                            atleast(pool, turned, u.count(-1))
                            pool.wait_ge(s_staged, u.count(1))
                        stage_scatter(o)
                        if u.valid(UNITS):
                            gather(u)
                        if o.valid(UNITS):
                            pool.wait_ge(out_made, o.count(1))
                            pool.wait_ge(o_staged, o.count(1))
                        stage_gather(u.back(-1))
                        if o.valid(UNITS):
                            scatter(o)

                    slots(pool, UNITS, 6, slot, ahead=1)
                    for b in range(2):
                        pool.wait_ge(scattered[b], 64 * (UNITS // 2))

                @block.tensor
                def _(pe):
                    def turn(u):
                        pe.wait_ge(gathered[u.off % 2], u.halves(1) * 64)
                        pe.wait_ge(targets_in[u.off % 2], u.halves(1) * 16)
                        atleast(pe, copied, u.count(0))
                        atleast(pe, held, u.count(0))
                        for j in range(4):
                            last = nc.tensor.transpose(pA[:, j * 128:(j + 1) * 128], pairs[u.off % 2][:, j, :], ident)
                        last.then_inc(turned, 1)

                    def logits(u):
                        b = u.off % 2
                        pe.wait_ge(copied, u.count(1))
                        pe.wait_ge(held, u.count(1))
                        atleast(pe, term_made, u.count(-1))
                        d = D[:, bass.ds(u.halves(0) * COLS, COLS)]
                        sel = c128("dA") if b == 0 else c128("dB")
                        nc.tensor.matmul(pL[b][:, :], c128("Wqq"), xe[b][:, :], start=True, stop=False)
                        nc.tensor.matmul(pL[b][:, :], sel, d, start=False, stop=True)
                        nc.tensor.matmul(pW[b][:, :], c128("Wv"), xe[b][:, :], start=True, stop=False)
                        nc.tensor.matmul(pW[b][:, :], sel, d, start=False, stop=True).then_inc(linear, 1)

                    def falls(u):
                        b = u.off % 2
                        pe.wait_ge(carried, u.count(1))
                        pe.wait_ge(topped, u.count(1))
                        pe.wait_ge(mask_in[b], u.halves(1) * 32)
                        atleast(pe, exps_made, u.count(0))
                        nc.tensor.matmul(pF[:, :], ones[0:1, :], mask[b][0:1, :], start=True, stop=False)
                        nc.tensor.matmul(pF[:, :], ident, top[b][:, 0:COLS], start=False, stop=False)
                        nc.tensor.matmul(pF[:, :], minus[:, :], top[b][:, 1:], start=False, stop=True).then_inc(fell_made, 1)

                    def turn_sums(u):
                        b = u.off % 2
                        pe.wait_ge(summed, u.count(1))
                        atleast(pe, quo_made, u.count(0))
                        for j in range(4):
                            last = nc.tensor.transpose(pS[:, j * 128:(j + 1) * 128], sums[b][:, j * 128:(j + 1) * 128], ident)
                        atleast(pe, res_made, u.count(0))
                        for j in range(4):
                            last = nc.tensor.transpose(pD[:, j * 128:(j + 1) * 128], xe[b][:, j * 128:(j + 1) * 128], ident)
                        last.then_inc(rows_made, 1)

                    def slot(u):
                        if u.valid(UNITS):
                            turn(u)
                        if u.back(1).valid(UNITS):
                            falls(u.back(1))
                        if u.valid(UNITS):
                            logits(u)
                        if u.back(1).valid(UNITS):
                            turn_sums(u.back(1))

                    slots(pe, UNITS, 5, slot)

                @block.scalar
                def _(act):
                    def copy(u):
                        b = u.off % 2
                        act.wait_ge(turned, u.count(1))
                        atleast(act, rows_made, u.count(-1))
                        nc.scalar.activation(xe[b][0:64, :], pA[0:64, :], ACT.Copy).then_inc(copied, 1)

                    def exps(u):
                        b = u.off % 2
                        act.wait_ge(below_made, u.count(1))
                        act.wait_ge(fell_made, u.count(1))
                        atleast(act, summed, u.count(-1))
                        nc.scalar.activation(decay[b][:, :], pF[:, :], ACT.Exp)
                        nc.scalar.activation(term[b][:, :], below[:, :], ACT.Exp).then_inc(exps_made, 1)

                    def square(u):
                        act.wait_ge(cen_made, u.count(1))
                        atleast(act, s2_made, u.count(0))
                        nc.scalar.activation(sqr[:, :, :], cen[u.off % 2][:, :, :], ACT.Square, scale=F ** -0.5).then_inc(sqr_made, 1)

                    def slot(u):
                        if u.valid(UNITS):
                            copy(u)
                        if u.back(1).valid(UNITS):
                            exps(u.back(1))
                        if u.back(2).valid(UNITS):
                            square(u.back(2))

                    slots(act, UNITS, 5, slot)

                @block.vector
                def _(dve):
                    def hold(u):
                        b = u.off % 2
                        dve.wait_ge(turned, u.count(1))
                        dve.wait_ge(mask_in[b], u.halves(1) * 32)
                        atleast(dve, rows_made, u.count(-1))
                        atleast(dve, held, u.count(0))
                        nc.vector.tensor_tensor_scan(xe[b][64:128, :], goes[b][64:128, :], pA[64:128, :],
                                                     xe[1 - b][64:128, COLS - 1:COLS], ALU.mult, ALU.add).then_inc(held, 1)

                    def maxima(u):
                        b = u.off % 2
                        before = top[1 - b][:, COLS:COLS + 1]
                        dve.wait_ge(linear, u.count(1))
                        dve.wait_ge(mask_in[b], u.halves(1) * 32)
                        atleast(dve, topped, u.count(0))
                        atleast(dve, fell_made, u.count(-1))
                        nc.vector.tensor_copy(top[b][:, 0:1], before).then_inc(carried, 1)
                        nc.vector.tensor_tensor_scan(top[b][:, 1:], mask[b][:, :], pL[b][:, :], before, ALU.add, ALU.max)\
                            .then_inc(topped, 1)

                    def subtract_top(u):
                        b = u.off % 2
                        dve.wait_ge(topped, u.count(1))
                        atleast(dve, exps_made, u.count(0))
                        nc.vector.tensor_tensor(below[:, :], pL[b][:, :], top[b][:, 1:], ALU.subtract).then_inc(below_made, 1)

                    def weigh(u):
                        b = u.off % 2
                        dve.wait_ge(exps_made, u.count(1))
                        nc.vector.tensor_tensor(term[b][64:128, :], term[b][64:128, :], pW[b][64:128, :], ALU.mult)\
                            .then_inc(term_made, 1)

                    def scan_sums(u):
                        b = u.off % 2
                        dve.wait_ge(term_made, u.count(1))
                        atleast(dve, summed, u.count(0))
                        atleast(dve, rows_made, u.count(-1))
                        nc.vector.tensor_tensor_scan(sums[b][:, :], decay[b][:, :], term[b][:, :],
                                                     sums[1 - b][:, COLS - 1:COLS], ALU.mult, ALU.add).then_inc(summed, 1)

                    def invert(u):
                        dve.wait_ge(rows_made, u.count(1))
                        atleast(dve, quo_made, u.count(0))
                        nc.vector.reciprocal(inv[:, :, :], sum_rows(u)[:, :, 0, :]).then_inc(inv_made, 1)

                    def sum_rows(u):
                        return pS[:, :].rearrange("p (t s f) -> p t s f", t=4, s=2)

                    def divide(u):
                        dve.wait_ge(inv_made, u.count(1))
                        atleast(dve, res_made, u.count(0))
                        nc.vector.tensor_tensor(quo[:, :, :], sum_rows(u)[:, :, 1, :], inv[:, :, :], ALU.mult).then_inc(quo_made, 1)

                    def residual(u):
                        dve.wait_ge(quo_made, u.count(1))
                        atleast(dve, cen_made, u.count(0))
                        nc.vector.tensor_tensor(res[:, :, :], quo[:, :, :],
                                                pD[:, :].rearrange("p (j g) -> p j g", j=4)[:, :, F:2 * F], ALU.add)\
                            .then_inc(res_made, 1)

                    def average(u):
                        dve.wait_ge(res_made, u.count(1))
                        nc.vector.tensor_reduce(mean[:, :], res[:, :, :], AX.X, ALU.add).then_inc(mean_made, 1)

                    def negate(u):
                        dve.wait_ge(mean_made, u.count(1))
                        nc.vector.tensor_scalar(nmean[:, :], mean[:, :], -1.0 / F, None, ALU.mult).then_inc(nmean_made, 1)

                    def centre(u):
                        dve.wait_ge(nmean_made, u.count(1))
                        atleast(dve, out_made, u.count(-1))
                        nc.vector.tensor_tensor(cen[u.off % 2][:, :, :], res[:, :, :],
                                                nmean[:, :].unsqueeze(2).to_broadcast([128, 4, F]), ALU.add).then_inc(cen_made, 1)

                    def sum_squares(u):
                        dve.wait_ge(sqr_made, u.count(1))
                        nc.vector.tensor_reduce(s2[:, :], sqr[:, :, :], AX.X, ALU.add).then_inc(s2_made, 1)

                    def add_eps(u):
                        dve.wait_ge(s2_made, u.count(1))
                        nc.vector.tensor_scalar(v[:, :], s2[:, :], EPS, None, ALU.add).then_inc(v_made, 1)

                    def root(u, k):
                        if u.valid(UNITS):
                            if k == 1:
                                dve.wait_ge(v_made, u.count(1))
                            root_step(nc, dve, k, v[:, :], w[:, :], ta[:, :], tb[:, :], root_steps, u.count(0), roots_made)

                    def scale(u):
                        b = u.off % 2
                        dve.wait_ge(roots_made, u.count(1))
                        atleast(dve, scattered[b], u.halves(0) * 64)
                        nc.vector.tensor_tensor(orow[b][:, :, :], cen[b][:, :, :], w[:, :].unsqueeze(2).to_broadcast([128, 4, F]),
                                                ALU.mult).then_inc(out_made, 1)

                    def slot(u):
                        if u.static() and u.count(0) == 0:
                            nc.vector.memset(xe[1][64:128, COLS - 1:COLS], 0.0)
                            nc.vector.memset(top[1][:, COLS:COLS + 1], -BIG)
                            nc.vector.memset(sums[1][:, COLS - 1:COLS], 0.0).then_inc(cleared, 1)
                            dve.wait_ge(cleared, 1)
                        a, b, c = u.back(1), u.back(2), u.back(3)
                        if a.valid(UNITS):
                            maxima(a)
                        if u.valid(UNITS):
                            hold(u)
                        if c.valid(UNITS):
                            sum_squares(c)
                            add_eps(c)
                        root(c, 1)
                        if a.valid(UNITS):
                            subtract_top(a)
                        root(c, 2)
                        if b.valid(UNITS):
                            invert(b)
                        root(c, 3)
                        root(c, 4)
                        if b.valid(UNITS):
                            divide(b)
                        root(c, 5)
                        root(c, 6)
                        if a.valid(UNITS):
                            weigh(a)
                        root(c, 7)
                        if b.valid(UNITS):
                            residual(b)
                        root(c, 8)
                        if a.valid(UNITS):
                            scan_sums(a)
                        if b.valid(UNITS):
                            average(b)
                        if c.valid(UNITS):
                            scale(c)
                        if b.valid(UNITS):
                            negate(b)
                            centre(b)

                    slots(dve, UNITS, 5, slot)


def _layout(a):
    import numpy as np
    src, dst = a["src"], a["dst"]
    pad = EP - E

    def rows(v):
        return np.ascontiguousarray(v.reshape(TILES, 128).T)

    def blocks(v):
        return np.ascontiguousarray(v.reshape(2, QR, 128).transpose(1, 0, 2))

    zero = np.zeros(pad, np.int32)
    s_rows, d_rows = rows(np.concatenate([src, zero])), rows(np.concatenate([dst, zero]))
    gidx = np.stack([s_rows.reshape(128, UNITS, 4), d_rows.reshape(128, UNITS, 4)], axis=2)
    own = np.arange(N, N + pad, dtype=np.int32)
    d = np.concatenate([dst, own])
    edge = np.array([-1], np.int32)
    before, after = np.concatenate([edge, d[:-1]]), np.concatenate([d[1:], edge])
    dblk = np.stack([blocks(before), blocks(d), blocks(after)], axis=1)
    drow = np.stack([rows(d), rows(after), rows(before)], axis=1)
    eaT = np.concatenate([a["edge_attr_16"].T, np.zeros((16, pad), np.float32)], axis=1)
    e3 = np.concatenate([a["edge_attr_3"].T, np.zeros((3, pad), np.float32)], axis=1)
    ea3 = e3.reshape(3, PAIRS, 2, COLS).transpose(2, 0, 1, 3).reshape(6, PAIRS * COLS)
    ea3 = np.concatenate([ea3, np.ones((1, PAIRS * COLS), np.float32)], axis=0)

    def twice(v):
        return np.concatenate([v, v], axis=-1)

    W, Wp, We = a["L0_gnn_W"], a["L0_gnn_Wp"], a["L0_gnn_W_edge"]
    p64 = np.concatenate([
        twice(W.reshape(F, H, F).transpose(2, 1, 0)).reshape(F, -1),
        twice(Wp.reshape(H, F, F).transpose(1, 0, 2)).reshape(F, -1),
        We.reshape(16, H, F).transpose(2, 1, 0).reshape(F, -1),
        a["L0_gnn_att_src"].T, a["L0_gnn_att_dst"].T, a["L0_gnn_att_edge"].T,
        a["L0_gnn_bias"].reshape(H, F).T], axis=1)

    def col(n):
        return twice(a[n])[:, None]

    def diag(w):
        o = np.zeros((128, 2 * w.shape[1]), np.float32)
        o[:F, :w.shape[1]] = w
        o[F:, w.shape[1]:] = w
        return o

    k, m = np.arange(128)[:, None], np.arange(128)[None, :]
    same = (k // F == m // F).astype(np.float32)
    eye = np.eye(128, dtype=np.float32)
    r = np.arange(24)[:, None]
    head = np.zeros((128, H * 128), np.float32)
    for h in range(H):
        head[:24, h * 128:(h + 1) * 128] = r % 8 == h + 4 * (m // F)
    p128 = np.concatenate([
        col("L0_gnn_bp"), col("L0_gnn_gamma"), col("L0_gnn_beta"), col("L1_gnn_g1"), col("L1_gnn_b1"),
        col("L1_gnn_bd2"), col("L1_gnn_g2"), col("L1_gnn_b2"),
        diag(a["L1_gnn_Wd1"].T), col("L1_gnn_bd1"), diag(a["L1_gnn_Wd2"].T),
        np.concatenate([twice(a["L1_gnn_W2"]), twice(a["L1_gnn_W1"])], axis=0),
        np.pad(a["L1_gnn_W3"], ((0, F), (F, 0))),
        eye, eye - same / F, (k // F == np.arange(2)[None, :]).astype(np.float32) / F,
        (k == m % F).astype(np.float32), (k == F + m % F).astype(np.float32), head], axis=1)
    return {"x": a["x"], "gidx": gidx.reshape(128, -1), "drow": drow.reshape(128, -1),
            "dblk": dblk.reshape(QR, -1), "eaT": eaT, "ea3": ea3, "p64": p64.astype(np.float32),
            "p128": p128.astype(np.float32)}


def kernel(**inputs):
    import numpy as _np
    import concourse.bacc as _bacc
    from concourse import mybir as _mybir
    from concourse.bass_utils import run_bass_kernel_spmd as _run

    nc = _bacc.Bacc("TRN2", target_bir_lowering=False, num_devices=1)
    arrays, args = {}, []
    for name, a in _layout({n: _np.asarray(v) for n, v in inputs.items()}).items():
        a = _np.ascontiguousarray(a)
        arrays[f"in_{name}_dram"] = a
        args.append(nc.dram_tensor(f"in_{name}_dram", a.shape, _mybir.dt.from_np(a.dtype), kind="ExternalInput").ap())
    out = nc.dram_tensor("out_0_dram", (N, F), _mybir.dt.float32, kind="ExternalOutput").ap()
    gnn(nc, *args, out)
    r = _run(nc, [arrays], core_ids=[0])
    return r.results[0]["out_0_dram"]
```
